# Optimizing a Trainium2 kernel written in Bass

```python
import numpy as np
import jax
import jax.numpy as jnp

def _softmax(x, axis=-1):
    return jax.nn.softmax(x, axis=axis)

def _gelu(x):
    return jax.nn.gelu(x, approximate=True)

def _silu(x):
    return jax.nn.silu(x)

def _sigmoid(x):
    return jax.nn.sigmoid(x)

def _layernorm(x, axis=-1, eps=1e-05):
    m = jnp.mean(x, axis=axis, keepdims=True)
    v = jnp.var(x, axis=axis, keepdims=True)
    return (x - m) / jnp.sqrt(v + eps)

def _scatter_add(tgt, idx, src, axis=0):
    return tgt.at[idx].add(src)

def _segment_sum(src, seg, n):
    return jax.ops.segment_sum(src, seg, n)
kernel_name = 'mk_decoder_postln_d1_seqx_r8_b4ac10'

def setup_inputs(seed: int=0):
    np.random.seed(seed)
    _w = jnp.asarray

    def _rec_inputs():
        import jax
        import jax.numpy as jnp
        _rk = jax.random.key(seed)
        x = -0.0002928 + 1 * jax.random.normal(jax.random.fold_in(_rk, 1), (32, 128, 128), jnp.float32)
        _lenS = 128 - jax.random.randint(jax.random.fold_in(_rk, 7), (32,), 0, max(1, 128 // 4) + 1, jnp.int32)
        _lenS2 = 128 - jax.random.randint(jax.random.fold_in(_rk, 8), (32,), 0, max(1, 128 // 4) + 1, jnp.int32)
        _ctx_1024P = jax.random.normal(jax.random.fold_in(_rk, 11), (32, 16, 128), jnp.float32)
        _ctx_1024c = jax.random.dirichlet(jax.random.fold_in(_rk, 511), 0.3 * jnp.ones((16,), jnp.float32), (32, 128))
        _ctx_1024t = jnp.einsum('bsk,bkd->bsd', _ctx_1024c, _ctx_1024P)
        _ctx_1024t = _ctx_1024t * jax.lax.rsqrt(jnp.mean(jnp.square(_ctx_1024t)) + 1e-12) * 0.953939
        ctx_1024 = -1.39393e-06 + 0.999914 * (_ctx_1024t + 0.3 * jax.random.normal(jax.random.fold_in(_rk, 611), (32, 128, 128), jnp.float32))
        return (x, ctx_1024)
    x, ctx_1024 = _rec_inputs()

    def _L0_attn_setup():
        import math
        import jax, jax.numpy as jnp
        import numpy as np
        NUM_HEADS = 16
        EMBED = 128
        B, T = (2, 256)
        key = jax.random.key(seed)
        k1, k2 = jax.random.split(key)
        x = jax.random.normal(k1, (B, T, EMBED), dtype=jnp.float32)
        bound = 1.0 / math.sqrt(NUM_HEADS * EMBED)
        weight = jax.random.uniform(k2, (NUM_HEADS * EMBED, EMBED), dtype=jnp.float32, minval=-bound, maxval=bound)
        return {'x': x, 'weight': weight}
    _L0_attn_all = _L0_attn_setup()
    _L0_attn_in = {k: v for k, v in _L0_attn_all.items() if k in ('weight',)}
    del _L0_attn_all

    def _L0_xattn_setup():
        import jax, jax.numpy as jnp
        import numpy as np
        import math
        D_MODEL = 128
        N_HEADS = 16
        HEAD_DIM = D_MODEL // N_HEADS
        WINDOW = 64
        B, S = (2, 256)

        def _window_mask(seq_len: int, w: int) -> jnp.ndarray:
            idx = jnp.arange(seq_len)
            return jnp.abs(idx[:, None] - idx[None, :]) <= w
        key = jax.random.key(seed)
        ks = jax.random.split(key, 11)
        s = 1.0 / math.sqrt(D_MODEL)
        return {'query': jax.random.normal(ks[0], (B, S, D_MODEL), jnp.float32), 'key': jax.random.normal(ks[1], (B, S, D_MODEL), jnp.float32), 'value': jax.random.normal(ks[2], (B, S, D_MODEL), jnp.float32), 'Wq': jax.random.normal(ks[3], (D_MODEL, D_MODEL), jnp.float32) * s, 'bq': jnp.zeros((D_MODEL,), jnp.float32), 'Wk': jax.random.normal(ks[4], (D_MODEL, D_MODEL), jnp.float32) * s, 'bk': jnp.zeros((D_MODEL,), jnp.float32), 'Wv': jax.random.normal(ks[5], (D_MODEL, D_MODEL), jnp.float32) * s, 'bv': jnp.zeros((D_MODEL,), jnp.float32), 'Wo': jax.random.normal(ks[6], (D_MODEL, D_MODEL), jnp.float32) * s, 'bo': jnp.zeros((D_MODEL,), jnp.float32)}
    _L0_xattn_all = _L0_xattn_setup()
    _L0_xattn_in = {k: v for k, v in _L0_xattn_all.items() if k in ('Wq', 'bq', 'Wk', 'bk', 'Wv', 'bv', 'Wo', 'bo')}
    del _L0_xattn_all

    def _L0_ffn_setup():
        import jax, jax.numpy as jnp
        import numpy as np
        DIM = 128
        DEPTH = 2
        HEADS = 8
        DIM_HEAD = 64
        WINDOW = 64
        INNER = HEADS * DIM_HEAD
        HID = int(DIM * 4 * 2 / 3)
        B, N = (2, 1024)
        QK_SCALE = 8.0

        def shift_token(t):
            t1, t2 = jnp.split(t, 2, axis=-1)
            t2 = jnp.pad(t2, ((0, 0), (1, 0), (0, 0)))[:, :-1]
            return jnp.concatenate([t1, t2], axis=-1)

        def l2norm(t):
            return t / jnp.clip(jnp.linalg.norm(t, axis=-1, keepdims=True), 1e-12)

        def rotate_half(x):
            x1, x2 = jnp.split(x, 2, axis=-1)
            return jnp.concatenate([-x2, x1], axis=-1)

        def rotary_xpos(q, k):
            n = q.shape[-2]
            half_idx = jnp.arange(0, DIM_HEAD, 2, dtype=jnp.float32)
            inv_freq = 1.0 / 10000.0 ** (half_idx / DIM_HEAD)
            t = jnp.arange(n, dtype=jnp.float32)
            freqs = t[:, None] * inv_freq[None, :]
            freqs = jnp.concatenate([freqs, freqs], axis=-1)
            base = (half_idx + 0.4 * DIM_HEAD) / (1.4 * DIM_HEAD)
            power = (t - n // 2) / float(WINDOW // 2)
            scale = base[None, :] ** power[:, None]
            scale = jnp.concatenate([scale, scale], axis=-1)
            cos, sin = (jnp.cos(freqs), jnp.sin(freqs))
            q = q * cos * scale + rotate_half(q) * sin * scale
            k = k * cos / scale + rotate_half(k) * sin / scale
            return (q, k)

        def local_attention(q, k, v):
            b, h, n, d = q.shape
            w = n // WINDOW
            bq = q.reshape(b, h, w, WINDOW, d) * QK_SCALE
            bk = k.reshape(b, h, w, WINDOW, d)
            bv = v.reshape(b, h, w, WINDOW, d)

            def look_around(t):
                p = jnp.pad(t, ((0, 0), (0, 0), (1, 0), (0, 0), (0, 0)))
                return jnp.concatenate([p[:, :, :w], p[:, :, 1:]], axis=3)
            bk, bv = (look_around(bk), look_around(bv))
            bt = jnp.arange(n).reshape(w, WINDOW)
            btp = jnp.pad(bt, ((1, 0), (0, 0)), constant_values=-1)
            btk = jnp.concatenate([btp[:w], btp[1:]], axis=1)
            sim = jnp.einsum('bhwid,bhwjd->bhwij', bq, bk)
            i = bt[:, :, None]
            j = btk[:, None, :]
            mask = (i < j) | (i > j + WINDOW) | (j == -1)
            sim = jnp.where(mask, -jnp.finfo(sim.dtype).max, sim)
            attn = jax.nn.softmax(sim, axis=-1)
            out = jnp.einsum('bhwij,bhwjd->bhwid', attn, bv)
            return out.reshape(b, h, n, d)

        def _layer(x, wqkv, qs, ksc, wo, lg, lb, w1, b1, w2, b2):
            b, n, _ = x.shape
            h = shift_token(x)
            qkv = h @ wqkv
            q, k, v = jnp.split(qkv, 3, axis=-1)
            to_heads = lambda t: t.reshape(b, n, HEADS, DIM_HEAD).transpose(0, 2, 1, 3)
            q, k, v = (to_heads(q), to_heads(k), to_heads(v))
            q = l2norm(q) * qs
            k = l2norm(k) * ksc
            q, k = rotary_xpos(q, k)
            o = local_attention(q, k, v)
            o = o.transpose(0, 2, 1, 3).reshape(b, n, INNER)
            x = x + o @ wo
            h = shift_token(x)
            mu = h.mean(-1, keepdims=True)
            var = h.var(-1, keepdims=True)
            h = (h - mu) / jnp.sqrt(var + 1e-05) * lg + lb
            h = h @ w1 + b1
            a, g = jnp.split(h, 2, axis=-1)
            h = a * jax.nn.gelu(g, approximate=False)
            x = x + h @ w2 + b2
            return x
        key = jax.random.key(seed)
        ks = jax.random.split(key, 6)
        return {'x': jax.random.normal(ks[0], (B, N, DIM), jnp.float32), 'wqkv': jax.random.normal(ks[1], (DEPTH, DIM, 3 * INNER), jnp.float32) * 0.02, 'q_scale': jnp.ones((DEPTH, DIM_HEAD), jnp.float32), 'k_scale': jnp.ones((DEPTH, DIM_HEAD), jnp.float32), 'wo': jax.random.normal(ks[2], (DEPTH, INNER, DIM), jnp.float32) * 0.02, 'ln_g': jnp.ones((DEPTH, DIM), jnp.float32), 'ln_b': jnp.zeros((DEPTH, DIM), jnp.float32), 'w1': jax.random.normal(ks[3], (DEPTH, DIM, 2 * HID), jnp.float32) * 0.02, 'b1': jnp.zeros((DEPTH, 2 * HID), jnp.float32), 'w2': jax.random.normal(ks[4], (DEPTH, HID, DIM), jnp.float32) * 0.02, 'b2': jnp.zeros((DEPTH, DIM), jnp.float32)}
    _L0_ffn_all = _L0_ffn_setup()
    _L0_ffn_in = {k: v for k, v in _L0_ffn_all.items() if k in ('wqkv', 'q_scale', 'k_scale', 'wo', 'ln_g', 'ln_b', 'w1', 'b1', 'w2', 'b2')}
    del _L0_ffn_all
    return {'x': x, 'ctx_1024': ctx_1024, 'L0_attn_weight': _L0_attn_in['weight'], 'L0_xattn_Wq': _L0_xattn_in['Wq'], 'L0_xattn_bq': _L0_xattn_in['bq'], 'L0_xattn_Wk': _L0_xattn_in['Wk'], 'L0_xattn_bk': _L0_xattn_in['bk'], 'L0_xattn_Wv': _L0_xattn_in['Wv'], 'L0_xattn_bv': _L0_xattn_in['bv'], 'L0_xattn_Wo': _L0_xattn_in['Wo'], 'L0_xattn_bo': _L0_xattn_in['bo'], 'L0_ffn_wqkv': _L0_ffn_in['wqkv'], 'L0_ffn_q_scale': _L0_ffn_in['q_scale'], 'L0_ffn_k_scale': _L0_ffn_in['k_scale'], 'L0_ffn_wo': _L0_ffn_in['wo'], 'L0_ffn_ln_g': _L0_ffn_in['ln_g'], 'L0_ffn_ln_b': _L0_ffn_in['ln_b'], 'L0_ffn_w1': _L0_ffn_in['w1'], 'L0_ffn_b1': _L0_ffn_in['b1'], 'L0_ffn_w2': _L0_ffn_in['w2'], 'L0_ffn_b2': _L0_ffn_in['b2']}

def reference(x, ctx_1024, L0_attn_weight, L0_xattn_Wq, L0_xattn_bq, L0_xattn_Wk, L0_xattn_bk, L0_xattn_Wv, L0_xattn_bv, L0_xattn_Wo, L0_xattn_bo, L0_ffn_wqkv, L0_ffn_q_scale, L0_ffn_k_scale, L0_ffn_wo, L0_ffn_ln_g, L0_ffn_ln_b, L0_ffn_w1, L0_ffn_b1, L0_ffn_w2, L0_ffn_b2):
    import jax
    import jax.numpy as jnp

    def _L0_attn_ref(x, weight):
        import math
        import jax, jax.numpy as jnp
        import numpy as np
        NUM_HEADS = 16
        EMBED = 128
        B, T = (2, 256)
        b, t, c = x.shape
        nh = NUM_HEADS
        hs = c // nh
        y = x.reshape(b, t, nh, hs).transpose(0, 2, 1, 3)
        scores = jnp.einsum('bhtk,bhsk->bhts', y, y) / math.sqrt(hs)
        attn = jax.nn.softmax(scores, axis=-1)
        o = jnp.einsum('bhts,bsc->bhtc', attn, x)
        o = o.transpose(0, 2, 1, 3).reshape(b, t, nh * c)
        return o @ weight

    def _L0_xattn_ref(query, key, value, Wq, bq, Wk, bk, Wv, bv, Wo, bo):
        import jax, jax.numpy as jnp
        import numpy as np
        import math
        D_MODEL = 128
        N_HEADS = 16
        HEAD_DIM = D_MODEL // N_HEADS
        WINDOW = 64
        B, S = (2, 256)

        def _window_mask(seq_len: int, w: int) -> jnp.ndarray:
            idx = jnp.arange(seq_len)
            return jnp.abs(idx[:, None] - idx[None, :]) <= w
        b, s, _ = query.shape
        Q = (query @ Wq.T + bq).reshape(b, s, N_HEADS, HEAD_DIM).transpose(0, 2, 1, 3)
        K = (key @ Wk.T + bk).reshape(b, s, N_HEADS, HEAD_DIM).transpose(0, 2, 1, 3)
        V = (value @ Wv.T + bv).reshape(b, s, N_HEADS, HEAD_DIM).transpose(0, 2, 1, 3)
        scale = 1.0 / math.sqrt(HEAD_DIM)
        scores = jnp.einsum('bhqd,bhkd->bhqk', Q, K) * scale
        mask = _window_mask(s, WINDOW)
        scores = jnp.where(mask[None, None], scores, jnp.float32(-jnp.inf))
        attn = jax.nn.softmax(scores, axis=-1)
        out = jnp.einsum('bhqk,bhkd->bhqd', attn, V)
        out = out.transpose(0, 2, 1, 3).reshape(b, s, D_MODEL)
        return out @ Wo.T + bo

    def _L0_ffn_ref(x, wqkv, q_scale, k_scale, wo, ln_g, ln_b, w1, b1, w2, b2):
        import jax, jax.numpy as jnp
        import numpy as np
        DIM = 128
        DEPTH = 2
        HEADS = 8
        DIM_HEAD = 64
        WINDOW = 64
        INNER = HEADS * DIM_HEAD
        HID = int(DIM * 4 * 2 / 3)
        B, N = (2, 1024)
        QK_SCALE = 8.0

        def shift_token(t):
            t1, t2 = jnp.split(t, 2, axis=-1)
            t2 = jnp.pad(t2, ((0, 0), (1, 0), (0, 0)))[:, :-1]
            return jnp.concatenate([t1, t2], axis=-1)

        def l2norm(t):
            return t / jnp.clip(jnp.linalg.norm(t, axis=-1, keepdims=True), 1e-12)

        def rotate_half(x):
            x1, x2 = jnp.split(x, 2, axis=-1)
            return jnp.concatenate([-x2, x1], axis=-1)

        def rotary_xpos(q, k):
            n = q.shape[-2]
            half_idx = jnp.arange(0, DIM_HEAD, 2, dtype=jnp.float32)
            inv_freq = 1.0 / 10000.0 ** (half_idx / DIM_HEAD)
            t = jnp.arange(n, dtype=jnp.float32)
            freqs = t[:, None] * inv_freq[None, :]
            freqs = jnp.concatenate([freqs, freqs], axis=-1)
            base = (half_idx + 0.4 * DIM_HEAD) / (1.4 * DIM_HEAD)
            power = (t - n // 2) / float(WINDOW // 2)
            scale = base[None, :] ** power[:, None]
            scale = jnp.concatenate([scale, scale], axis=-1)
            cos, sin = (jnp.cos(freqs), jnp.sin(freqs))
            q = q * cos * scale + rotate_half(q) * sin * scale
            k = k * cos / scale + rotate_half(k) * sin / scale
            return (q, k)

        def local_attention(q, k, v):
            b, h, n, d = q.shape
            w = n // WINDOW
            bq = q.reshape(b, h, w, WINDOW, d) * QK_SCALE
            bk = k.reshape(b, h, w, WINDOW, d)
            bv = v.reshape(b, h, w, WINDOW, d)

            def look_around(t):
                p = jnp.pad(t, ((0, 0), (0, 0), (1, 0), (0, 0), (0, 0)))
                return jnp.concatenate([p[:, :, :w], p[:, :, 1:]], axis=3)
            bk, bv = (look_around(bk), look_around(bv))
            bt = jnp.arange(n).reshape(w, WINDOW)
            btp = jnp.pad(bt, ((1, 0), (0, 0)), constant_values=-1)
            btk = jnp.concatenate([btp[:w], btp[1:]], axis=1)
            sim = jnp.einsum('bhwid,bhwjd->bhwij', bq, bk)
            i = bt[:, :, None]
            j = btk[:, None, :]
            mask = (i < j) | (i > j + WINDOW) | (j == -1)
            sim = jnp.where(mask, -jnp.finfo(sim.dtype).max, sim)
            attn = jax.nn.softmax(sim, axis=-1)
            out = jnp.einsum('bhwij,bhwjd->bhwid', attn, bv)
            return out.reshape(b, h, n, d)

        def _layer(x, wqkv, qs, ksc, wo, lg, lb, w1, b1, w2, b2):
            b, n, _ = x.shape
            h = shift_token(x)
            qkv = h @ wqkv
            q, k, v = jnp.split(qkv, 3, axis=-1)
            to_heads = lambda t: t.reshape(b, n, HEADS, DIM_HEAD).transpose(0, 2, 1, 3)
            q, k, v = (to_heads(q), to_heads(k), to_heads(v))
            q = l2norm(q) * qs
            k = l2norm(k) * ksc
            q, k = rotary_xpos(q, k)
            o = local_attention(q, k, v)
            o = o.transpose(0, 2, 1, 3).reshape(b, n, INNER)
            x = x + o @ wo
            h = shift_token(x)
            mu = h.mean(-1, keepdims=True)
            var = h.var(-1, keepdims=True)
            h = (h - mu) / jnp.sqrt(var + 1e-05) * lg + lb
            h = h @ w1 + b1
            a, g = jnp.split(h, 2, axis=-1)
            h = a * jax.nn.gelu(g, approximate=False)
            x = x + h @ w2 + b2
            return x
        for l in range(DEPTH):
            x = _layer(x, wqkv[l], q_scale[l], k_scale[l], wo[l], ln_g[l], ln_b[l], w1[l], b1[l], w2[l], b2[l])
        return x
    x = _layernorm(x + _L0_attn_ref(x, L0_attn_weight), axis=-1)
    x = _layernorm(x + _L0_xattn_ref(x, ctx_1024, ctx_1024, L0_xattn_Wq, L0_xattn_bq, L0_xattn_Wk, L0_xattn_bk, L0_xattn_Wv, L0_xattn_bv, L0_xattn_Wo, L0_xattn_bo), axis=-1)
    x = _layernorm(x + _L0_ffn_ref(x, L0_ffn_wqkv, L0_ffn_q_scale, L0_ffn_k_scale, L0_ffn_wo, L0_ffn_ln_g, L0_ffn_ln_b, L0_ffn_w1, L0_ffn_b1, L0_ffn_w2, L0_ffn_b2), axis=-1)
    return x

_drawn_inputs = setup_inputs


def setup_inputs(seed=0):
    import zlib

    import numpy as np

    out = dict(_drawn_inputs(seed))
    spreads = {'L0_xattn_bq': (0.0, 0.37),
     'L0_xattn_bk': (0.0, 2.0),
     'L0_xattn_bv': (0.0, 0.1),
     'L0_xattn_bo': (0.0, 0.1),
     'L0_ffn_q_scale': (1.0, 0.6),
     'L0_ffn_k_scale': (1.0, 0.6),
     'L0_ffn_ln_g': (1.0, 0.6),
     'L0_ffn_ln_b': (0.0, 0.8),
     'L0_ffn_b1': (0.0, 0.8),
     'L0_ffn_b2': (0.0, 0.552)}
    factors = {'L0_ffn_w1': 6.214, 'L0_ffn_w2': 6.154}
    for name, (base, spread) in spreads.items():
        noise = np.random.default_rng([zlib.crc32(name.encode()), seed]).standard_normal(out[name].shape)
        drawn = base * np.exp(spread * noise) if base else spread * noise
        out[name] = jnp.asarray(drawn.astype(out[name].dtype))
    for name, factor in factors.items():
        out[name] = (out[name] * factor).astype(out[name].dtype)
    return out
```

```python
from contextlib import ExitStack

import numpy as np

import concourse.bass as bass
from concourse import mybir

F32 = mybir.dt.float32
BF16 = mybir.dt.bfloat16
ALU = mybir.AluOpType
ACT = mybir.ActivationFunctionType
AX = mybir.AxisListType

T = 128
D = 128
H = 16
HD = D // H
GH = 4
G = H // GH
LH = 8
LD = 64
INNER = LH * LD
HID = 341
FC = (114, 114, 113)
FO = (0, 114, 228)
WINDOW = 64
EPS = 1e-5
MASKED = -1e30
STEP = 16
SETS = ((0, 3), (3, 3), (6, 3), (9, 3), (12, 3), (15, 1))
SET_UP = (2, 2, 2, 2, 2, 6)

C_ID = 0
C_SHIFT = C_ID + 128
C_MASKN = C_SHIFT + 128
C_MASKT = C_MASKN + 128
C_BAND = C_MASKT + 128
C_GRP = C_BAND + 128
C_HEAD = C_GRP + 4 * 128
C_ROW = C_HEAD + H
C_OWN = C_ROW + GH
C_COS = C_OWN + GH * 128
C_SIN = C_COS + 2 * LD
C_END = C_SIN + 2 * LD


def shape_constants():
    c = np.zeros((128, C_END), np.float32)
    p = np.arange(128)
    c[:, C_ID:C_ID + 128] = np.eye(128)
    c[:, C_SHIFT:C_SHIFT + 128] = np.eye(128, k=1)
    i, j = p[:, None], p[None, :]
    allowed = (j <= i) & (j >= i - WINDOW)
    c[:, C_MASKN:C_MASKN + 128] = np.where(allowed, 0.0, MASKED)
    c[:, C_MASKT:C_MASKT + 128] = np.where(allowed.T, 0.0, MASKED)
    c[:, C_BAND:C_BAND + 128] = np.where(np.abs(i - j) <= WINDOW, 0.0, MASKED)
    head = p % 16
    for g in range(4):
        rows = (p < 32) & (head // GH == g)
        c[:, C_GRP + 128 * g:C_GRP + 128 * (g + 1)] = rows[:, None]
    c[:, C_HEAD:C_HEAD + H] = (p[:, None] // HD == np.arange(H)) * np.float32(1.0 / np.sqrt(HD))
    c[:, C_ROW:C_ROW + GH] = (p[:, None] < 32) & (head[:, None] % GH == np.arange(GH))
    for n in range(GH):
        c[:, C_OWN + 128 * n:C_OWN + 128 * (n + 1)] = (p // HD) % GH == n
    half = np.arange(0, LD, 2, dtype=np.float32)
    inv = np.float32(1.0) / np.float32(10000.0) ** (half / np.float32(LD))
    t = np.arange(T, dtype=np.float32)
    freq = t[:, None] * inv[None, :]
    freq = np.concatenate([freq, freq], axis=-1)
    base = (half + np.float32(0.4 * LD)) / np.float32(1.4 * LD)
    power = (t - T // 2) / np.float32(WINDOW // 2)
    scale = base[None, :] ** power[:, None]
    scale = np.concatenate([scale, scale], axis=-1)
    sign = np.where(np.arange(LD) < LD // 2, -1.0, 1.0).astype(np.float32)
    cos, sin = np.cos(freq), np.sin(freq) * sign
    c[:, C_COS:C_COS + LD] = cos / scale
    c[:, C_COS + LD:C_COS + 2 * LD] = cos * scale * 8.0
    c[:, C_SIN:C_SIN + LD] = sin / scale
    c[:, C_SIN + LD:C_SIN + 2 * LD] = sin * scale * 8.0
    return c


def again(v):
    return not (isinstance(v, int) and v == 0)


def weave(*parts):
    parts = list(parts)
    while parts:
        for part in list(parts):
            if next(part, "end") == "end":
                parts.remove(part)


class Stage:
    pass


def decoder_kernel(nc, x, ctx_in, consts, w_heads, wqT, bq, wkT, bk, wvT, bv, woT, bo,
                   wqkv, q_scale, k_scale, wo, ln_g, ln_b, w1, b1, w2, b2, out):
    B = x.shape[0]
    LAST = 4
    x_rows = x.rearrange("b t d -> (b t) d")
    ctx_rows = ctx_in.rearrange("b t d -> (b t) d")
    out_rows = out.rearrange("b t d -> (b t) d")

    with ExitStack() as ctx:
        def sb(name, shape, dt=F32):
            return ctx.enter_context(nc.sbuf_tensor(name, shape, dt))

        def sem(name):
            return ctx.enter_context(nc.semaphore(name))

        con = sb("con", [128, C_END])
        ident = con[:, C_ID:C_ID + 128]
        shift_m = con[:, C_SHIFT:C_SHIFT + 128]
        head_mask = con[:, C_HEAD:C_HEAD + H]
        row_mask = con[:, C_ROW:C_ROW + GH]
        own = con[:, C_OWN:C_OWN + GH * 128].rearrange("p (j c) -> p j c", j=GH)
        ident_b = sb("ident_b", [128, 128], BF16)
        mask_n = sb("mask_n", [128, GH, 128], BF16)
        mask_t = sb("mask_t", [128, GH, 128], BF16)
        mask_w = sb("mask_w", [128, GH, 128], BF16)
        group_b = sb("group_b", [128, G, 128], BF16)
        half_neg = sb("half_neg", [128, H])
        wz = sb("wz", [128, H * 128])
        wq_s, wk_s, wv_s, wo_s = (sb(n, [128, 128]) for n in ("wq_s", "wk_s", "wv_s", "wo_s"))
        bq_c, bk_c = sb("bq_c", [128, 1]), sb("bk_c", [128, 1])
        bv_r, bo_r = sb("bv_r", [128, 128]), sb("bo_r", [128, 128])
        wqkv_s = [sb(f"wqkv_s{l}", [128, 3 * INNER]) for l in range(2)]
        wo3_s = [sb(f"wo3_s{l}", [128, LH // 2, 128]) for l in range(2)]
        w1_r = [sb(f"w1_r{l}", [128, 2 * HID]) for l in range(2)]
        w1_s = [sb(f"w1_s{l}", [128, 2 * HID]) for l in range(2)]
        w2_s = [sb(f"w2_s{l}", [128, 3, 128]) for l in range(2)]
        b1_r = [sb(f"b1_r{l}", [128, 6]) for l in range(2)]
        b1_s = [sb(f"b1_s{l}", [128, 6]) for l in range(2)]
        lg_c = [sb(f"lg_c{l}", [128, 1]) for l in range(2)]
        lb_c = [sb(f"lb_c{l}", [128, 1]) for l in range(2)]
        b2_r = [sb(f"b2_r{l}", [128, 128]) for l in range(2)]
        scale_r = [sb(f"scale_r{l}", [128, 2, LD]) for l in range(2)]
        scale_x = [sb(f"scale_x{l}", [128, 2, LD]) for l in range(2)]
        cos_t = [sb(f"cos_t{l}", [128, 2, LD]) for l in range(2)]
        sin_t = [sb(f"sin_t{l}", [128, 2, LD]) for l in range(2)]

        loaded = sem("weights_loaded")
        prep_v = sem("prepared_by_vector")
        prep_p = sem("prepared_by_pool")
        prep_mm = sem("bias_products")
        stored = sem("stored")

        def stage(name):
            s = Stage()
            s.ps = ctx.enter_context(nc.psum_tensor(f"{name}_ps", [128, 1024], F32))
            s.b0, s.b1 = s.ps[:, 0:512], s.ps[:, 512:1024]
            s.x_copied = sem(f"{name}_x_copied")
            s.xT_psum = sem(f"{name}_xT_psum")
            s.xT_ready = sem(f"{name}_xT_ready")
            s.q_low = sem(f"{name}_q_low")
            s.k_low = sem(f"{name}_k_low")
            s.scores_n_psum = sem(f"{name}_scores_n_psum")
            s.max_done = sem(f"{name}_max_done")
            s.neg_split = sem(f"{name}_neg_split")
            s.rows_psum = sem(f"{name}_rows_psum")
            s.rows_ready = sem(f"{name}_rows_ready")
            s.scores_t_psum = sem(f"{name}_scores_t_psum")
            s.exp_done = sem(f"{name}_exp_done")
            s.resid = sem(f"{name}_resid")
            return s

        def norm_signals(s, name):
            s.moments = sem(f"{name}_moments")
            s.rstd = sem(f"{name}_rstd")
            s.normed = sem(f"{name}_normed")

        def local_signals(s, name):
            s.qkv_psum = sem(f"{name}_qkv_psum")
            s.squares = sem(f"{name}_squares")
            s.square_sum = sem(f"{name}_square_sum")
            s.rnorm = sem(f"{name}_rnorm")
            s.qk_norm = sem(f"{name}_qk_norm")
            s.v_psum = sem(f"{name}_v_psum")
            s.v_ready = sem(f"{name}_v_ready")
            s.rot_sin = sem(f"{name}_rot_sin")
            s.rot_cos = sem(f"{name}_rot_cos")
            s.roped = sem(f"{name}_roped")
            s.qkT_psum = sem(f"{name}_qkT_psum")
            s.kT_ready = sem(f"{name}_kT_ready")
            s.q_split = sem(f"{name}_q_split")
            s.av_psum = sem(f"{name}_av_psum")
            s.inverse = sem(f"{name}_inverse")
            s.oT_psum = sem(f"{name}_oT_psum")
            s.oT_ready = sem(f"{name}_oT_ready")
            s.o_ready = sem(f"{name}_o_ready")
            s.proj_psum = sem(f"{name}_proj_psum")
            s.mid_done = sem(f"{name}_mid_done")
            s.mid_bias = sem(f"{name}_mid_bias")
            s.mid_moments = sem(f"{name}_mid_moments")
            s.mid_rstd = sem(f"{name}_mid_rstd")
            s.shifted_psum = sem(f"{name}_shifted_psum")
            s.hT_psum = sem(f"{name}_hT_psum")
            s.hT_ready = sem(f"{name}_hT_ready")
            s.hnorm = sem(f"{name}_hnorm")
            s.mlp_in_psum = sem(f"{name}_mlp_in_psum")
            s.gelu_done = sem(f"{name}_gelu_done")
            s.hid_done = sem(f"{name}_hid_done")
            s.mlp_psum = sem(f"{name}_mlp_psum")

        SELF, CROSS = stage("self"), stage("cross")
        LOC = [stage("local0"), stage("local1")]
        norm_signals(SELF, "self")
        norm_signals(CROSS, "cross")
        norm_signals(LOC[1], "local1")
        for l in range(2):
            local_signals(LOC[l], f"local{l}")
        SELF.q_wide = sem("self_q_wide")
        SELF.z_psum = sem("self_z_psum")
        SELF.z_ready = sem("self_z_ready")
        SELF.av_psum = sem("self_av_psum")
        SELF.rden = sem("self_rden")
        SELF.y_ready = sem("self_y_ready")
        SELF.tree = sem("self_tree")
        SELF.x_loaded = sem("self_x_loaded")
        CROSS.q_wide = sem("cross_q_wide")
        CROSS.c_loaded = sem("cross_c_loaded")
        CROSS.cT_psum = sem("cross_cT_psum")
        CROSS.cT_ready = sem("cross_cT_ready")
        CROSS.kT_psum = sem("cross_kT_psum")
        CROSS.kT_ready = sem("cross_kT_ready")
        CROSS.v_psum = sem("cross_v_psum")
        CROSS.v_ready = sem("cross_v_ready")
        CROSS.q_psum = sem("cross_q_psum")
        CROSS.av_psum = sem("cross_av_psum")
        CROSS.inverse = sem("cross_inverse")
        CROSS.v_own = sem("cross_v_own")
        CROSS.o_ready = sem("cross_o_ready")
        CROSS.proj_psum = sem("cross_proj_psum")
        CROSS.x_bias = sem("cross_x_bias")
        LOC[0].kept = sem("local0_kept")
        LOC[1].base_bias = sem("local1_base_bias")
        for s, n in ((SELF, "self"), (CROSS, "cross")):
            s.q = sb(f"{n}_q", [128, H, 128])
            s.qb = sb(f"{n}_qb", [128, H, 128], BF16)
            s.xT = sb(f"{n}_xT", [128, 128])
            s.kb = sb(f"{n}_kb", [128, 128], BF16)
            s.e = sb(f"{n}_e", [128, H, 128])
        for s, n, h in ((SELF, "self", H), (CROSS, "cross", H), (LOC[0], "local0", LH), (LOC[1], "local1", LH)):
            s.heads = h
            s.m = sb(f"{n}_m", [128, h])
            s.neg = sb(f"{n}_neg", [128, 128], BF16)
            s.rows = sb(f"{n}_rows", [128, GH, 128], BF16)
            s.st = sb(f"{n}_st", [128, 2, 6])
            s.mv2 = sb(f"{n}_mv2", [128, 2])
            s.rs2 = sb(f"{n}_rs2", [128, 1])
            s.mv = sb(f"{n}_mv", [128, 2])
            s.ve = sb(f"{n}_ve", [128, 1])
            s.rs = sb(f"{n}_rs", [128, 1])
            s.r = sb(f"{n}_r", [128, 128])
        SELF.windowed, CROSS.windowed = False, True
        SELF.xin = sb("self_xin", [128, 128])
        SELF.x = sb("self_x", [128, 128])
        SELF.k = SELF.xT
        SELF.z = sb("self_z", [128, H, 129])
        SELF.rd = sb("self_rd", [128, H])
        SELF.y = sb("self_y", [128, H, 128])
        SELF.out = sb("self_out", [128, 128])
        CROSS.cin = sb("cross_cin", [128, 128])
        CROSS.cT = sb("cross_cT", [128, 128])
        CROSS.k = sb("cross_k", [128, 128])
        CROSS.v = sb("cross_v", [128, 128])
        CROSS.x = sb("cross_x", [128, 128])
        CROSS.xb = sb("cross_xb", [128, 128])
        CROSS.vm = sb("cross_vm", [128, GH, 128])
        CROSS.o = sb("cross_o", [128, 128])
        CROSS.out = sb("cross_out", [128, 128])
        for l, s in enumerate(LOC):
            n = f"local{l}"
            s.x = sb(f"{n}_x", [128, 2, 128])
            s.xT = sb(f"{n}_xT", [128, 128])
            s.ss = sb(f"{n}_ss", [128, 2 * LH])
            s.sc = sb(f"{n}_sc", [128, 2 * LH])
            s.rn = sb(f"{n}_rn", [128, 2 * LH])
            s.qk = sb(f"{n}_qk", [128, 2, LH, LD])
            s.qs = sb(f"{n}_qs", [128, 2, LH, LD])
            s.sq = s.qs[:, :, :, :].rearrange("p a h d -> p (a h) d")
            s.qc = sb(f"{n}_qc", [128, 2, LH, LD])
            s.qr = s.qc[:, :, :, :].rearrange("p a h d -> p (a h d)")
            s.v = sb(f"{n}_v", [128, LH, LD + 1])
            s.k = sb(f"{n}_k", [128, LH // 2, 128])
            s.kb = sb(f"{n}_kb", [128, LH // 2, 128], BF16)
            s.q = sb(f"{n}_q", [128, LH // 2, 2, 128])
            s.qb = sb(f"{n}_qb", [128, LH // 2, 2, 128], BF16)
            s.e = sb(f"{n}_e", [128, LH, 128])
            s.rd = sb(f"{n}_rd", [128, LH])
            s.o = sb(f"{n}_o", [128, INNER])
            s.oT = sb(f"{n}_oT", [128, LH // 2, 128])
            s.mid = sb(f"{n}_mid", [128, 128])
            s.midb = sb(f"{n}_midb", [128, 128])
            s.hn = sb(f"{n}_hn", [128, 128])
            s.hT = sb(f"{n}_hT", [128, 128])
            s.gate = sb(f"{n}_gate", [128, 3, 128])
            s.hid = s.gate
            s.out = sb(f"{n}_out", [128, 2, 128])
            s.base = sb(f"{n}_base", [128, 128])

        block = ctx.enter_context(nc.Block())

        def loop(eng, iteration):
            fill = LAST + 1
            for n in range(fill):
                iteration(STEP * n)
            if B > fill:
                with eng.Fori(STEP * fill, STEP * B, STEP) as i:
                    iteration(i)
            for n in range(max(B, fill), B + LAST):
                iteration(STEP * n)

        def at(i, skew):
            if isinstance(i, int):
                v = i - STEP * skew
                return v if 0 <= v < STEP * B else None
            return i - STEP * skew if skew else i

        def sample_rows(a, v):
            if isinstance(v, int):
                return a[v * (T // STEP):v * (T // STEP) + T, :]
            return a.rearrange("(b t) d -> b t d", t=T)[bass.ds(v // STEP, 1), :, :].rearrange("b t d -> (b t) d")

        SETUP = [
            (con[:, :], consts), (wz[:, :], w_heads), (wq_s[:, :], wqT), (wk_s[:, :], wkT),
            (wv_s[:, :], wvT), (wo_s[:, :], woT),
            (bq_c[:, :], bq.rearrange("(p a) -> p a", a=1)), (bk_c[:, :], bk.rearrange("(p a) -> p a", a=1)),
            (bv_r[:, :], bv.partition_broadcast(128)), (bo_r[:, :], bo.partition_broadcast(128)),
        ]
        for l in range(2):
            SETUP += [
                (wqkv_s[l][:, :], wqkv[l]), (wo3_s[l][:, :, :], wo[l].rearrange("(c p) n -> p c n", p=128)),
                (w1_r[l][:, :], w1[l]), (b2_r[l][:, :], b2[l].partition_broadcast(128)),
                (lg_c[l][:, :], ln_g[l].rearrange("(p a) -> p a", a=1)),
                (lb_c[l][:, :], ln_b[l].rearrange("(p a) -> p a", a=1)),
                (w2_s[l][0:FC[0], 0:2, :], w2[l][0:2 * FC[0], :].rearrange("(c p) n -> p c n", p=FC[0])),
                (w2_s[l][0:FC[2], 2, :], w2[l][2 * FC[0]:HID, :]),
            ]
            for half in range(2):
                for c in range(3):
                    lo = half * HID + FO[c]
                    SETUP.append((b1_r[l][0:FC[c], 3 * half + c:3 * half + c + 1],
                                  b1[l][lo:lo + FC[c]].rearrange("(p a) -> p a", a=1)))
            for k, s in enumerate((k_scale, q_scale)):
                SETUP.append((scale_r[l][:, k, :], s[l].partition_broadcast(128)))
                for a in range(2):
                    SETUP.append((scale_x[l][:, k, 32 * a:32 * a + 32],
                                  s[l][32 * (1 - a):32 * (1 - a) + 32].partition_broadcast(128)))
        ALL_LOADED = 16 * len(SETUP)
        N_PREP_V = 17
        N_PREP_P = 6

        def stages(eng, self_stage, cross_stage, local_stage):
            def iteration(i):
                parts = []
                if at(i, 1) is not None:
                    parts.append(self_stage(at(i, 1)))
                if at(i, 2) is not None:
                    parts.append(cross_stage(at(i, 2)))
                for l in range(2):
                    if at(i, 3 + l) is not None:
                        parts.append(local_stage(l, at(i, 3 + l)))
                weave(*parts)
            loop(eng, iteration)

        @block.sync
        def _(sp):
            for tile, source in SETUP:
                sp.dma_start(tile, source).then_inc(loaded, 16)

            def iteration(i):
                v = at(i, 0)
                if v is not None:
                    if again(v):
                        sp.wait_ge(SELF.x_copied, v)
                    sp.dma_start(SELF.xin[:, :], sample_rows(x_rows, v)).then_inc(SELF.x_loaded, 16)
                v = at(i, 1)
                if v is not None:
                    if again(v):
                        sp.wait_ge(CROSS.cT_psum, v)
                    sp.dma_start(CROSS.cin[:, :], sample_rows(ctx_rows, v)).then_inc(CROSS.c_loaded, 16)
                v = at(i, 4)
                if v is not None:
                    sp.wait_ge(LOC[1].normed, v + STEP)
                    sp.dma_start(sample_rows(out_rows, v), LOC[1].out[:, 0, :]).then_inc(stored, 16)

            loop(nc.sync, iteration)
            sp.wait_ge(stored, STEP * B)

        @block.tensor
        def _(pe):
            pe.wait_ge(loaded, ALL_LOADED)
            pe.wait_ge(prep_v, N_PREP_V)
            pe.wait_ge(prep_p, N_PREP_P)
            for l in range(2):
                for half in range(2):
                    for c in range(3):
                        lo = half * HID + FO[c]
                        last = nc.tensor.matmul(LOC[l].b0[0:FC[c], 3 * half + c:3 * half + c + 1],
                                                w1_r[l][:, lo:lo + FC[c]], lb_c[l][:, :], start=True, stop=True)
            last.then_inc(prep_mm, 1)
            pe.wait_ge(prep_v, N_PREP_V + 8)

            def max_to_rows(s, v):
                pe.wait_ge(s.neg_split, v + STEP)
                nc.tensor.transpose(s.b1.bitcast(BF16)[:, 0:128], s.neg[:, :], ident_b[:, :]).then_inc(s.rows_psum, STEP)

            def core16(s, v):
                pe.wait_ge(s.k_low, v + STEP)
                for g in range(G):
                    bank = s.b0 if g % 2 else s.b1
                    if g % 2 == 0:
                        pe.wait_ge(s.q_low, v + 8 * (g // 2) + 8)
                    if g >= 2:
                        pe.wait_ge(s.max_done, v + 4 * (g - 1))
                    for j in range(GH):
                        last = nc.tensor.matmul(bank[:, 128 * j:128 * j + 128], s.qb[:, GH * g + j, :],
                                                s.kb[:, :], start=(j == 0), stop=not s.windowed, skip_group_check=True)
                    if s.windowed:
                        last = nc.tensor.matmul(bank, ident_b[:, :], mask_w[:, :, :], start=False, stop=True,
                                                skip_group_check=True)
                    last.then_inc(s.scores_n_psum, 4)
                    yield
                pe.wait_ge(s.max_done, v + STEP)
                nc.tensor.matmul(s.b0, s.k[:, :], s.q[:, 0:GH, :], start=True, stop=False)
                yield
                max_to_rows(s, v)
                yield
                for g in range(G):
                    bank = s.b1 if g % 2 else s.b0
                    if g == 0:
                        pe.wait_ge(s.rows_ready, v + STEP)
                    else:
                        if g >= 2:
                            pe.wait_ge(s.exp_done, v + 4 * (g - 1))
                        nc.tensor.matmul(bank, s.k[:, :], s.q[:, GH * g:GH * g + GH, :], start=True, stop=False)
                    if s.windowed:
                        nc.tensor.matmul(bank, ident_b[:, :], mask_w[:, :, :], start=False, stop=False)
                    nc.tensor.matmul(bank, group_b[:, g, :], s.rows[:, :, :], start=False, stop=True)\
                        .then_inc(s.scores_t_psum, 4)
                    yield

            def self_stage(v):
                s = SELF
                pe.wait_ge(s.x_copied, v + STEP)
                if again(v):
                    pe.wait_ge(s.y_ready, v)
                nc.tensor.transpose(s.b0[:, 0:128], s.x[:, :], ident).then_inc(s.xT_psum, STEP)
                yield
                for g in range(G):
                    bank = s.b0 if g % 2 else s.b1
                    if g == 0:
                        pe.wait_ge(s.xT_ready, v + STEP)
                    if g >= 2:
                        pe.wait_ge(s.z_ready, v + 4 * (g - 1))
                    nc.tensor.matmul(bank, s.xT[:, :], wz[:, 512 * g:512 * g + 512], start=True, stop=True)\
                        .then_inc(s.z_psum, 4)
                    yield
                pe.wait_ge(s.z_ready, v + STEP)
                yield from core16(s, v)
                for n, (h0, hn) in enumerate(SETS):
                    bank = s.b1 if n % 2 else s.b0
                    pe.wait_ge(s.exp_done, v + 4 * max((h0 + hn - 1) // GH + 1, 3 + n if n < 2 else 0))
                    if n >= 2:
                        pe.wait_ge(s.y_ready, v + 2 * (n - 1))
                    for j in range(hn):
                        last = nc.tensor.matmul(bank[:, 129 * j:129 * j + 129], s.e[:, h0 + j, :],
                                                s.z[:, h0 + j, :], start=True, stop=True)
                    last.then_inc(s.av_psum, SET_UP[n])
                    yield
                for _ in range(4):
                    yield

            def cross_stage(v):
                s = CROSS
                pe.wait_ge(s.c_loaded, v + STEP)
                if again(v):
                    pe.wait_ge(s.o_ready, v)
                nc.tensor.transpose(s.b0[:, 0:128], s.cin[:, :], ident).then_inc(s.cT_psum, STEP)
                yield
                pe.wait_ge(s.cT_ready, v + STEP)
                if again(v):
                    pe.wait_ge(s.resid, v)
                nc.tensor.matmul(s.b1[:, 0:128], wk_s[:, :], s.cT[:, :], start=True, stop=True).then_inc(s.kT_psum, STEP)
                nc.tensor.matmul(s.b0[:, 0:128], s.cT[:, :], wv_s[:, :], start=True, stop=True).then_inc(s.v_psum, STEP)
                yield
                pe.wait_ge(s.x_copied, v + STEP)
                pe.wait_ge(s.kT_ready, v + STEP)
                nc.tensor.transpose(s.b1[:, 0:128], s.x[:, :], ident).then_inc(s.xT_psum, STEP)
                yield
                pe.wait_ge(s.xT_ready, v + STEP)
                pe.wait_ge(s.v_ready, v + STEP)
                nc.tensor.matmul(s.b0[:, 0:128], wq_s[:, :], s.xT[:, :], start=True, stop=True).then_inc(s.q_psum, STEP)
                yield
                pe.wait_ge(s.q_wide, v + STEP)
                yield from core16(s, v)
                pe.wait_ge(s.exp_done, v + STEP)
                for j in range(GH):
                    for g in range(G):
                        last = nc.tensor.matmul(s.b1[32 * g:32 * g + 32, 0:128], own[:, j, 32 * g:32 * g + 32],
                                                s.e[:, GH * g + j, :], start=(j == 0), stop=(j == GH - 1))
                last.then_inc(s.av_psum, 8)
                yield
                pe.wait_ge(s.v_own, v + STEP)
                for j in range(GH):
                    for g in range(G):
                        last = nc.tensor.matmul(s.b0[32 * g:32 * g + 32, 0:128], s.vm[:, j, 32 * g:32 * g + 32],
                                                s.e[:, GH * g + j, :], start=(j == 0), stop=(j == GH - 1))
                last.then_inc(s.av_psum, 8)
                yield
                pe.wait_ge(s.o_ready, v + STEP)
                last = nc.tensor.matmul(s.b1[:, 0:128], s.o[:, :], wo_s[:, :], start=True, stop=True)
                last.then_inc(s.proj_psum, STEP)
                yield
                for _ in range(3):
                    yield

            def masked_scores(s, g, bank):
                for p in range(2):
                    nc.tensor.matmul(bank[:, 256 * p:256 * p + 256], s.k[:, 2 * g + p, :], s.q[:, 2 * g + p, :, :],
                                     start=(p == 0), stop=False, skip_group_check=True)
                nc.tensor.matmul(bank, ident_b[:, :], mask_t[:, :, :], start=False, stop=False, skip_group_check=True)

            def local_stage(l, v):
                s = LOC[l]
                pe.wait_ge(s.x_copied, v + STEP)
                if again(v):
                    pe.wait_ge(s.resid, v)
                nc.tensor.transpose(s.b0[:, 0:128], s.x[:, 0, :], ident).then_inc(s.xT_psum, STEP)
                yield
                pe.wait_ge(s.xT_ready, v + STEP)
                nc.tensor.matmul(s.b1, s.xT[:, :], wqkv_s[l][:, 0:INNER], start=True, stop=True)
                yield
                nc.tensor.matmul(s.b0, s.xT[:, :], wqkv_s[l][:, INNER:2 * INNER], start=True, stop=True)\
                    .then_inc(s.qkv_psum, STEP)
                yield
                yield
                pe.wait_ge(s.qk_norm, v + STEP)
                nc.tensor.matmul(s.b0, s.xT[:, :], wqkv_s[l][:, 2 * INNER:3 * INNER], start=True, stop=True)\
                    .then_inc(s.v_psum, STEP)
                yield
                yield
                pe.wait_ge(s.roped, v + STEP)
                for p in range(LH // 2):
                    last = nc.tensor.transpose(s.b1[:, 128 * p:128 * p + 128],
                                               s.qr[:, INNER + 128 * p:INNER + 128 * p + 128], ident)
                last.then_inc(s.qkT_psum, 8)
                pe.wait_ge(s.v_ready, v + STEP)
                for p in range(LH // 2):
                    last = nc.tensor.transpose(s.b0[:, 128 * p:128 * p + 128], s.qr[:, 128 * p:128 * p + 128], ident)
                last.then_inc(s.qkT_psum, 8)
                yield
                yield
                pe.wait_ge(s.q_low, v + STEP)
                pe.wait_ge(s.k_low, v + STEP)
                for g in range(2):
                    bank = s.b0 if g else s.b1
                    for j in range(GH):
                        nc.tensor.matmul(bank[:, 128 * j:128 * j + 128], s.qb[:, 2 * g + j // 2, j % 2, :],
                                         s.kb[:, 2 * g + j // 2, :], start=(j == 0), stop=False,
                                         skip_group_check=True)
                    nc.tensor.matmul(bank, ident_b[:, :], mask_n[:, :, :], start=False, stop=True,
                                     skip_group_check=True).then_inc(s.scores_n_psum, 8)
                    yield
                pe.wait_ge(s.max_done, v + STEP)
                masked_scores(s, 0, s.b0)
                yield
                max_to_rows(s, v)
                yield
                pe.wait_ge(s.rows_ready, v + STEP)
                nc.tensor.matmul(s.b0, group_b[:, 0, :], s.rows[:, :, :], start=False, stop=True,
                                 skip_group_check=True).then_inc(s.scores_t_psum, 8)
                masked_scores(s, 1, s.b1)
                nc.tensor.matmul(s.b1, group_b[:, 1, :], s.rows[:, :, :], start=False, stop=True,
                                 skip_group_check=True).then_inc(s.scores_t_psum, 8)
                yield
                yield
                pe.wait_ge(s.exp_done, v + STEP)
                pe.wait_ge(s.v_ready, v + STEP)
                for g in range(2):
                    bank = s.b1 if g else s.b0
                    for j in range(GH):
                        last = nc.tensor.matmul(bank[:, (LD + 1) * j:(LD + 1) * j + LD + 1], s.e[:, GH * g + j, :],
                                                s.v[:, GH * g + j, :], start=True, stop=True)
                    last.then_inc(s.av_psum, 8)
                yield
                pe.wait_ge(s.o_ready, v + STEP)
                for p in range(LH // 2):
                    last = nc.tensor.transpose(s.b0[:, 128 * p:128 * p + 128], s.o[:, 128 * p:128 * p + 128], ident)
                last.then_inc(s.oT_psum, STEP)
                yield
                pe.wait_ge(s.oT_ready, v + STEP)
                for p in range(LH // 2):
                    last = nc.tensor.matmul(s.b1[:, 0:128], s.oT[:, p, :], wo3_s[l][:, p, :],
                                            start=(p == 0), stop=(p == LH // 2 - 1))
                last.then_inc(s.proj_psum, STEP)
                yield
                pe.wait_ge(s.mid_done, v + STEP)
                nc.tensor.matmul(s.b0[:, 0:64], shift_m, s.mid[:, 64:128], start=True, stop=True)\
                    .then_inc(s.shifted_psum, STEP)
                yield
                pe.wait_ge(s.hnorm, v + STEP)
                nc.tensor.transpose(s.b1[:, 0:128], s.hn[:, :], ident).then_inc(s.hT_psum, STEP)
                yield
                pe.wait_ge(s.hT_ready, v + STEP)
                for c in range(3):
                    lo = HID + FO[c]
                    last = nc.tensor.matmul(s.b0[0:FC[c], 128 * c:128 * c + 128], w1_s[l][:, lo:lo + FC[c]],
                                            s.hT[:, :], start=True, stop=True)
                last.then_inc(s.mlp_in_psum, 8)
                for c in range(3):
                    last = nc.tensor.matmul(s.b1[0:FC[c], 128 * c:128 * c + 128], w1_s[l][:, FO[c]:FO[c] + FC[c]],
                                            s.hT[:, :], start=True, stop=True)
                last.then_inc(s.mlp_in_psum, 8)
                yield
                pe.wait_ge(s.hid_done, v + STEP)
                for c in range(3):
                    last = nc.tensor.matmul(s.b0[:, 0:128], s.hid[0:FC[c], c, :], w2_s[l][0:FC[c], c, :],
                                            start=(c == 0), stop=(c == 2))
                last.then_inc(s.mlp_psum, STEP)
                yield
                yield

            stages(nc.tensor, self_stage, cross_stage, local_stage)


        @block.scalar
        def _(act):
            act.wait_ge(loaded, ALL_LOADED)
            act.wait_ge(prep_v, N_PREP_V + 8)

            def exps(s, v, g, n):
                bank = s.b1 if g % 2 else s.b0
                act.wait_ge(s.scores_t_psum, v + STEP // n * (g + 1))
                nc.scalar.activation(s.e[:, GH * g:GH * g + GH, :], bank.rearrange("p (j t) -> p j t", j=GH), ACT.Exp)\
                    .then_inc(s.exp_done, STEP // n)

            def self_stage(v):
                s = SELF
                act.wait_ge(s.xT_psum, v + STEP)
                nc.scalar.activation(s.xT[:, :], s.b0[:, 0:128], ACT.Copy).then_inc(s.xT_ready, STEP)
                yield
                for g in range(G):
                    bank = s.b0 if g % 2 else s.b1
                    act.wait_ge(s.z_psum, v + 4 * g + 4)
                    nc.scalar.activation(s.z[:, GH * g:GH * g + GH, 0:128], bank.rearrange("p (j n) -> p j n", j=GH), ACT.Copy)\
                        .then_inc(s.z_ready, 4)
                    yield
                for _ in range(6):
                    yield
                for g in range(G):
                    exps(s, v, g, G)
                    yield
                for _ in range(10):
                    yield

            def cross_stage(v):
                s = CROSS
                act.wait_ge(s.cT_psum, v + STEP)
                nc.scalar.activation(s.cT[:, :], s.b0[:, 0:128], ACT.Copy).then_inc(s.cT_ready, STEP)
                yield
                act.wait_ge(s.kT_psum, v + STEP)
                nc.scalar.activation(s.k[:, :], s.b1[:, 0:128], ACT.Identity, bias=bk_c[:, :]).then_inc(s.kT_ready, STEP)
                yield
                act.wait_ge(s.xT_psum, v + STEP)
                nc.scalar.activation(s.xT[:, :], s.b1[:, 0:128], ACT.Copy).then_inc(s.xT_ready, STEP)
                yield
                for _ in range(7):
                    yield
                for g in range(G):
                    exps(s, v, g, G)
                    yield
                for _ in range(6):
                    yield

            def local_stage(l, v):
                s = LOC[l]
                act.wait_ge(s.xT_psum, v + STEP)
                nc.scalar.activation(s.xT[0:64, :], s.b0[0:64, 0:128], ACT.Copy).then_inc(s.xT_ready, 8)
                nc.scalar.activation(s.xT[64:128, 1:128], s.b0[64:128, 0:127], ACT.Copy).then_inc(s.xT_ready, 8)
                yield
                yield
                act.wait_ge(s.qkv_psum, v + STEP)
                nc.scalar.activation(s.sq, s.ps[:, :].rearrange("p (h d) -> p h d", d=LD), ACT.Square)\
                    .then_inc(s.squares, STEP)
                yield
                yield
                act.wait_ge(s.v_psum, v + STEP)
                nc.scalar.activation(s.v[:, :, 0:LD], s.b0.rearrange("p (h d) -> p h d", h=LH), ACT.Copy).then_inc(s.v_ready, STEP)
                yield
                yield
                act.wait_ge(s.qkT_psum, v + 8)
                for a in range(2):
                    nc.scalar.activation(s.q[64 * a:64 * a + 64, :, a, :],
                                         s.b1[64 * a:64 * a + 64, :].rearrange("p (c t) -> p c t", c=LH // 2), ACT.Copy)\
                        .then_inc(s.q_split, 8)
                act.wait_ge(s.qkT_psum, v + STEP)
                nc.scalar.activation(s.k[:, :, :], s.b0.rearrange("p (c t) -> p c t", c=LH // 2), ACT.Copy)\
                    .then_inc(s.kT_ready, STEP)
                yield
                for _ in range(5):
                    yield
                exps(s, v, 0, 2)
                yield
                exps(s, v, 1, 2)
                yield
                yield
                act.wait_ge(s.oT_psum, v + STEP)
                nc.scalar.activation(s.oT[:, :, :], s.b0.rearrange("p (c t) -> p c t", c=LH // 2), ACT.Copy)\
                    .then_inc(s.oT_ready, STEP)
                yield
                for _ in range(2):
                    yield
                act.wait_ge(s.hT_psum, v + STEP)
                nc.scalar.activation(s.hT[:, :], s.b1[:, 0:128], ACT.Copy).then_inc(s.hT_ready, STEP)
                yield
                act.wait_ge(s.mlp_in_psum, v + 8)
                for c in range(3):
                    last = nc.scalar.activation(s.gate[0:FC[c], c, :], s.b0[0:FC[c], 128 * c:128 * c + 128], ACT.Gelu,
                                                bias=b1_s[l][0:FC[c], 3 + c:4 + c])
                last.then_inc(s.gelu_done, STEP)
                yield
                yield
                yield

            stages(nc.scalar, self_stage, cross_stage, local_stage)

        @block.vector
        def _(dve):
            for s in LOC:
                nc.vector.memset(s.v[:, :, LD:LD + 1], 1.0).then_inc(prep_v, 1)
            nc.vector.memset(SELF.z[:, :, 128:129], 1.0).then_inc(prep_v, 1)
            for s in (SELF, CROSS, LOC[0], LOC[1]):
                nc.vector.memset(s.neg[:, :], 0.0).then_inc(prep_v, 1)
            for s in LOC:
                nc.vector.memset(s.q[:, :, :, :], 0.0).then_inc(prep_v, 1)
                nc.vector.memset(s.xT[64:128, 0:1], 0.0).then_inc(prep_v, 1)
            dve.wait_ge(loaded, ALL_LOADED)
            for l in range(2):
                nc.vector.tensor_scalar(w1_s[l][:, :], w1_r[l][:, :], lg_c[l][:, :], None, ALU.mult).then_inc(prep_v, 1)
            for l in range(2):
                nc.vector.tensor_tensor(cos_t[l][:, :, :], scale_r[l][:, :, :],
                                        con[:, C_COS:C_COS + 2 * LD].rearrange("p (a d) -> p a d", a=2), ALU.mult)\
                    .then_inc(prep_v, 1)
                nc.vector.tensor_tensor(sin_t[l][:, :, :], scale_x[l][:, :, :],
                                        con[:, C_SIN:C_SIN + 2 * LD].rearrange("p (a d) -> p a d", a=2), ALU.mult)\
                    .then_inc(prep_v, 1)
            dve.wait_ge(prep_mm, 1)
            for l in range(2):
                for c0, c1, f in ((0, 2, FC[0]), (2, 3, FC[2]), (3, 5, FC[0]), (5, 6, FC[2])):
                    nc.vector.tensor_tensor(b1_s[l][0:f, c0:c1], LOC[l].b0[0:f, c0:c1], b1_r[l][0:f, c0:c1], ALU.add)\
                        .then_inc(prep_v, 1)
            dve.wait_ge(prep_p, N_PREP_P)

            def row_max(s, v, g, bank, n):
                dve.wait_ge(s.scores_n_psum, v + STEP // n * (g + 1))
                nc.vector.tensor_reduce(s.m[:, GH * g:GH * g + GH], bank.rearrange("p (j t) -> p j t", j=GH), AX.X, ALU.max)\
                    .then_inc(s.max_done, STEP // n)

            def split_max(s, v):
                h = s.heads
                dve.wait_ge(s.max_done, v + STEP)
                nc.vector.tensor_scalar(s.neg[:, 0:h], s.m[:, :], -1.0, None, ALU.mult).then_inc(s.neg_split, 8)
                dve.wait_ge(s.neg_split, v + 8)
                nc.vector.scalar_tensor_tensor(out=s.neg[:, 16:16 + h], in0=s.m[:, :], scalar=-1.0, in1=s.neg[:, 0:h],
                                               op0=ALU.mult, op1=ALU.subtract).then_inc(s.neg_split, 8)

            def spread_rows(s, v):
                dve.wait_ge(s.rows_psum, v + STEP)
                nc.vector.tensor_tensor(s.rows[:, :, :],
                                        s.b1.bitcast(BF16)[:, 0:128].unsqueeze(1).to_broadcast([128, GH, 128]),
                                        row_mask.unsqueeze(2).to_broadcast([128, GH, 128]), ALU.mult)\
                    .then_inc(s.rows_ready, STEP)

            def moments(s, v):
                dve.wait_ge(s.resid, v + STEP)
                nc.vector.bn_stats(s.st[:, 0, :], s.r[:, :]).then_inc(s.moments, 8)
                dve.wait_ge(s.moments, v + 8)
                nc.vector.bn_aggr(s.mv[:, :], s.st[:, 0, :]).then_inc(s.moments, 8)

            def normalise(s, v, out):
                dve.wait_ge(s.rstd, v + STEP)
                nc.vector.tensor_scalar(out, s.r[:, :], s.mv[:, 0:1], s.rs[:, :], ALU.subtract, ALU.mult)\
                    .then_inc(s.normed, STEP)

            def self_stage(v):
                s = SELF
                yield
                dve.wait_ge(s.xT_ready, v + STEP)
                for a in range(2):
                    nc.vector.tensor_tensor(s.q[:, 8 * a:8 * a + 8, :], s.xT[:, :].unsqueeze(1).to_broadcast([128, 8, 128]),
                                            head_mask[:, 8 * a:8 * a + 8].unsqueeze(2).to_broadcast([128, 8, 128]), ALU.mult)\
                        .then_inc(s.q_wide, 8)
                yield
                for _ in range(3):
                    yield
                for g in range(G):
                    row_max(s, v, g, s.b0 if g % 2 else s.b1, G)
                    yield
                split_max(s, v)
                yield
                spread_rows(s, v)
                yield
                for _ in range(4):
                    yield
                done = 0
                for n, (h0, hn) in enumerate(SETS):
                    done += SET_UP[n]
                    bank = (s.b1 if n % 2 else s.b0)[:, 0:129 * hn].rearrange("p (j n) -> p j n", n=129)
                    dve.wait_ge(s.av_psum, v + done)
                    nc.vector.reciprocal(s.rd[:, h0:h0 + hn].unsqueeze(2), bank[:, :, 128:129]).then_inc(s.rden, SET_UP[n])
                    dve.wait_ge(s.rden, v + done)
                    nc.vector.tensor_tensor(s.y[:, h0:h0 + hn, :], bank[:, :, 0:128],
                                            s.rd[:, h0:h0 + hn].unsqueeze(2).to_broadcast([128, hn, 128]), ALU.mult)\
                        .then_inc(s.y_ready, SET_UP[n])
                    yield
                yield
                dve.wait_ge(s.tree, v + STEP)
                nc.vector.tensor_tensor(s.r[:, :], s.y[:, 0, :], s.y[:, 1, :], ALU.add).then_inc(s.resid, 8)
                dve.wait_ge(s.resid, v + 8)
                nc.vector.tensor_tensor(s.r[:, :], s.r[:, :], s.x[:, :], ALU.add).then_inc(s.resid, 8)
                moments(s, v)
                yield
                yield
                if again(v):
                    dve.wait_ge(CROSS.x_bias, v)
                normalise(s, v, s.out[:, :])
                yield

            def cross_stage(v):
                s = CROSS
                yield
                dve.wait_ge(s.v_psum, v + STEP)
                nc.vector.tensor_tensor(s.v[:, :], s.b0[:, 0:128], bv_r[:, :], ALU.add).then_inc(s.v_ready, STEP)
                yield
                yield
                dve.wait_ge(s.q_psum, v + STEP)
                for a in range(2):
                    nc.vector.scalar_tensor_tensor(
                        out=s.q[:, 8 * a:8 * a + 8, :], in0=s.b0[:, 0:128].unsqueeze(1).to_broadcast([128, 8, 128]),
                        scalar=bq_c[:, :], in1=head_mask[:, 8 * a:8 * a + 8].unsqueeze(2).to_broadcast([128, 8, 128]),
                        op0=ALU.add, op1=ALU.mult).then_inc(s.q_wide, 8)
                yield
                for g in range(G):
                    row_max(s, v, g, s.b0 if g % 2 else s.b1, G)
                    yield
                split_max(s, v)
                yield
                spread_rows(s, v)
                yield
                for _ in range(4):
                    yield
                dve.wait_ge(s.av_psum, v + 8)
                nc.vector.reciprocal(s.o[:, :], s.b1[:, 0:128]).then_inc(s.inverse, STEP)
                yield
                dve.wait_ge(s.inverse, v + STEP)
                dve.wait_ge(s.av_psum, v + STEP)
                nc.vector.tensor_tensor(s.o[:, :], s.b0[:, 0:128], s.o[:, :], ALU.mult).then_inc(s.o_ready, STEP)
                yield
                dve.wait_ge(s.proj_psum, v + STEP)
                dve.wait_ge(s.x_bias, v + STEP)
                nc.vector.tensor_tensor(s.r[:, :], s.b1[:, 0:128], s.xb[:, :], ALU.add).then_inc(s.resid, STEP)
                moments(s, v)
                yield
                yield
                if again(v):
                    dve.wait_ge(LOC[0].x_copied, v)
                normalise(s, v, s.out[:, :])
                yield
                yield

            def local_stage(l, v):
                s = LOC[l]
                yield
                yield
                dve.wait_ge(s.squares, v + STEP)
                nc.vector.tensor_reduce(s.ss[:, :], s.sq, AX.X, ALU.add).then_inc(s.square_sum, STEP)
                yield
                dve.wait_ge(s.rnorm, v + STEP)
                nc.vector.tensor_tensor(s.qk[:, :, :, :].rearrange("p a h d -> p (a h) d"),
                                        s.ps[:, :].rearrange("p (h d) -> p h d", d=LD),
                                        s.rn[:, :].unsqueeze(2).to_broadcast([128, 2 * LH, LD]), ALU.mult)\
                    .then_inc(s.qk_norm, STEP)
                yield
                dve.wait_ge(s.qk_norm, v + STEP)
                nc.vector.tensor_tensor(s.qc[:, :, :, :], s.qk[:, :, :, :],
                                        cos_t[l][:, :, :].unsqueeze(2).to_broadcast([128, 2, LH, LD]), ALU.mult)\
                    .then_inc(s.rot_cos, STEP)
                yield
                dve.wait_ge(s.rot_cos, v + STEP)
                dve.wait_ge(s.rot_sin, v + STEP)
                nc.vector.tensor_tensor(s.qr, s.qr,
                                        s.qs[:, :, :, :].rearrange("p a h d -> p (a h d)"), ALU.add).then_inc(s.roped, STEP)
                yield
                yield
                yield
                for g in range(2):
                    row_max(s, v, g, s.b0 if g else s.b1, 2)
                    yield
                split_max(s, v)
                yield
                spread_rows(s, v)
                yield
                for _ in range(2):
                    yield
                for g in range(2):
                    bank = (s.b1 if g else s.b0)[:, 0:GH * (LD + 1)].rearrange("p (j d) -> p j d", j=GH)
                    dve.wait_ge(s.av_psum, v + 8 * g + 8)
                    nc.vector.reciprocal(s.rd[:, GH * g:GH * g + GH].unsqueeze(2), bank[:, :, LD:LD + 1]).then_inc(s.inverse, 8)
                    dve.wait_ge(s.inverse, v + 8 * g + 8)
                    nc.vector.tensor_tensor(s.o[:, 256 * g:256 * g + 256].rearrange("p (j d) -> p j d", j=GH), bank[:, :, 0:LD],
                                            s.rd[:, GH * g:GH * g + GH].unsqueeze(2).to_broadcast([128, GH, LD]), ALU.mult)\
                        .then_inc(s.o_ready, 8)
                yield
                yield
                dve.wait_ge(s.proj_psum, v + STEP)
                nc.vector.tensor_tensor(s.mid[:, :], s.b1[:, 0:128], s.x[:, 0, :], ALU.add).then_inc(s.mid_done, STEP)
                yield
                dve.wait_ge(s.mid_done, v + STEP)
                nc.vector.bn_stats(s.st[:, 0, :], s.mid[:, 0:64]).then_inc(s.mid_moments, 4)
                dve.wait_ge(s.shifted_psum, v + STEP)
                nc.vector.bn_stats(s.st[:, 1, :], s.b0[:, 0:64]).then_inc(s.mid_moments, 4)
                dve.wait_ge(s.mid_moments, v + 8)
                nc.vector.bn_aggr(s.mv2[:, :], s.st[:, :, :].rearrange("p a b -> p (a b)")).then_inc(s.mid_moments, 8)
                yield
                dve.wait_ge(s.mid_rstd, v + STEP)
                nc.vector.tensor_scalar(s.hn[:, 0:64], s.mid[:, 0:64], s.mv2[:, 0:1], s.rs2[:, :],
                                        ALU.subtract, ALU.mult).then_inc(s.hnorm, 8)
                nc.vector.tensor_scalar(s.hn[:, 64:128], s.b0[:, 0:64], s.mv2[:, 0:1], s.rs2[:, :],
                                        ALU.subtract, ALU.mult).then_inc(s.hnorm, 8)
                yield
                dve.wait_ge(s.mlp_in_psum, v + STEP)
                dve.wait_ge(s.gelu_done, v + STEP)
                for c in range(3):
                    last = nc.vector.scalar_tensor_tensor(
                        out=s.hid[0:FC[c], c, :], in0=s.b1[0:FC[c], 128 * c:128 * c + 128], scalar=b1_s[l][0:FC[c], c:c + 1],
                        in1=s.gate[0:FC[c], c, :], op0=ALU.add, op1=ALU.mult)
                last.then_inc(s.hid_done, STEP)
                yield
                dve.wait_ge(s.mlp_psum, v + STEP)
                dve.wait_ge(s.mid_bias, v + STEP)
                if l == 0:
                    if again(v):
                        dve.wait_ge(LOC[1].x_copied, v)
                    nc.vector.tensor_tensor(s.out[:, 0, :], s.b0[:, 0:128], s.midb[:, :], ALU.add).then_inc(s.resid, STEP)
                    yield
                else:
                    nc.vector.tensor_tensor(s.r[:, :], s.b0[:, 0:128], s.midb[:, :], ALU.add).then_inc(s.resid, STEP)
                    moments(s, v)
                    yield
                    if again(v):
                        dve.wait_ge(stored, v)
                    normalise(s, v, s.out[:, 0, :])
                yield

            stages(nc.vector, self_stage, cross_stage, local_stage)

        @block.gpsimd
        def _(pool):
            nc.gpsimd.memset(half_neg[:, :], -0.5).then_inc(prep_p, 1)
            pool.wait_ge(loaded, ALL_LOADED)

            def copy(out, in_):
                return nc.gpsimd.tensor_scalar(out, in_, 1.0, 0.0, ALU.mult, ALU.add)

            copy(ident_b[:, :], ident).then_inc(prep_p, 1)
            copy(group_b[:, :, :], con[:, C_GRP:C_GRP + 512].rearrange("p (g t) -> p g t", g=4)).then_inc(prep_p, 1)
            for tile, at_ in ((mask_n, C_MASKN), (mask_t, C_MASKT), (mask_w, C_BAND)):
                copy(tile[:, :, :], con[:, at_:at_ + 128].unsqueeze(1).to_broadcast([128, GH, 128])).then_inc(prep_p, 1)
            pool.wait_ge(prep_v, N_PREP_V + 8)

            def inverse_root(s, v, moments_done, mv, out, done):
                pool.wait_ge(moments_done, v + STEP)
                nc.gpsimd.tensor_scalar(s.ve[:, :], mv[:, 1:2], EPS, 1.0, ALU.add, ALU.mult).then_inc(done, 8)
                pool.wait_ge(done, v + 8)
                nc.gpsimd.tensor_tensor(out, s.ve[:, :], half_neg[:, 0:1], ALU.pow).then_inc(done, 8)

            def low_queries(s, v):
                for a in range(2):
                    pool.wait_ge(s.q_wide, v + 8 * a + 8)
                    copy(s.qb[:, 8 * a:8 * a + 8, :], s.q[:, 8 * a:8 * a + 8, :]).then_inc(s.q_low, 8)

            def self_stage(v):
                s = SELF
                pool.wait_ge(s.x_loaded, v + STEP)
                if again(v):
                    pool.wait_ge(s.resid, v)
                copy(s.x[:, :], s.xin[:, :]).then_inc(s.x_copied, STEP)
                yield
                pool.wait_ge(s.xT_ready, v + STEP)
                copy(s.kb[:, :], s.xT[:, :]).then_inc(s.k_low, STEP)
                low_queries(s, v)
                yield
                for _ in range(15):
                    yield
                pool.wait_ge(s.y_ready, v + 6)
                nc.gpsimd.tensor_tensor(s.y[:, 0:4, :], s.y[:, 0:4, :], s.y[:, 4:8, :], ALU.add).then_inc(s.tree, 4)
                yield
                yield
                yield
                pool.wait_ge(s.y_ready, v + STEP)
                nc.gpsimd.tensor_tensor(s.y[:, 8:12, :], s.y[:, 8:12, :], s.y[:, 12:16, :], ALU.add).then_inc(s.tree, 4)
                pool.wait_ge(s.tree, v + 8)
                nc.gpsimd.tensor_tensor(s.y[:, 0:4, :], s.y[:, 0:4, :], s.y[:, 8:12, :], ALU.add).then_inc(s.tree, 4)
                pool.wait_ge(s.tree, v + 12)
                nc.gpsimd.tensor_tensor(s.y[:, 0:2, :], s.y[:, 0:2, :], s.y[:, 2:4, :], ALU.add).then_inc(s.tree, 4)
                yield
                yield
                inverse_root(s, v, s.moments, s.mv, s.rs[:, :], s.rstd)
                yield
                yield
                yield

            def cross_stage(v):
                s = CROSS
                pool.wait_ge(SELF.normed, v + STEP)
                if again(v):
                    pool.wait_ge(s.resid, v)
                copy(s.x[:, :], SELF.out[:, :]).then_inc(s.x_copied, STEP)
                nc.gpsimd.tensor_tensor(s.xb[:, :], SELF.out[:, :], bo_r[:, :], ALU.add).then_inc(s.x_bias, STEP)
                yield
                pool.wait_ge(s.kT_ready, v + STEP)
                copy(s.kb[:, :], s.k[:, :]).then_inc(s.k_low, STEP)
                yield
                pool.wait_ge(s.v_ready, v + STEP)
                nc.gpsimd.tensor_tensor(s.vm[:, :, :], s.v[:, :].unsqueeze(1).to_broadcast([128, GH, 128]), own, ALU.mult)\
                    .then_inc(s.v_own, STEP)
                yield
                low_queries(s, v)
                yield
                for _ in range(12):
                    yield
                inverse_root(s, v, s.moments, s.mv, s.rs[:, :], s.rstd)
                yield
                for _ in range(3):
                    yield

            def local_stage(l, v):
                s = LOC[l]
                if l == 0:
                    pool.wait_ge(CROSS.normed, v + STEP)
                    if again(v):
                        pool.wait_ge(s.mid_done, v)
                        pool.wait_ge(s.kept, v)
                    copy(s.x[:, 0, :], CROSS.out[:, :]).then_inc(s.x_copied, STEP)
                else:
                    pool.wait_ge(LOC[0].resid, v + STEP)
                    pool.wait_ge(LOC[0].kept, v + STEP)
                    if again(v):
                        pool.wait_ge(s.mid_done, v)
                        pool.wait_ge(s.base_bias, v)
                    copy(s.x[:, :, :], LOC[0].out[:, :, :]).then_inc(s.x_copied, STEP)
                yield
                pool.wait_ge(s.x_copied, v + STEP)
                if l == 0:
                    if again(v):
                        pool.wait_ge(LOC[1].x_copied, v)
                    copy(s.out[:, 1, :], s.x[:, 0, :]).then_inc(s.kept, STEP)
                else:
                    if again(v):
                        pool.wait_ge(s.mid_bias, v)
                    nc.gpsimd.tensor_tensor(s.base[:, :], s.x[:, 1, :], b2_r[l][:, :], ALU.add).then_inc(s.base_bias, STEP)
                yield
                yield
                pool.wait_ge(s.square_sum, v + STEP)
                nc.gpsimd.tensor_scalar(s.sc[:, :], s.ss[:, :], 1e-24, 1.0, ALU.max, ALU.mult).then_inc(s.rnorm, 8)
                pool.wait_ge(s.rnorm, v + 8)
                nc.gpsimd.tensor_tensor(s.rn[:, :], s.sc[:, :], half_neg[:, :], ALU.pow).then_inc(s.rnorm, 8)
                yield
                pool.wait_ge(s.qk_norm, v + STEP)
                for a in range(2):
                    nc.gpsimd.tensor_tensor(
                        s.qs[:, a, :, :].rearrange("p h (u d) -> p h u d", u=2),
                        s.qk[:, a, :, :].rearrange("p h (u d) -> p h u d", u=2)[:, :, ::-1, :],
                        sin_t[l][:, a, :].rearrange("p (u d) -> p u d", u=2).unsqueeze(1).to_broadcast([128, LH, 2, LD // 2]),
                        ALU.mult).then_inc(s.rot_sin, 8)
                yield
                yield
                pool.wait_ge(s.q_split, v + STEP)
                copy(s.qb[:, :, :, :].rearrange("p c a t -> p (c a) t"), s.q[:, :, :, :].rearrange("p c a t -> p (c a) t"))\
                    .then_inc(s.q_low, STEP)
                pool.wait_ge(s.kT_ready, v + STEP)
                copy(s.kb[:, :, :], s.k[:, :, :]).then_inc(s.k_low, STEP)
                yield
                for _ in range(9):
                    yield
                pool.wait_ge(s.mid_done, v + STEP)
                addend = b2_r[l] if l == 0 else s.base
                if l == 1:
                    pool.wait_ge(s.base_bias, v + STEP)
                nc.gpsimd.tensor_tensor(s.midb[:, :], s.mid[:, :], addend[:, :], ALU.add).then_inc(s.mid_bias, STEP)
                yield
                inverse_root(s, v, s.mid_moments, s.mv2, s.rs2[:, :], s.mid_rstd)
                yield
                yield
                yield
                if l == 1:
                    inverse_root(s, v, s.moments, s.mv, s.rs[:, :], s.rstd)
                yield
                yield

            stages(nc.gpsimd, self_stage, cross_stage, local_stage)


def kernel(**inputs):
    import numpy as _np
    import concourse.bacc as _bacc
    from concourse import mybir as _mybir
    from concourse.bass_utils import run_bass_kernel_spmd as _run

    a = {k: _np.ascontiguousarray(v) for k, v in inputs.items()}
    w = a["L0_attn_weight"]
    arrays = {
        "x": a["x"], "ctx_in": a["ctx_1024"], "consts": shape_constants(),
        "w_heads": _np.ascontiguousarray(w.reshape(H, D, D).transpose(1, 0, 2)).reshape(D, H * D),
        "wqT": _np.ascontiguousarray(a["L0_xattn_Wq"].T), "bq": a["L0_xattn_bq"],
        "wkT": _np.ascontiguousarray(a["L0_xattn_Wk"].T), "bk": a["L0_xattn_bk"],
        "wvT": _np.ascontiguousarray(a["L0_xattn_Wv"].T), "bv": a["L0_xattn_bv"],
        "woT": _np.ascontiguousarray(a["L0_xattn_Wo"].T), "bo": a["L0_xattn_bo"],
    }
    for n in ("wqkv", "q_scale", "k_scale", "wo", "ln_g", "ln_b", "w1", "b1", "w2", "b2"):
        arrays[n] = a[f"L0_ffn_{n}"]
    nc = _bacc.Bacc("TRN2", target_bir_lowering=False, num_devices=1)
    args = [nc.dram_tensor(n, t.shape, _mybir.dt.from_np(t.dtype), kind="ExternalInput").ap()
            for n, t in arrays.items()]
    args.append(nc.dram_tensor("out", a["x"].shape, _mybir.dt.float32, kind="ExternalOutput").ap())
    decoder_kernel(nc, *args)
    r = _run(nc, [arrays], core_ids=[0])
    return r.results[0]["out"]
```

```python
from contextlib import ExitStack

import numpy as np

import concourse.bass as bass
from concourse import mybir

F32 = mybir.dt.float32
BF16 = mybir.dt.bfloat16
ALU = mybir.AluOpType
ACT = mybir.ActivationFunctionType
AX = mybir.AxisListType

T = 128
D = 128
H = 16
HD = D // H
GH = 4
G = H // GH
LH = 8
LD = 64
INNER = LH * LD
HID = 341
FC = (114, 114, 113)
FO = (0, 114, 228)
WINDOW = 64
EPS = 1e-5
MASKED = -1e30
STEP = 16
SETS = ((0, 3), (3, 3), (6, 3), (9, 3), (12, 3), (15, 1))
SET_UP = (2, 2, 2, 2, 2, 6)

C_ID = 0
C_SHIFT = C_ID + 128
C_MASKN = C_SHIFT + 128
C_MASKT = C_MASKN + 128
C_BAND = C_MASKT + 128
C_GRP = C_BAND + 128
C_HEAD = C_GRP + 4 * 128
C_ROW = C_HEAD + H
C_OWN = C_ROW + GH
C_COS = C_OWN + GH * 128
C_SIN = C_COS + 2 * LD
C_END = C_SIN + 2 * LD


ORDER_TENSOR = (
    "LSCLLMSSMSSCMSSCSSLCSSLMSSSLSMSSMLLCSCMMLCLMMLLCMMLLMMSCCMLSMLCMCSLCMCMM"
    "CCLMCLLL")
ORDER_VECTOR = (
    "SLSLLMLLCSSMSSLSSMSLMMLMMCMSCSLCLLMSLMMMLCSMSCSCLLMCMMMCLLCMSMLLSMMSMSLL"
    "SSLMCSCSMSCMCLCSMLL")
ORDER_SCALAR = (
    "LSLMLCLSSMSSCMCMLLSMLSSLSMMMLLMMMLCCCMCMLL")
ORDER_GPSIMD = (
    "LSCMLMSLLLLLMSMMLMCMCMLLCMMCSLMMMLLSSSSSCMCML")

def shape_constants():
    c = np.zeros((128, C_END), np.float32)
    p = np.arange(128)
    c[:, C_ID:C_ID + 128] = np.eye(128)
    c[:, C_SHIFT:C_SHIFT + 128] = np.eye(128, k=1)
    i, j = p[:, None], p[None, :]
    allowed = (j <= i) & (j >= i - WINDOW)
    c[:, C_MASKN:C_MASKN + 128] = np.where(allowed, 0.0, MASKED)
    c[:, C_MASKT:C_MASKT + 128] = np.where(allowed.T, 0.0, MASKED)
    c[:, C_BAND:C_BAND + 128] = np.where(np.abs(i - j) <= WINDOW, 0.0, MASKED)
    head = p % 16
    for g in range(4):
        rows = (p < 32) & (head // GH == g)
        c[:, C_GRP + 128 * g:C_GRP + 128 * (g + 1)] = rows[:, None]
    c[:, C_HEAD:C_HEAD + H] = (p[:, None] // HD == np.arange(H)) * np.float32(1.0 / np.sqrt(HD))
    c[:, C_ROW:C_ROW + GH] = (p[:, None] < 32) & (head[:, None] % GH == np.arange(GH))
    for n in range(GH):
        c[:, C_OWN + 128 * n:C_OWN + 128 * (n + 1)] = (p // HD) % GH == n
    half = np.arange(0, LD, 2, dtype=np.float32)
    inv = np.float32(1.0) / np.float32(10000.0) ** (half / np.float32(LD))
    t = np.arange(T, dtype=np.float32)
    freq = t[:, None] * inv[None, :]
    freq = np.concatenate([freq, freq], axis=-1)
    base = (half + np.float32(0.4 * LD)) / np.float32(1.4 * LD)
    power = (t - T // 2) / np.float32(WINDOW // 2)
    scale = base[None, :] ** power[:, None]
    scale = np.concatenate([scale, scale], axis=-1)
    sign = np.where(np.arange(LD) < LD // 2, -1.0, 1.0).astype(np.float32)
    cos, sin = np.cos(freq), np.sin(freq) * sign
    c[:, C_COS:C_COS + LD] = cos / scale
    c[:, C_COS + LD:C_COS + 2 * LD] = cos * scale * 8.0
    c[:, C_SIN:C_SIN + LD] = sin / scale
    c[:, C_SIN + LD:C_SIN + 2 * LD] = sin * scale * 8.0
    return c


def again(v):
    return not (isinstance(v, int) and v == 0)


def weave(order, parts):
    for letter in order:
        if letter in parts:
            next(parts[letter], None)
    for letter, part in parts.items():
        assert next(part, "end") == "end", (letter, "has steps that the order does not place")


class Stage:
    pass


def decoder_kernel(nc, x, ctx_in, consts, w_heads, wqT, bq, wkT, bk, wvT, bv, woT, bo,
                   wqkv, q_scale, k_scale, wo, ln_g, ln_b, w1, b1, w2, b2, out):
    B = x.shape[0]
    LAST = 4
    x_rows = x.rearrange("b t d -> (b t) d")
    ctx_rows = ctx_in.rearrange("b t d -> (b t) d")
    out_rows = out.rearrange("b t d -> (b t) d")

    with ExitStack() as ctx:
        def sb(name, shape, dt=F32):
            return ctx.enter_context(nc.sbuf_tensor(name, shape, dt))

        def sem(name):
            return ctx.enter_context(nc.semaphore(name))

        con = sb("con", [128, C_END])
        ident = con[:, C_ID:C_ID + 128]
        shift_m = con[:, C_SHIFT:C_SHIFT + 128]
        head_mask = con[:, C_HEAD:C_HEAD + H]
        row_mask = con[:, C_ROW:C_ROW + GH]
        own = con[:, C_OWN:C_OWN + GH * 128].rearrange("p (j c) -> p j c", j=GH)
        ident_b = sb("ident_b", [128, 128], BF16)
        mask_n = sb("mask_n", [128, GH, 128], BF16)
        mask_t = sb("mask_t", [128, GH, 128], BF16)
        mask_w = sb("mask_w", [128, GH, 128], BF16)
        group_b = sb("group_b", [128, G, 128], BF16)
        half_neg = sb("half_neg", [128, H])
        wz = sb("wz", [128, H * 128])
        wq_s, wk_s, wv_s, wo_s = (sb(n, [128, 128]) for n in ("wq_s", "wk_s", "wv_s", "wo_s"))
        bq_c, bk_c = sb("bq_c", [128, 1]), sb("bk_c", [128, 1])
        bv_r, bo_r = sb("bv_r", [128, 128]), sb("bo_r", [128, 128])
        wqkv_s = [sb(f"wqkv_s{l}", [128, 3 * INNER]) for l in range(2)]
        wo3_s = [sb(f"wo3_s{l}", [128, LH // 2, 128]) for l in range(2)]
        w1_r = [sb(f"w1_r{l}", [128, 2 * HID]) for l in range(2)]
        w1_s = [sb(f"w1_s{l}", [128, 2 * HID]) for l in range(2)]
        w2_s = [sb(f"w2_s{l}", [128, 3, 128]) for l in range(2)]
        b1_r = [sb(f"b1_r{l}", [128, 6]) for l in range(2)]
        b1_s = [sb(f"b1_s{l}", [128, 6]) for l in range(2)]
        lg_c = [sb(f"lg_c{l}", [128, 1]) for l in range(2)]
        lb_c = [sb(f"lb_c{l}", [128, 1]) for l in range(2)]
        b2_r = [sb(f"b2_r{l}", [128, 128]) for l in range(2)]
        scale_r = [sb(f"scale_r{l}", [128, 2, LD]) for l in range(2)]
        scale_x = [sb(f"scale_x{l}", [128, 2, LD]) for l in range(2)]
        cos_t = [sb(f"cos_t{l}", [128, 2, LD]) for l in range(2)]
        sin_t = [sb(f"sin_t{l}", [128, 2, LD]) for l in range(2)]

        loaded = sem("attention_weights_loaded")
        local_loaded = sem("local_weights_loaded")
        prep_v = sem("prepared_by_vector")
        prep_p = sem("prepared_by_pool")
        prep_mm = sem("bias_products")
        stored = sem("stored")

        def stage(name):
            s = Stage()
            s.ps = ctx.enter_context(nc.psum_tensor(f"{name}_ps", [128, 1024], F32))
            s.b0, s.b1 = s.ps[:, 0:512], s.ps[:, 512:1024]
            s.x_copied = sem(f"{name}_x_copied")
            s.xT_psum = sem(f"{name}_xT_psum")
            s.xT_ready = sem(f"{name}_xT_ready")
            s.q_low = sem(f"{name}_q_low")
            s.k_low = sem(f"{name}_k_low")
            s.scores_n_psum = sem(f"{name}_scores_n_psum")
            s.max_done = sem(f"{name}_max_done")
            s.neg_split = sem(f"{name}_neg_split")
            s.rows_psum = sem(f"{name}_rows_psum")
            s.rows_ready = sem(f"{name}_rows_ready")
            s.scores_t_psum = sem(f"{name}_scores_t_psum")
            s.exp_done = sem(f"{name}_exp_done")
            s.resid = sem(f"{name}_resid")
            return s

        def norm_signals(s, name):
            s.moments = sem(f"{name}_moments")
            s.rstd = sem(f"{name}_rstd")
            s.normed = sem(f"{name}_normed")

        def local_signals(s, name):
            s.qkv_psum = sem(f"{name}_qkv_psum")
            s.squares = sem(f"{name}_squares")
            s.square_sum = sem(f"{name}_square_sum")
            s.rnorm = sem(f"{name}_rnorm")
            s.qk_norm = sem(f"{name}_qk_norm")
            s.v_psum = sem(f"{name}_v_psum")
            s.v_ready = sem(f"{name}_v_ready")
            s.rot_sin = sem(f"{name}_rot_sin")
            s.rot_cos = sem(f"{name}_rot_cos")
            s.roped = sem(f"{name}_roped")
            s.qkT_psum = sem(f"{name}_qkT_psum")
            s.kT_ready = sem(f"{name}_kT_ready")
            s.q_split = sem(f"{name}_q_split")
            s.av_psum = sem(f"{name}_av_psum")
            s.inverse = sem(f"{name}_inverse")
            s.oT_psum = sem(f"{name}_oT_psum")
            s.oT_ready = sem(f"{name}_oT_ready")
            s.o_ready = sem(f"{name}_o_ready")
            s.proj_psum = sem(f"{name}_proj_psum")
            s.mid_done = sem(f"{name}_mid_done")
            s.mid_bias = sem(f"{name}_mid_bias")
            s.mid_moments = sem(f"{name}_mid_moments")
            s.mid_rstd = sem(f"{name}_mid_rstd")
            s.shifted_psum = sem(f"{name}_shifted_psum")
            s.hT_psum = sem(f"{name}_hT_psum")
            s.hT_ready = sem(f"{name}_hT_ready")
            s.hnorm = sem(f"{name}_hnorm")
            s.mlp_in_psum = sem(f"{name}_mlp_in_psum")
            s.gelu_done = sem(f"{name}_gelu_done")
            s.hid_done = sem(f"{name}_hid_done")
            s.mlp_psum = sem(f"{name}_mlp_psum")

        SELF, CROSS = stage("self"), stage("cross")
        LOC = [stage("local0"), stage("local1")]
        norm_signals(SELF, "self")
        norm_signals(CROSS, "cross")
        norm_signals(LOC[1], "local1")
        for l in range(2):
            local_signals(LOC[l], f"local{l}")
        SELF.q_wide = sem("self_q_wide")
        SELF.z_psum = sem("self_z_psum")
        SELF.z_ready = sem("self_z_ready")
        SELF.av_psum = sem("self_av_psum")
        SELF.rden = sem("self_rden")
        SELF.y_ready = sem("self_y_ready")
        SELF.tree = sem("self_tree")
        SELF.x_loaded = sem("self_x_loaded")
        CROSS.q_wide = sem("cross_q_wide")
        CROSS.c_loaded = sem("cross_c_loaded")
        CROSS.cT_psum = sem("cross_cT_psum")
        CROSS.cT_ready = sem("cross_cT_ready")
        CROSS.kT_psum = sem("cross_kT_psum")
        CROSS.kT_ready = sem("cross_kT_ready")
        CROSS.v_psum = sem("cross_v_psum")
        CROSS.v_ready = sem("cross_v_ready")
        CROSS.q_psum = sem("cross_q_psum")
        CROSS.av_psum = sem("cross_av_psum")
        CROSS.inverse = sem("cross_inverse")
        CROSS.v_own = sem("cross_v_own")
        CROSS.o_ready = sem("cross_o_ready")
        CROSS.proj_psum = sem("cross_proj_psum")
        CROSS.x_bias = sem("cross_x_bias")
        LOC[0].kept = sem("local0_kept")
        LOC[1].base_bias = sem("local1_base_bias")
        for s, n in ((SELF, "self"), (CROSS, "cross")):
            s.q = sb(f"{n}_q", [128, H, 128])
            s.qb = sb(f"{n}_qb", [128, H, 128], BF16)
            s.xT = sb(f"{n}_xT", [128, 128])
            s.kb = sb(f"{n}_kb", [128, 128], BF16)
            s.e = sb(f"{n}_e", [128, H, 128])
        for s, n, h in ((SELF, "self", H), (CROSS, "cross", H), (LOC[0], "local0", LH), (LOC[1], "local1", LH)):
            s.heads = h
            s.m = sb(f"{n}_m", [128, h])
            s.neg = sb(f"{n}_neg", [128, 128], BF16)
            s.rows = sb(f"{n}_rows", [128, GH, 128], BF16)
            s.st = sb(f"{n}_st", [128, 2, 6])
            s.mv2 = sb(f"{n}_mv2", [128, 2])
            s.rs2 = sb(f"{n}_rs2", [128, 1])
            s.mv = sb(f"{n}_mv", [128, 2])
            s.ve = sb(f"{n}_ve", [128, 1])
            s.rs = sb(f"{n}_rs", [128, 1])
            s.r = sb(f"{n}_r", [128, 128])
        SELF.windowed, CROSS.windowed = False, True
        SELF.xin = sb("self_xin", [128, 128])
        SELF.x = sb("self_x", [128, 128])
        SELF.k = SELF.xT
        SELF.z = sb("self_z", [128, H, 129])
        SELF.rd = sb("self_rd", [128, H])
        SELF.y = sb("self_y", [128, H, 128])
        SELF.out = sb("self_out", [128, 128])
        CROSS.cin = sb("cross_cin", [128, 128])
        CROSS.cT = sb("cross_cT", [128, 128])
        CROSS.k = sb("cross_k", [128, 128])
        CROSS.v = sb("cross_v", [128, 128])
        CROSS.x = sb("cross_x", [128, 128])
        CROSS.xb = sb("cross_xb", [128, 128])
        CROSS.vm = sb("cross_vm", [128, GH, 128])
        CROSS.o = sb("cross_o", [128, 128])
        CROSS.out = sb("cross_out", [128, 128])
        for l, s in enumerate(LOC):
            n = f"local{l}"
            s.x = sb(f"{n}_x", [128, 2, 128])
            s.xT = sb(f"{n}_xT", [128, 128])
            s.ss = sb(f"{n}_ss", [128, 2 * LH])
            s.sc = sb(f"{n}_sc", [128, 2 * LH])
            s.rn = sb(f"{n}_rn", [128, 2 * LH])
            s.qk = sb(f"{n}_qk", [128, 2, LH, LD])
            s.qs = sb(f"{n}_qs", [128, 2, LH, LD])
            s.sq = s.qs[:, :, :, :].rearrange("p a h d -> p (a h) d")
            s.qc = sb(f"{n}_qc", [128, 2, LH, LD])
            s.qr = s.qc[:, :, :, :].rearrange("p a h d -> p (a h d)")
            s.v = sb(f"{n}_v", [128, LH, LD + 1])
            s.k = sb(f"{n}_k", [128, LH // 2, 128])
            s.kb = sb(f"{n}_kb", [128, LH // 2, 128], BF16)
            s.q = sb(f"{n}_q", [128, LH // 2, 2, 128])
            s.qb = sb(f"{n}_qb", [128, LH // 2, 2, 128], BF16)
            s.e = sb(f"{n}_e", [128, LH, 128])
            s.rd = sb(f"{n}_rd", [128, LH])
            s.o = sb(f"{n}_o", [128, INNER])
            s.oT = sb(f"{n}_oT", [128, LH // 2, 128])
            s.mid = sb(f"{n}_mid", [128, 128])
            s.midb = sb(f"{n}_midb", [128, 128])
            s.hn = sb(f"{n}_hn", [128, 128])
            s.hT = sb(f"{n}_hT", [128, 128])
            s.gate = sb(f"{n}_gate", [128, 3, 128])
            s.hid = s.gate
            s.out = sb(f"{n}_out", [128, 2, 128])
            s.base = sb(f"{n}_base", [128, 128])

        block = ctx.enter_context(nc.Block())

        def loop(eng, iteration, prepare_local, before):
            fill = LAST + 1
            for n in range(fill):
                if n == before:
                    prepare_local()
                iteration(STEP * n)
            if B > fill:
                with eng.Fori(STEP * fill, STEP * B, STEP) as i:
                    iteration(i)
            for n in range(max(B, fill), B + LAST):
                iteration(STEP * n)

        def at(i, skew):
            if isinstance(i, int):
                v = i - STEP * skew
                return v if 0 <= v < STEP * B else None
            return i - STEP * skew if skew else i

        def sample_rows(a, v):
            if isinstance(v, int):
                return a[v * (T // STEP):v * (T // STEP) + T, :]
            return a.rearrange("(b t) d -> b t d", t=T)[bass.ds(v // STEP, 1), :, :].rearrange("b t d -> (b t) d")

        SETUP = [
            (con[:, :], consts), (wz[:, :], w_heads), (wq_s[:, :], wqT), (wk_s[:, :], wkT),
            (wv_s[:, :], wvT), (wo_s[:, :], woT),
            (bq_c[:, :], bq.rearrange("(p a) -> p a", a=1)), (bk_c[:, :], bk.rearrange("(p a) -> p a", a=1)),
            (bv_r[:, :], bv.partition_broadcast(128)), (bo_r[:, :], bo.partition_broadcast(128)),
        ]
        SETUP_LOCAL = []
        for l in range(2):
            SETUP_LOCAL += [
                (wqkv_s[l][:, :], wqkv[l]), (wo3_s[l][:, :, :], wo[l].rearrange("(c p) n -> p c n", p=128)),
                (w1_r[l][:, :], w1[l]), (b2_r[l][:, :], b2[l].partition_broadcast(128)),
                (lg_c[l][:, :], ln_g[l].rearrange("(p a) -> p a", a=1)),
                (lb_c[l][:, :], ln_b[l].rearrange("(p a) -> p a", a=1)),
                (w2_s[l][0:FC[0], 0:2, :], w2[l][0:2 * FC[0], :].rearrange("(c p) n -> p c n", p=FC[0])),
                (w2_s[l][0:FC[2], 2, :], w2[l][2 * FC[0]:HID, :]),
            ]
            for half in range(2):
                for c in range(3):
                    lo = half * HID + FO[c]
                    SETUP_LOCAL.append((b1_r[l][0:FC[c], 3 * half + c:3 * half + c + 1],
                                        b1[l][lo:lo + FC[c]].rearrange("(p a) -> p a", a=1)))
            for k, s in enumerate((k_scale, q_scale)):
                SETUP_LOCAL.append((scale_r[l][:, k, :], s[l].partition_broadcast(128)))
                for a in range(2):
                    SETUP_LOCAL.append((scale_x[l][:, k, 32 * a:32 * a + 32],
                                        s[l][32 * (1 - a):32 * (1 - a) + 32].partition_broadcast(128)))
        LOADED = 16 * len(SETUP)
        LOCAL_LOADED = 16 * len(SETUP_LOCAL)
        PREP_V_FIXED = 11
        PREP_V_LOCAL = 17
        PREP_V_BIAS = 25
        N_PREP_P = 6

        def stages(eng, order, prepare_local, self_stage, cross_stage, local_stage):
            def iteration(i):
                parts = {}
                if at(i, 1) is not None:
                    parts["S"] = self_stage(at(i, 1))
                if at(i, 2) is not None:
                    parts["C"] = cross_stage(at(i, 2))
                for l in range(2):
                    if at(i, 3 + l) is not None:
                        parts["LM"[l]] = local_stage(l, at(i, 3 + l))
                weave(order, parts)
            loop(eng, iteration, prepare_local, 3)

        @block.sync
        def _(sp):
            for tile, source in SETUP:
                sp.dma_start(tile, source).then_inc(loaded, 16)

            def prepare_local():
                for tile, source in SETUP_LOCAL:
                    sp.dma_start(tile, source).then_inc(local_loaded, 16)

            def iteration(i):
                v = at(i, 0)
                if v is not None:
                    if again(v):
                        sp.wait_ge(SELF.x_copied, v)
                    sp.dma_start(SELF.xin[:, :], sample_rows(x_rows, v)).then_inc(SELF.x_loaded, 16)
                v = at(i, 1)
                if v is not None:
                    if again(v):
                        sp.wait_ge(CROSS.cT_psum, v)
                    sp.dma_start(CROSS.cin[:, :], sample_rows(ctx_rows, v)).then_inc(CROSS.c_loaded, 16)
                v = at(i, 4)
                if v is not None:
                    sp.wait_ge(LOC[1].normed, v + STEP)
                    sp.dma_start(sample_rows(out_rows, v), LOC[1].out[:, 0, :]).then_inc(stored, 16)

            loop(nc.sync, iteration, prepare_local, 1)
            sp.wait_ge(stored, STEP * B)

        @block.tensor
        def _(pe):
            pe.wait_ge(loaded, LOADED)
            pe.wait_ge(prep_v, PREP_V_FIXED)
            pe.wait_ge(prep_p, N_PREP_P)

            def prepare_local():
                pe.wait_ge(local_loaded, LOCAL_LOADED)
                for l in range(2):
                    for half in range(2):
                        for c in range(3):
                            lo = half * HID + FO[c]
                            last = nc.tensor.matmul(LOC[l].b0[0:FC[c], 3 * half + c:3 * half + c + 1],
                                                    w1_r[l][:, lo:lo + FC[c]], lb_c[l][:, :], start=True, stop=True)
                last.then_inc(prep_mm, 1)
                pe.wait_ge(prep_v, PREP_V_BIAS)

            def max_to_rows(s, v):
                pe.wait_ge(s.neg_split, v + STEP)
                nc.tensor.transpose(s.b1.bitcast(BF16)[:, 0:128], s.neg[:, :], ident_b[:, :]).then_inc(s.rows_psum, STEP)

            def core16(s, v):
                pe.wait_ge(s.k_low, v + STEP)
                for g in range(G):
                    bank = s.b0 if g % 2 else s.b1
                    if g % 2 == 0:
                        pe.wait_ge(s.q_low, v + 8 * (g // 2) + 8)
                    if g >= 2:
                        pe.wait_ge(s.max_done, v + 4 * (g - 1))
                    for j in range(GH):
                        last = nc.tensor.matmul(bank[:, 128 * j:128 * j + 128], s.qb[:, GH * g + j, :],
                                                s.kb[:, :], start=(j == 0), stop=not s.windowed, skip_group_check=True)
                    if s.windowed:
                        last = nc.tensor.matmul(bank, ident_b[:, :], mask_w[:, :, :], start=False, stop=True,
                                                skip_group_check=True)
                    last.then_inc(s.scores_n_psum, 4)
                    yield
                pe.wait_ge(s.max_done, v + STEP)
                nc.tensor.matmul(s.b0, s.k[:, :], s.q[:, 0:GH, :], start=True, stop=False)
                yield
                max_to_rows(s, v)
                yield
                for g in range(G):
                    bank = s.b1 if g % 2 else s.b0
                    if g == 0:
                        pe.wait_ge(s.rows_ready, v + STEP)
                    else:
                        if g >= 2:
                            pe.wait_ge(s.exp_done, v + 4 * (g - 1))
                        nc.tensor.matmul(bank, s.k[:, :], s.q[:, GH * g:GH * g + GH, :], start=True, stop=False)
                    if s.windowed:
                        nc.tensor.matmul(bank, ident_b[:, :], mask_w[:, :, :], start=False, stop=False)
                    nc.tensor.matmul(bank, group_b[:, g, :], s.rows[:, :, :], start=False, stop=True)\
                        .then_inc(s.scores_t_psum, 4)
                    yield

            def self_stage(v):
                s = SELF
                pe.wait_ge(s.x_copied, v + STEP)
                if again(v):
                    pe.wait_ge(s.y_ready, v - SET_UP[-1])
                nc.tensor.transpose(s.b0[:, 0:128], s.x[:, :], ident).then_inc(s.xT_psum, STEP)
                yield
                for g in range(G):
                    bank = s.b0 if g % 2 else s.b1
                    if g == 0:
                        pe.wait_ge(s.xT_ready, v + STEP)
                        if again(v):
                            pe.wait_ge(s.y_ready, v)
                    if g >= 2:
                        pe.wait_ge(s.z_ready, v + 4 * (g - 1))
                    nc.tensor.matmul(bank, s.xT[:, :], wz[:, 512 * g:512 * g + 512], start=True, stop=True)\
                        .then_inc(s.z_psum, 4)
                    yield
                pe.wait_ge(s.z_ready, v + STEP)
                yield from core16(s, v)
                for n, (h0, hn) in enumerate(SETS):
                    bank = s.b1 if n % 2 else s.b0
                    pe.wait_ge(s.exp_done, v + 4 * max((h0 + hn - 1) // GH + 1, 3 + n if n < 2 else 0))
                    if n >= 2:
                        pe.wait_ge(s.y_ready, v + 2 * (n - 1))
                    for j in range(hn):
                        last = nc.tensor.matmul(bank[:, 129 * j:129 * j + 129], s.e[:, h0 + j, :],
                                                s.z[:, h0 + j, :], start=True, stop=True)
                    last.then_inc(s.av_psum, SET_UP[n])
                    yield

            def cross_stage(v):
                s = CROSS
                pe.wait_ge(s.c_loaded, v + STEP)
                if again(v):
                    pe.wait_ge(s.o_ready, v)
                nc.tensor.transpose(s.b0[:, 0:128], s.cin[:, :], ident).then_inc(s.cT_psum, STEP)
                yield
                pe.wait_ge(s.cT_ready, v + STEP)
                if again(v):
                    pe.wait_ge(s.resid, v)
                nc.tensor.matmul(s.b1[:, 0:128], wk_s[:, :], s.cT[:, :], start=True, stop=True).then_inc(s.kT_psum, STEP)
                nc.tensor.matmul(s.b0[:, 0:128], s.cT[:, :], wv_s[:, :], start=True, stop=True).then_inc(s.v_psum, STEP)
                yield
                pe.wait_ge(s.x_copied, v + STEP)
                pe.wait_ge(s.kT_ready, v + STEP)
                nc.tensor.transpose(s.b1[:, 0:128], s.x[:, :], ident).then_inc(s.xT_psum, STEP)
                yield
                pe.wait_ge(s.xT_ready, v + STEP)
                pe.wait_ge(s.v_ready, v + STEP)
                nc.tensor.matmul(s.b0[:, 0:128], wq_s[:, :], s.xT[:, :], start=True, stop=True).then_inc(s.q_psum, STEP)
                yield
                pe.wait_ge(s.q_wide, v + STEP)
                yield from core16(s, v)
                pe.wait_ge(s.exp_done, v + STEP)
                for j in range(GH):
                    for g in range(G):
                        last = nc.tensor.matmul(s.b1[32 * g:32 * g + 32, 0:128], own[:, j, 32 * g:32 * g + 32],
                                                s.e[:, GH * g + j, :], start=(j == 0), stop=(j == GH - 1))
                last.then_inc(s.av_psum, 8)
                yield
                pe.wait_ge(s.v_own, v + STEP)
                for j in range(GH):
                    for g in range(G):
                        last = nc.tensor.matmul(s.b0[32 * g:32 * g + 32, 0:128], s.vm[:, j, 32 * g:32 * g + 32],
                                                s.e[:, GH * g + j, :], start=(j == 0), stop=(j == GH - 1))
                last.then_inc(s.av_psum, 8)
                yield
                pe.wait_ge(s.o_ready, v + STEP)
                last = nc.tensor.matmul(s.b1[:, 0:128], s.o[:, :], wo_s[:, :], start=True, stop=True)
                last.then_inc(s.proj_psum, STEP)
                yield

            def masked_scores(s, g, bank):
                for p in range(2):
                    nc.tensor.matmul(bank[:, 256 * p:256 * p + 256], s.k[:, 2 * g + p, :], s.q[:, 2 * g + p, :, :],
                                     start=(p == 0), stop=False, skip_group_check=True)
                nc.tensor.matmul(bank, ident_b[:, :], mask_t[:, :, :], start=False, stop=False, skip_group_check=True)

            def local_stage(l, v):
                s = LOC[l]
                pe.wait_ge(s.x_copied, v + STEP)
                if again(v):
                    pe.wait_ge(s.hid_done, v)
                nc.tensor.transpose(s.b1[:, 0:128], s.x[:, 0, :], ident).then_inc(s.xT_psum, STEP)
                yield
                pe.wait_ge(s.xT_ready, v + STEP)
                nc.tensor.matmul(s.b1, s.xT[:, :], wqkv_s[l][:, 0:INNER], start=True, stop=True)\
                    .then_inc(s.qkv_psum, 8)
                yield
                if again(v):
                    pe.wait_ge(s.resid, v)
                nc.tensor.matmul(s.b0, s.xT[:, :], wqkv_s[l][:, INNER:2 * INNER], start=True, stop=True)\
                    .then_inc(s.qkv_psum, 8)
                yield
                pe.wait_ge(s.qk_norm, v + 8)
                nc.tensor.matmul(s.b1, s.xT[:, :], wqkv_s[l][:, 2 * INNER:3 * INNER], start=True, stop=True)\
                    .then_inc(s.v_psum, STEP)
                yield
                pe.wait_ge(s.roped, v + 8)
                pe.wait_ge(s.v_ready, v + STEP)
                for p in range(LH // 2):
                    last = nc.tensor.transpose(s.b1[:, 128 * p:128 * p + 128],
                                               s.qr[:, INNER + 128 * p:INNER + 128 * p + 128], ident)
                last.then_inc(s.qkT_psum, 8)
                yield
                pe.wait_ge(s.roped, v + STEP)
                for p in range(LH // 2):
                    last = nc.tensor.transpose(s.b0[:, 128 * p:128 * p + 128], s.qr[:, 128 * p:128 * p + 128], ident)
                last.then_inc(s.qkT_psum, 8)
                yield
                pe.wait_ge(s.q_low, v + STEP)
                pe.wait_ge(s.k_low, v + STEP)
                for g in range(2):
                    bank = s.b0 if g else s.b1
                    for j in range(GH):
                        nc.tensor.matmul(bank[:, 128 * j:128 * j + 128], s.qb[:, 2 * g + j // 2, j % 2, :],
                                         s.kb[:, 2 * g + j // 2, :], start=(j == 0), stop=False,
                                         skip_group_check=True)
                    nc.tensor.matmul(bank, ident_b[:, :], mask_n[:, :, :], start=False, stop=True,
                                     skip_group_check=True).then_inc(s.scores_n_psum, 8)
                    yield
                pe.wait_ge(s.max_done, v + STEP)
                masked_scores(s, 0, s.b0)
                yield
                max_to_rows(s, v)
                yield
                pe.wait_ge(s.rows_ready, v + STEP)
                nc.tensor.matmul(s.b0, group_b[:, 0, :], s.rows[:, :, :], start=False, stop=True,
                                 skip_group_check=True).then_inc(s.scores_t_psum, 8)
                yield
                masked_scores(s, 1, s.b1)
                nc.tensor.matmul(s.b1, group_b[:, 1, :], s.rows[:, :, :], start=False, stop=True,
                                 skip_group_check=True).then_inc(s.scores_t_psum, 8)
                yield
                for g in range(2):
                    bank = s.b1 if g else s.b0
                    pe.wait_ge(s.exp_done, v + 8 * g + 8)
                    for j in range(GH):
                        last = nc.tensor.matmul(bank[:, (LD + 1) * j:(LD + 1) * j + LD + 1], s.e[:, GH * g + j, :],
                                                s.v[:, GH * g + j, :], start=True, stop=True)
                    last.then_inc(s.av_psum, 8)
                    yield
                for p in range(LH // 2):
                    if p % 2 == 0:
                        pe.wait_ge(s.o_ready, v + 4 * p + 8)
                    last = nc.tensor.transpose(s.b0[:, 128 * p:128 * p + 128], s.o[:, 128 * p:128 * p + 128], ident)
                last.then_inc(s.oT_psum, STEP)
                yield
                pe.wait_ge(s.oT_ready, v + STEP)
                for p in range(LH // 2):
                    last = nc.tensor.matmul(s.b1[:, 0:128], s.oT[:, p, :], wo3_s[l][:, p, :],
                                            start=(p == 0), stop=(p == LH // 2 - 1))
                last.then_inc(s.proj_psum, STEP)
                yield
                pe.wait_ge(s.mid_done, v + STEP)
                nc.tensor.matmul(s.b0[:, 0:64], shift_m, s.mid[:, 64:128], start=True, stop=True)\
                    .then_inc(s.shifted_psum, STEP)
                yield
                pe.wait_ge(s.hnorm, v + STEP)
                nc.tensor.transpose(s.b1[:, 0:128], s.hn[:, :], ident).then_inc(s.hT_psum, STEP)
                yield
                pe.wait_ge(s.hT_ready, v + STEP)
                for c in range(3):
                    lo = HID + FO[c]
                    last = nc.tensor.matmul(s.b0[0:FC[c], 128 * c:128 * c + 128], w1_s[l][:, lo:lo + FC[c]],
                                            s.hT[:, :], start=True, stop=True)
                last.then_inc(s.mlp_in_psum, 8)
                yield
                for c in range(3):
                    last = nc.tensor.matmul(s.b1[0:FC[c], 128 * c:128 * c + 128], w1_s[l][:, FO[c]:FO[c] + FC[c]],
                                            s.hT[:, :], start=True, stop=True)
                last.then_inc(s.mlp_in_psum, 8)
                yield
                pe.wait_ge(s.hid_done, v + STEP)
                for c in range(3):
                    last = nc.tensor.matmul(s.b0[:, 0:128], s.hid[0:FC[c], c, :], w2_s[l][0:FC[c], c, :],
                                            start=(c == 0), stop=(c == 2))
                last.then_inc(s.mlp_psum, STEP)
                yield

            stages(nc.tensor, ORDER_TENSOR, prepare_local, self_stage, cross_stage, local_stage)


        @block.scalar
        def _(act):
            act.wait_ge(loaded, LOADED)
            act.wait_ge(prep_v, PREP_V_FIXED)

            def prepare_local():
                act.wait_ge(prep_v, PREP_V_BIAS)

            def exps(s, v, g, n):
                bank = s.b1 if g % 2 else s.b0
                act.wait_ge(s.scores_t_psum, v + STEP // n * (g + 1))
                nc.scalar.activation(s.e[:, GH * g:GH * g + GH, :], bank.rearrange("p (j t) -> p j t", j=GH), ACT.Exp)\
                    .then_inc(s.exp_done, STEP // n)

            def self_stage(v):
                s = SELF
                act.wait_ge(s.xT_psum, v + STEP)
                nc.scalar.activation(s.xT[:, :], s.b0[:, 0:128], ACT.Copy).then_inc(s.xT_ready, STEP)
                yield
                for g in range(G):
                    bank = s.b0 if g % 2 else s.b1
                    act.wait_ge(s.z_psum, v + 4 * g + 4)
                    nc.scalar.activation(s.z[:, GH * g:GH * g + GH, 0:128], bank.rearrange("p (j n) -> p j n", j=GH), ACT.Copy)\
                        .then_inc(s.z_ready, 4)
                    yield
                for g in range(G):
                    exps(s, v, g, G)
                    yield

            def cross_stage(v):
                s = CROSS
                act.wait_ge(s.cT_psum, v + STEP)
                nc.scalar.activation(s.cT[:, :], s.b0[:, 0:128], ACT.Copy).then_inc(s.cT_ready, STEP)
                yield
                act.wait_ge(s.kT_psum, v + STEP)
                nc.scalar.activation(s.k[:, :], s.b1[:, 0:128], ACT.Identity, bias=bk_c[:, :]).then_inc(s.kT_ready, STEP)
                yield
                act.wait_ge(s.xT_psum, v + STEP)
                nc.scalar.activation(s.xT[:, :], s.b1[:, 0:128], ACT.Copy).then_inc(s.xT_ready, STEP)
                yield
                for g in range(G):
                    exps(s, v, g, G)
                    yield

            def local_stage(l, v):
                s = LOC[l]
                act.wait_ge(s.xT_psum, v + STEP)
                nc.scalar.activation(s.xT[0:64, :], s.b1[0:64, 0:128], ACT.Copy).then_inc(s.xT_ready, 8)
                nc.scalar.activation(s.xT[64:128, 1:128], s.b1[64:128, 0:127], ACT.Copy).then_inc(s.xT_ready, 8)
                yield
                for a in (1, 0):
                    act.wait_ge(s.qkv_psum, v + STEP - 8 * a)
                    nc.scalar.activation(s.sq[:, LH * a:LH * a + LH, :],
                                         s.ps[:, INNER * a:INNER * a + INNER].rearrange("p (h d) -> p h d", d=LD), ACT.Square)\
                        .then_inc(s.squares, 8)
                    yield
                yield
                act.wait_ge(s.v_psum, v + STEP)
                nc.scalar.activation(s.v[:, :, 0:LD], s.b1.rearrange("p (h d) -> p h d", h=LH), ACT.Copy).then_inc(s.v_ready, STEP)
                yield
                act.wait_ge(s.qkT_psum, v + 8)
                for a in range(2):
                    nc.scalar.activation(s.q[64 * a:64 * a + 64, :, a, :],
                                         s.b1[64 * a:64 * a + 64, :].rearrange("p (c t) -> p c t", c=LH // 2), ACT.Copy)\
                        .then_inc(s.q_split, 8)
                    yield
                act.wait_ge(s.qkT_psum, v + STEP)
                nc.scalar.activation(s.k[:, :, :], s.b0.rearrange("p (c t) -> p c t", c=LH // 2), ACT.Copy)\
                    .then_inc(s.kT_ready, STEP)
                yield
                exps(s, v, 0, 2)
                yield
                exps(s, v, 1, 2)
                yield
                act.wait_ge(s.oT_psum, v + STEP)
                nc.scalar.activation(s.oT[:, :, :], s.b0.rearrange("p (c t) -> p c t", c=LH // 2), ACT.Copy)\
                    .then_inc(s.oT_ready, STEP)
                yield
                act.wait_ge(s.hT_psum, v + STEP)
                nc.scalar.activation(s.hT[:, :], s.b1[:, 0:128], ACT.Copy).then_inc(s.hT_ready, STEP)
                yield
                act.wait_ge(s.mlp_in_psum, v + 8)
                for c in range(3):
                    last = nc.scalar.activation(s.gate[0:FC[c], c, :], s.b0[0:FC[c], 128 * c:128 * c + 128], ACT.Gelu,
                                                bias=b1_s[l][0:FC[c], 3 + c:4 + c])
                last.then_inc(s.gelu_done, STEP)
                yield

            stages(nc.scalar, ORDER_SCALAR, prepare_local, self_stage, cross_stage, local_stage)

        @block.vector
        def _(dve):
            for s in LOC:
                nc.vector.memset(s.v[:, :, LD:LD + 1], 1.0).then_inc(prep_v, 1)
            nc.vector.memset(SELF.z[:, :, 128:129], 1.0).then_inc(prep_v, 1)
            for s in (SELF, CROSS, LOC[0], LOC[1]):
                nc.vector.memset(s.neg[:, :], 0.0).then_inc(prep_v, 1)
            for s in LOC:
                nc.vector.memset(s.q[:, :, :, :], 0.0).then_inc(prep_v, 1)
                nc.vector.memset(s.xT[64:128, 0:1], 0.0).then_inc(prep_v, 1)
            dve.wait_ge(loaded, LOADED)
            dve.wait_ge(prep_p, N_PREP_P)

            def prepare_local():
                dve.wait_ge(local_loaded, LOCAL_LOADED)
                for l in range(2):
                    nc.vector.tensor_scalar(w1_s[l][:, :], w1_r[l][:, :], lg_c[l][:, :], None, ALU.mult).then_inc(prep_v, 1)
                for l in range(2):
                    nc.vector.tensor_tensor(cos_t[l][:, :, :], scale_r[l][:, :, :],
                                            con[:, C_COS:C_COS + 2 * LD].rearrange("p (a d) -> p a d", a=2), ALU.mult)\
                        .then_inc(prep_v, 1)
                    nc.vector.tensor_tensor(sin_t[l][:, :, :], scale_x[l][:, :, :],
                                            con[:, C_SIN:C_SIN + 2 * LD].rearrange("p (a d) -> p a d", a=2), ALU.mult)\
                        .then_inc(prep_v, 1)
                dve.wait_ge(prep_mm, 1)
                for l in range(2):
                    for c0, c1, f in ((0, 2, FC[0]), (2, 3, FC[2]), (3, 5, FC[0]), (5, 6, FC[2])):
                        nc.vector.tensor_tensor(b1_s[l][0:f, c0:c1], LOC[l].b0[0:f, c0:c1], b1_r[l][0:f, c0:c1], ALU.add)\
                            .then_inc(prep_v, 1)

            def row_max(s, v, g, bank, n):
                dve.wait_ge(s.scores_n_psum, v + STEP // n * (g + 1))
                nc.vector.tensor_reduce(s.m[:, GH * g:GH * g + GH], bank.rearrange("p (j t) -> p j t", j=GH), AX.X, ALU.max)\
                    .then_inc(s.max_done, STEP // n)

            def split_max(s, v):
                h = s.heads
                dve.wait_ge(s.max_done, v + STEP)
                nc.vector.tensor_scalar(s.neg[:, 0:h], s.m[:, :], -1.0, None, ALU.mult).then_inc(s.neg_split, 8)
                yield
                dve.wait_ge(s.neg_split, v + 8)
                nc.vector.scalar_tensor_tensor(out=s.neg[:, 16:16 + h], in0=s.m[:, :], scalar=-1.0, in1=s.neg[:, 0:h],
                                               op0=ALU.mult, op1=ALU.subtract).then_inc(s.neg_split, 8)

            def spread_rows(s, v):
                dve.wait_ge(s.rows_psum, v + STEP)
                nc.vector.tensor_tensor(s.rows[:, :, :],
                                        s.b1.bitcast(BF16)[:, 0:128].unsqueeze(1).to_broadcast([128, GH, 128]),
                                        row_mask.unsqueeze(2).to_broadcast([128, GH, 128]), ALU.mult)\
                    .then_inc(s.rows_ready, STEP)

            def moments(s, v):
                dve.wait_ge(s.resid, v + STEP)
                nc.vector.bn_stats(s.st[:, 0, :], s.r[:, :]).then_inc(s.moments, 8)
                yield
                dve.wait_ge(s.moments, v + 8)
                nc.vector.bn_aggr(s.mv[:, :], s.st[:, 0, :]).then_inc(s.moments, 8)

            def normalise(s, v, out):
                dve.wait_ge(s.rstd, v + STEP)
                nc.vector.tensor_scalar(out, s.r[:, :], s.mv[:, 0:1], s.rs[:, :], ALU.subtract, ALU.mult)\
                    .then_inc(s.normed, STEP)

            def self_stage(v):
                s = SELF
                dve.wait_ge(s.xT_ready, v + STEP)
                for a in range(2):
                    nc.vector.tensor_tensor(s.q[:, 8 * a:8 * a + 8, :], s.xT[:, :].unsqueeze(1).to_broadcast([128, 8, 128]),
                                            head_mask[:, 8 * a:8 * a + 8].unsqueeze(2).to_broadcast([128, 8, 128]), ALU.mult)\
                        .then_inc(s.q_wide, 8)
                    yield
                for g in range(G):
                    row_max(s, v, g, s.b0 if g % 2 else s.b1, G)
                    yield
                yield from split_max(s, v)
                yield
                spread_rows(s, v)
                yield
                done = 0
                for n, (h0, hn) in enumerate(SETS):
                    done += SET_UP[n]
                    bank = (s.b1 if n % 2 else s.b0)[:, 0:129 * hn].rearrange("p (j n) -> p j n", n=129)
                    dve.wait_ge(s.av_psum, v + done)
                    nc.vector.reciprocal(s.rd[:, h0:h0 + hn].unsqueeze(2), bank[:, :, 128:129]).then_inc(s.rden, SET_UP[n])
                    yield
                    dve.wait_ge(s.rden, v + done)
                    nc.vector.tensor_tensor(s.y[:, h0:h0 + hn, :], bank[:, :, 0:128],
                                            s.rd[:, h0:h0 + hn].unsqueeze(2).to_broadcast([128, hn, 128]), ALU.mult)\
                        .then_inc(s.y_ready, SET_UP[n])
                    yield
                dve.wait_ge(s.tree, v + STEP)
                nc.vector.tensor_tensor(s.r[:, :], s.y[:, 0, :], s.y[:, 1, :], ALU.add).then_inc(s.resid, 8)
                yield
                dve.wait_ge(s.resid, v + 8)
                nc.vector.tensor_tensor(s.r[:, :], s.r[:, :], s.x[:, :], ALU.add).then_inc(s.resid, 8)
                yield from moments(s, v)
                yield
                if again(v):
                    dve.wait_ge(CROSS.x_bias, v)
                normalise(s, v, s.out[:, :])
                yield

            def cross_stage(v):
                s = CROSS
                dve.wait_ge(s.v_psum, v + STEP)
                nc.vector.tensor_tensor(s.v[:, :], s.b0[:, 0:128], bv_r[:, :], ALU.add).then_inc(s.v_ready, STEP)
                yield
                dve.wait_ge(s.q_psum, v + STEP)
                for a in range(2):
                    nc.vector.scalar_tensor_tensor(
                        out=s.q[:, 8 * a:8 * a + 8, :], in0=s.b0[:, 0:128].unsqueeze(1).to_broadcast([128, 8, 128]),
                        scalar=bq_c[:, :], in1=head_mask[:, 8 * a:8 * a + 8].unsqueeze(2).to_broadcast([128, 8, 128]),
                        op0=ALU.add, op1=ALU.mult).then_inc(s.q_wide, 8)
                    yield
                for g in range(G):
                    row_max(s, v, g, s.b0 if g % 2 else s.b1, G)
                    yield
                yield from split_max(s, v)
                yield
                spread_rows(s, v)
                yield
                dve.wait_ge(s.av_psum, v + 8)
                nc.vector.reciprocal(s.o[:, :], s.b1[:, 0:128]).then_inc(s.inverse, STEP)
                yield
                dve.wait_ge(s.inverse, v + STEP)
                dve.wait_ge(s.av_psum, v + STEP)
                nc.vector.tensor_tensor(s.o[:, :], s.b0[:, 0:128], s.o[:, :], ALU.mult).then_inc(s.o_ready, STEP)
                yield
                dve.wait_ge(s.proj_psum, v + STEP)
                dve.wait_ge(s.x_bias, v + STEP)
                nc.vector.tensor_tensor(s.r[:, :], s.b1[:, 0:128], s.xb[:, :], ALU.add).then_inc(s.resid, STEP)
                yield from moments(s, v)
                yield
                if again(v):
                    dve.wait_ge(LOC[0].x_copied, v)
                normalise(s, v, s.out[:, :])
                yield

            def local_stage(l, v):
                s = LOC[l]
                for a in (1, 0):
                    dve.wait_ge(s.squares, v + STEP - 8 * a)
                    nc.vector.tensor_reduce(s.ss[:, LH * a:LH * a + LH], s.sq[:, LH * a:LH * a + LH, :], AX.X, ALU.add)\
                        .then_inc(s.square_sum, 8)
                    yield
                for a in (1, 0):
                    dve.wait_ge(s.rnorm, v + STEP - 8 * a)
                    nc.vector.tensor_tensor(s.qk[:, a, :, :],
                                            s.ps[:, INNER * a:INNER * a + INNER].rearrange("p (h d) -> p h d", d=LD),
                                            s.rn[:, LH * a:LH * a + LH].unsqueeze(2).to_broadcast([128, LH, LD]), ALU.mult)\
                        .then_inc(s.qk_norm, 8)
                    yield
                for a in (1, 0):
                    dve.wait_ge(s.qk_norm, v + STEP - 8 * a)
                    nc.vector.tensor_tensor(s.qc[:, a, :, :], s.qk[:, a, :, :],
                                            cos_t[l][:, a, :].unsqueeze(1).to_broadcast([128, LH, LD]), ALU.mult)\
                        .then_inc(s.rot_cos, 8)
                    yield
                    dve.wait_ge(s.rot_cos, v + STEP - 8 * a)
                    dve.wait_ge(s.rot_sin, v + STEP - 8 * a)
                    nc.vector.tensor_tensor(s.qc[:, a, :, :], s.qc[:, a, :, :], s.qs[:, a, :, :], ALU.add).then_inc(s.roped, 8)
                    yield
                for g in range(2):
                    row_max(s, v, g, s.b0 if g else s.b1, 2)
                    yield
                yield from split_max(s, v)
                yield
                spread_rows(s, v)
                yield
                for g in range(2):
                    bank = (s.b1 if g else s.b0)[:, 0:GH * (LD + 1)].rearrange("p (j d) -> p j d", j=GH)
                    dve.wait_ge(s.av_psum, v + 8 * g + 8)
                    nc.vector.reciprocal(s.rd[:, GH * g:GH * g + GH].unsqueeze(2), bank[:, :, LD:LD + 1]).then_inc(s.inverse, 8)
                    yield
                    dve.wait_ge(s.inverse, v + 8 * g + 8)
                    nc.vector.tensor_tensor(s.o[:, 256 * g:256 * g + 256].rearrange("p (j d) -> p j d", j=GH), bank[:, :, 0:LD],
                                            s.rd[:, GH * g:GH * g + GH].unsqueeze(2).to_broadcast([128, GH, LD]), ALU.mult)\
                        .then_inc(s.o_ready, 8)
                    yield
                dve.wait_ge(s.proj_psum, v + STEP)
                nc.vector.tensor_tensor(s.mid[:, :], s.b1[:, 0:128], s.x[:, 0, :], ALU.add).then_inc(s.mid_done, STEP)
                yield
                dve.wait_ge(s.mid_done, v + STEP)
                nc.vector.bn_stats(s.st[:, 0, :], s.mid[:, 0:64]).then_inc(s.mid_moments, 4)
                yield
                dve.wait_ge(s.shifted_psum, v + STEP)
                nc.vector.bn_stats(s.st[:, 1, :], s.b0[:, 0:64]).then_inc(s.mid_moments, 4)
                yield
                dve.wait_ge(s.mid_moments, v + 8)
                nc.vector.bn_aggr(s.mv2[:, :], s.st[:, :, :].rearrange("p a b -> p (a b)")).then_inc(s.mid_moments, 8)
                yield
                dve.wait_ge(s.mid_rstd, v + STEP)
                nc.vector.tensor_scalar(s.hn[:, 0:64], s.mid[:, 0:64], s.mv2[:, 0:1], s.rs2[:, :],
                                        ALU.subtract, ALU.mult).then_inc(s.hnorm, 8)
                nc.vector.tensor_scalar(s.hn[:, 64:128], s.b0[:, 0:64], s.mv2[:, 0:1], s.rs2[:, :],
                                        ALU.subtract, ALU.mult).then_inc(s.hnorm, 8)
                yield
                dve.wait_ge(s.mlp_in_psum, v + STEP)
                dve.wait_ge(s.gelu_done, v + STEP)
                for c in range(3):
                    last = nc.vector.scalar_tensor_tensor(
                        out=s.hid[0:FC[c], c, :], in0=s.b1[0:FC[c], 128 * c:128 * c + 128], scalar=b1_s[l][0:FC[c], c:c + 1],
                        in1=s.gate[0:FC[c], c, :], op0=ALU.add, op1=ALU.mult)
                last.then_inc(s.hid_done, STEP)
                yield
                dve.wait_ge(s.mlp_psum, v + STEP)
                dve.wait_ge(s.mid_bias, v + STEP)
                if l == 0:
                    if again(v):
                        dve.wait_ge(LOC[1].x_copied, v)
                    nc.vector.tensor_tensor(s.out[:, 0, :], s.b0[:, 0:128], s.midb[:, :], ALU.add).then_inc(s.resid, STEP)
                    yield
                else:
                    nc.vector.tensor_tensor(s.r[:, :], s.b0[:, 0:128], s.midb[:, :], ALU.add).then_inc(s.resid, STEP)
                    yield from moments(s, v)
                    yield
                    if again(v):
                        dve.wait_ge(stored, v)
                    normalise(s, v, s.out[:, 0, :])
                yield

            stages(nc.vector, ORDER_VECTOR, prepare_local, self_stage, cross_stage, local_stage)

        @block.gpsimd
        def _(pool):
            nc.gpsimd.memset(half_neg[:, :], -0.5).then_inc(prep_p, 1)
            pool.wait_ge(loaded, LOADED)

            def copy(out, in_):
                return nc.gpsimd.tensor_scalar(out, in_, 1.0, 0.0, ALU.mult, ALU.add)

            copy(ident_b[:, :], ident).then_inc(prep_p, 1)
            copy(group_b[:, :, :], con[:, C_GRP:C_GRP + 512].rearrange("p (g t) -> p g t", g=4)).then_inc(prep_p, 1)
            for tile, at_ in ((mask_n, C_MASKN), (mask_t, C_MASKT), (mask_w, C_BAND)):
                copy(tile[:, :, :], con[:, at_:at_ + 128].unsqueeze(1).to_broadcast([128, GH, 128])).then_inc(prep_p, 1)
            pool.wait_ge(prep_v, PREP_V_FIXED)

            def prepare_local():
                pool.wait_ge(local_loaded, LOCAL_LOADED)
                pool.wait_ge(prep_v, PREP_V_LOCAL)

            def inverse_root(s, v, moments_done, mv, out, done):
                pool.wait_ge(moments_done, v + STEP)
                nc.gpsimd.tensor_scalar(s.ve[:, :], mv[:, 1:2], EPS, 1.0, ALU.add, ALU.mult).then_inc(done, 8)
                yield
                pool.wait_ge(done, v + 8)
                nc.gpsimd.tensor_tensor(out, s.ve[:, :], half_neg[:, 0:1], ALU.pow).then_inc(done, 8)

            def low_queries(s, v):
                for a in range(2):
                    pool.wait_ge(s.q_wide, v + 8 * a + 8)
                    copy(s.qb[:, 8 * a:8 * a + 8, :], s.q[:, 8 * a:8 * a + 8, :]).then_inc(s.q_low, 8)
                    yield

            def self_stage(v):
                s = SELF
                pool.wait_ge(s.x_loaded, v + STEP)
                if again(v):
                    pool.wait_ge(s.resid, v)
                copy(s.x[:, :], s.xin[:, :]).then_inc(s.x_copied, STEP)
                yield
                pool.wait_ge(s.xT_ready, v + STEP)
                copy(s.kb[:, :], s.xT[:, :]).then_inc(s.k_low, STEP)
                yield from low_queries(s, v)
                pool.wait_ge(s.y_ready, v + 6)
                nc.gpsimd.tensor_tensor(s.y[:, 0:4, :], s.y[:, 0:4, :], s.y[:, 4:8, :], ALU.add).then_inc(s.tree, 4)
                yield
                pool.wait_ge(s.y_ready, v + STEP)
                nc.gpsimd.tensor_tensor(s.y[:, 8:12, :], s.y[:, 8:12, :], s.y[:, 12:16, :], ALU.add).then_inc(s.tree, 4)
                yield
                pool.wait_ge(s.tree, v + 8)
                nc.gpsimd.tensor_tensor(s.y[:, 0:4, :], s.y[:, 0:4, :], s.y[:, 8:12, :], ALU.add).then_inc(s.tree, 4)
                yield
                pool.wait_ge(s.tree, v + 12)
                nc.gpsimd.tensor_tensor(s.y[:, 0:2, :], s.y[:, 0:2, :], s.y[:, 2:4, :], ALU.add).then_inc(s.tree, 4)
                yield
                yield from inverse_root(s, v, s.moments, s.mv, s.rs[:, :], s.rstd)
                yield

            def cross_stage(v):
                s = CROSS
                pool.wait_ge(SELF.normed, v + STEP)
                if again(v):
                    pool.wait_ge(s.resid, v)
                copy(s.x[:, :], SELF.out[:, :]).then_inc(s.x_copied, STEP)
                nc.gpsimd.tensor_tensor(s.xb[:, :], SELF.out[:, :], bo_r[:, :], ALU.add).then_inc(s.x_bias, STEP)
                yield
                pool.wait_ge(s.kT_ready, v + STEP)
                copy(s.kb[:, :], s.k[:, :]).then_inc(s.k_low, STEP)
                yield
                pool.wait_ge(s.v_ready, v + STEP)
                nc.gpsimd.tensor_tensor(s.vm[:, :, :], s.v[:, :].unsqueeze(1).to_broadcast([128, GH, 128]), own, ALU.mult)\
                    .then_inc(s.v_own, STEP)
                yield
                yield from low_queries(s, v)
                yield from inverse_root(s, v, s.moments, s.mv, s.rs[:, :], s.rstd)
                yield

            def local_stage(l, v):
                s = LOC[l]
                if l == 0:
                    pool.wait_ge(CROSS.normed, v + STEP)
                    if again(v):
                        pool.wait_ge(s.mid_done, v)
                        pool.wait_ge(s.kept, v)
                    copy(s.x[:, 0, :], CROSS.out[:, :]).then_inc(s.x_copied, STEP)
                else:
                    pool.wait_ge(LOC[0].resid, v + STEP)
                    pool.wait_ge(LOC[0].kept, v + STEP)
                    if again(v):
                        pool.wait_ge(s.mid_done, v)
                        pool.wait_ge(s.base_bias, v)
                    copy(s.x[:, :, :], LOC[0].out[:, :, :]).then_inc(s.x_copied, STEP)
                yield
                pool.wait_ge(s.x_copied, v + STEP)
                if l == 0:
                    if again(v):
                        pool.wait_ge(LOC[1].x_copied, v)
                    copy(s.out[:, 1, :], s.x[:, 0, :]).then_inc(s.kept, STEP)
                else:
                    if again(v):
                        pool.wait_ge(s.mid_bias, v)
                    nc.gpsimd.tensor_tensor(s.base[:, :], s.x[:, 1, :], b2_r[l][:, :], ALU.add).then_inc(s.base_bias, STEP)
                yield
                for a in (1, 0):
                    heads = slice(LH * a, LH * a + LH)
                    pool.wait_ge(s.square_sum, v + STEP - 8 * a)
                    nc.gpsimd.tensor_scalar(s.sc[:, heads], s.ss[:, heads], 1e-24, 1.0, ALU.max, ALU.mult)\
                        .then_inc(s.rnorm, 4)
                    yield
                    pool.wait_ge(s.rnorm, v + 12 - 8 * a)
                    nc.gpsimd.tensor_tensor(s.rn[:, heads], s.sc[:, heads], half_neg[:, 0:LH], ALU.pow).then_inc(s.rnorm, 4)
                    yield
                for a in (1, 0):
                    pool.wait_ge(s.qk_norm, v + STEP - 8 * a)
                    nc.gpsimd.tensor_tensor(
                        s.qs[:, a, :, :].rearrange("p h (u d) -> p h u d", u=2),
                        s.qk[:, a, :, :].rearrange("p h (u d) -> p h u d", u=2)[:, :, ::-1, :],
                        sin_t[l][:, a, :].rearrange("p (u d) -> p u d", u=2).unsqueeze(1).to_broadcast([128, LH, 2, LD // 2]),
                        ALU.mult).then_inc(s.rot_sin, 8)
                    yield
                pool.wait_ge(s.q_split, v + STEP)
                copy(s.qb[:, :, :, :].rearrange("p c a t -> p (c a) t"), s.q[:, :, :, :].rearrange("p c a t -> p (c a) t"))\
                    .then_inc(s.q_low, STEP)
                yield
                pool.wait_ge(s.kT_ready, v + STEP)
                copy(s.kb[:, :, :], s.k[:, :, :]).then_inc(s.k_low, STEP)
                yield
                pool.wait_ge(s.mid_done, v + STEP)
                addend = b2_r[l] if l == 0 else s.base
                if l == 1:
                    pool.wait_ge(s.base_bias, v + STEP)
                nc.gpsimd.tensor_tensor(s.midb[:, :], s.mid[:, :], addend[:, :], ALU.add).then_inc(s.mid_bias, STEP)
                yield
                yield from inverse_root(s, v, s.mid_moments, s.mv2, s.rs2[:, :], s.mid_rstd)
                yield
                if l == 1:
                    yield from inverse_root(s, v, s.moments, s.mv, s.rs[:, :], s.rstd)
                yield

            stages(nc.gpsimd, ORDER_GPSIMD, prepare_local, self_stage, cross_stage, local_stage)


def kernel(**inputs):
    import numpy as _np
    import concourse.bacc as _bacc
    from concourse import mybir as _mybir
    from concourse.bass_utils import run_bass_kernel_spmd as _run

    a = {k: _np.ascontiguousarray(v) for k, v in inputs.items()}
    w = a["L0_attn_weight"]
    arrays = {
        "x": a["x"], "ctx_in": a["ctx_1024"], "consts": shape_constants(),
        "w_heads": _np.ascontiguousarray(w.reshape(H, D, D).transpose(1, 0, 2)).reshape(D, H * D),
        "wqT": _np.ascontiguousarray(a["L0_xattn_Wq"].T), "bq": a["L0_xattn_bq"],
        "wkT": _np.ascontiguousarray(a["L0_xattn_Wk"].T), "bk": a["L0_xattn_bk"],
        "wvT": _np.ascontiguousarray(a["L0_xattn_Wv"].T), "bv": a["L0_xattn_bv"],
        "woT": _np.ascontiguousarray(a["L0_xattn_Wo"].T), "bo": a["L0_xattn_bo"],
    }
    for n in ("wqkv", "q_scale", "k_scale", "wo", "ln_g", "ln_b", "w1", "b1", "w2", "b2"):
        arrays[n] = a[f"L0_ffn_{n}"]
    nc = _bacc.Bacc("TRN2", target_bir_lowering=False, num_devices=1)
    args = [nc.dram_tensor(n, t.shape, _mybir.dt.from_np(t.dtype), kind="ExternalInput").ap()
            for n, t in arrays.items()]
    args.append(nc.dram_tensor("out", a["x"].shape, _mybir.dt.float32, kind="ExternalOutput").ap())
    decoder_kernel(nc, *args)
    r = _run(nc, [arrays], core_ids=[0])
    return r.results[0]["out"]
```

```python
from contextlib import ExitStack

import numpy as np

import concourse.bass as bass
from concourse import mybir

F32 = mybir.dt.float32
BF16 = mybir.dt.bfloat16
ALU = mybir.AluOpType
ACT = mybir.ActivationFunctionType
AX = mybir.AxisListType

T = 128
D = 128
H = 16
HD = D // H
GH = 4
G = H // GH
LH = 8
LD = 64
INNER = LH * LD
HID = 341
FC = (114, 114, 113)
FO = (0, 114, 228)
WINDOW = 64
EPS = 1e-5
MASKED = -1e30
STEP = 16
SLOTS = 8
SETS = ((0, 3), (3, 3), (6, 3), (9, 3), (12, 3), (15, 1))
SET_UP = (2, 2, 2, 2, 2, 6)

C_ID = 0
C_SHIFT = C_ID + 128
C_MASKN = C_SHIFT + 128
C_MASKT = C_MASKN + 128
C_BAND = C_MASKT + 128
C_GRP = C_BAND + 128
C_ROW = C_GRP + 4 * 128
C_OWN = C_ROW + GH
C_COS = C_OWN + GH * 128
C_SIN = C_COS + 2 * LD
C_END = C_SIN + 2 * LD


ORDER_TENSOR = (
    "CMSNCSSMSMNSMCCNSASCMNASSABSCSNBSCSCBCCSSASSCCSBCCSCCASCABCBAASSBBAACBBS"
    "AABABABBABAB")
ORDER_VECTOR = (
    "MMSMSNCNCNSMCSCCNCMCSCCCMCCNSSASSNSASBCCSACCCBCBCAAABSANSBASBBBCSMSSAASC"
    "ASABBBSABNSBSCSCAAABABBSBSSACSB")
ORDER_SCALAR = (
    "CSSMSMNSSCNASSAABCACBSBSSSCCABCCBAAABBBABABAB")
ORDER_GPSIMD = (
    "SMNMMNCNASCCCSSSSMSCBCCCAAABABBAABBABBAANNBBSSCSSSCS")

def shape_constants():
    c = np.zeros((128, C_END), np.float32)
    p = np.arange(128)
    c[:, C_ID:C_ID + 128] = np.eye(128)
    c[:, C_SHIFT:C_SHIFT + 128] = np.eye(128, k=1)
    i, j = p[:, None], p[None, :]
    allowed = (j <= i) & (j >= i - WINDOW)
    c[:, C_MASKN:C_MASKN + 128] = np.where(allowed, 0.0, MASKED)
    c[:, C_MASKT:C_MASKT + 128] = np.where(allowed.T, 0.0, MASKED)
    c[:, C_BAND:C_BAND + 128] = np.where(np.abs(i - j) <= WINDOW, 0.0, MASKED)
    head = p % 16
    for g in range(4):
        rows = (p < 32) & (head // GH == g)
        c[:, C_GRP + 128 * g:C_GRP + 128 * (g + 1)] = rows[:, None]
    c[:, C_ROW:C_ROW + GH] = (p[:, None] < 32) & (head[:, None] % GH == np.arange(GH))
    for n in range(GH):
        c[:, C_OWN + 128 * n:C_OWN + 128 * (n + 1)] = (p // HD) % GH == n
    half = np.arange(0, LD, 2, dtype=np.float32)
    inv = np.float32(1.0) / np.float32(10000.0) ** (half / np.float32(LD))
    t = np.arange(T, dtype=np.float32)
    freq = t[:, None] * inv[None, :]
    freq = np.concatenate([freq, freq], axis=-1)
    base = (half + np.float32(0.4 * LD)) / np.float32(1.4 * LD)
    power = (t - T // 2) / np.float32(WINDOW // 2)
    scale = base[None, :] ** power[:, None]
    scale = np.concatenate([scale, scale], axis=-1)
    sign = np.where(np.arange(LD) < LD // 2, -1.0, 1.0).astype(np.float32)
    cos, sin = np.cos(freq), np.sin(freq) * sign
    c[:, C_COS:C_COS + LD] = cos / scale
    c[:, C_COS + LD:C_COS + 2 * LD] = cos * scale * 8.0
    c[:, C_SIN:C_SIN + LD] = sin / scale
    c[:, C_SIN + LD:C_SIN + 2 * LD] = sin * scale * 8.0
    return c


def again(v):
    return not (isinstance(v, int) and v == 0)


def weave(order, parts):
    for letter in order:
        if letter in parts:
            next(parts[letter], None)
    for letter, part in parts.items():
        assert next(part, "end") == "end", (letter, "has steps that the order does not place")


class Stage:
    pass


def decoder_kernel(nc, x, ctx_in, consts, w_heads, wqT, bq, wkT, bk, wvT, bv, woT, bo,
                   wqkv, q_scale, k_scale, wo, ln_g, ln_b, w1, b1, w2, b2, out):
    B = x.shape[0]
    LAST = 5
    x_rows = x.rearrange("b t d -> (b t) d")
    ctx_rows = ctx_in.rearrange("b t d -> (b t) d")
    out_rows = out.rearrange("b t d -> (b t) d")

    with ExitStack() as ctx:
        def sb(name, shape, dt=F32):
            return ctx.enter_context(nc.sbuf_tensor(name, shape, dt))

        def sem(name):
            return ctx.enter_context(nc.semaphore(name))

        con = sb("con", [128, C_END])
        ident = con[:, C_ID:C_ID + 128]
        shift_m = con[:, C_SHIFT:C_SHIFT + 128]
        row_mask = con[:, C_ROW:C_ROW + GH]
        own = con[:, C_OWN:C_OWN + GH * 128].rearrange("p (j c) -> p j c", j=GH)
        ident_b = sb("ident_b", [128, 128], BF16)
        mask_n = sb("mask_n", [128, GH, 128], BF16)
        mask_t = sb("mask_t", [128, GH, 128], BF16)
        mask_w = sb("mask_w", [128, GH, 128], BF16)
        group_b = sb("group_b", [128, G, 128], BF16)
        half_neg = sb("half_neg", [128, H])
        wz = sb("wz", [128, H * 128])
        wq_s, wk_s, wv_s, wo_s = (sb(n, [128, 128]) for n in ("wq_s", "wk_s", "wv_s", "wo_s"))
        bq_r, bk_r, bv_r, bo_r = (sb(n, [128, 128]) for n in ("bq_r", "bk_r", "bv_r", "bo_r"))
        wqkv_s = [sb(f"wqkv_s{l}", [128, 3 * INNER]) for l in range(2)]
        wo3_s = [sb(f"wo3_s{l}", [128, LH // 2, 128]) for l in range(2)]
        w1_r = [sb(f"w1_r{l}", [128, 2 * HID]) for l in range(2)]
        w1_s = [sb(f"w1_s{l}", [128, 2 * HID]) for l in range(2)]
        w2_s = [sb(f"w2_s{l}", [128, 3, 128]) for l in range(2)]
        b1_r = [sb(f"b1_r{l}", [128, 6]) for l in range(2)]
        b1_s = [sb(f"b1_s{l}", [128, 6]) for l in range(2)]
        lg_c = [sb(f"lg_c{l}", [128, 1]) for l in range(2)]
        lb_c = [sb(f"lb_c{l}", [128, 1]) for l in range(2)]
        b2_r = [sb(f"b2_r{l}", [128, 128]) for l in range(2)]
        scale_r = [sb(f"scale_r{l}", [128, 2, LD]) for l in range(2)]
        scale_x = [sb(f"scale_x{l}", [128, 2, LD]) for l in range(2)]
        cos_t = [sb(f"cos_t{l}", [128, 2, LD]) for l in range(2)]
        sin_t = [sb(f"sin_t{l}", [128, 2, LD]) for l in range(2)]

        loaded = sem("attention_weights_loaded")
        local_loaded = sem("local_weights_loaded")
        prep_v = sem("prepared_by_vector")
        prep_p = sem("prepared_by_pool")
        prep_mm = sem("bias_products")
        stored = sem("stored")

        def stage(name):
            s = Stage()
            s.ps = ctx.enter_context(nc.psum_tensor(f"{name}_ps", [128, 1024], F32))
            s.b0, s.b1 = s.ps[:, 0:512], s.ps[:, 512:1024]
            s.x_copied = sem(f"{name}_x_copied")
            s.xT_psum = sem(f"{name}_xT_psum")
            s.xT_ready = sem(f"{name}_xT_ready")
            s.low = sem(f"{name}_low")
            s.scores_n_psum = sem(f"{name}_scores_n_psum")
            s.max_done = sem(f"{name}_max_done")
            s.neg_split = sem(f"{name}_neg_split")
            s.rows_psum = sem(f"{name}_rows_psum")
            s.rows_ready = sem(f"{name}_rows_ready")
            s.scores_t_psum = sem(f"{name}_scores_t_psum")
            s.exp_done = sem(f"{name}_exp_done")
            s.resid = sem(f"{name}_resid")
            return s

        def norm_signals(s, name):
            s.moments = sem(f"{name}_moments")
            s.rstd = sem(f"{name}_rstd")
            s.normed = sem(f"{name}_normed")

        def local_signals(s, name):
            s.qkv_psum = sem(f"{name}_qkv_psum")
            s.squares = sem(f"{name}_squares")
            s.square_sum = sem(f"{name}_square_sum")
            s.rnorm = sem(f"{name}_rnorm")
            s.qk_norm = sem(f"{name}_qk_norm")
            s.v_psum = sem(f"{name}_v_psum")
            s.v_ready = sem(f"{name}_v_ready")
            s.rot_sin = sem(f"{name}_rot_sin")
            s.rot_cos = sem(f"{name}_rot_cos")
            s.roped = sem(f"{name}_roped")
            s.qkT_psum = sem(f"{name}_qkT_psum")
            s.kT_ready = sem(f"{name}_kT_ready")
            s.q_split = sem(f"{name}_q_split")
            s.av_psum = sem(f"{name}_av_psum")
            s.inverse = sem(f"{name}_inverse")
            s.oT_psum = sem(f"{name}_oT_psum")
            s.oT_ready = sem(f"{name}_oT_ready")
            s.o_ready = sem(f"{name}_o_ready")
            s.proj_psum = sem(f"{name}_proj_psum")
            s.mid_done = sem(f"{name}_mid_done")
            s.mid_bias = sem(f"{name}_mid_bias")
            s.mid_moments = sem(f"{name}_mid_moments")
            s.mid_rstd = sem(f"{name}_mid_rstd")
            s.shifted_psum = sem(f"{name}_shifted_psum")
            s.hT_psum = sem(f"{name}_hT_psum")
            s.hT_ready = sem(f"{name}_hT_ready")
            s.hnorm = sem(f"{name}_hnorm")
            s.mlp_in_psum = sem(f"{name}_mlp_in_psum")
            s.gelu_done = sem(f"{name}_gelu_done")
            s.hid_done = sem(f"{name}_hid_done")
            s.mlp_psum = sem(f"{name}_mlp_psum")

        SELF, CROSS = stage("self"), stage("cross")
        LOC = [stage("local0"), stage("local1")]
        norm_signals(SELF, "self")
        norm_signals(CROSS, "cross")
        norm_signals(LOC[1], "local1")
        for l in range(2):
            local_signals(LOC[l], f"local{l}")
        SELF.z_psum = sem("self_z_psum")
        SELF.z_ready = sem("self_z_ready")
        SELF.av_psum = sem("self_av_psum")
        SELF.rden = sem("self_rden")
        SELF.y_ready = sem("self_y_ready")
        SELF.tree = sem("self_tree")
        SELF.x_loaded = sem("self_x_loaded")
        for s, n in ((SELF, "self"), (CROSS, "cross")):
            s.parts = sem(f"{n}_parts")
            s.turned = sem(f"{n}_turned")
            s.q_wide = sem(f"{n}_q_wide")
            s.k_op = sem(f"{n}_k_op")
        CROSS.c_loaded = sem("cross_c_loaded")
        CROSS.cT_psum = sem("cross_cT_psum")
        CROSS.cT_ready = sem("cross_cT_ready")
        CROSS.k_psum = sem("cross_k_psum")
        CROSS.biased = sem("cross_biased")
        CROSS.v_psum = sem("cross_v_psum")
        CROSS.v_ready = sem("cross_v_ready")
        CROSS.q_psum = sem("cross_q_psum")
        CROSS.av_psum = sem("cross_av_psum")
        CROSS.inverse = sem("cross_inverse")
        CROSS.v_own = sem("cross_v_own")
        CROSS.o_ready = sem("cross_o_ready")
        CROSS.proj_psum = sem("cross_proj_psum")
        CROSS.x_bias = sem("cross_x_bias")
        LOC[0].kept = sem("local0_kept")
        LOC[1].base_bias = sem("local1_base_bias")
        for s, n in ((SELF, "self"), (CROSS, "cross")):
            s.kp = sb(f"{n}_kp", [128, 3, 128], BF16)
            s.qp = s.kp if s is SELF else sb(f"{n}_qp", [128, 3, 128], BF16)
            s.left = sb(f"{n}_left", [128, 128])
            s.ks = sb(f"{n}_ks", [128, H, SLOTS, HD], BF16)
            s.qs = sb(f"{n}_qs", [128, H, SLOTS, HD], BF16)
            s.kT = sb(f"{n}_kT", [128, H // 2, 128], BF16)
            s.qT = sb(f"{n}_qT", [128, H // 2, 2, 128], BF16)
            s.xT = sb(f"{n}_xT", [128, 128])
            s.e = sb(f"{n}_e", [128, H, 128])
        for s, n, h in ((SELF, "self", H), (CROSS, "cross", H), (LOC[0], "local0", LH), (LOC[1], "local1", LH)):
            s.heads = h
            s.scale = 1.0 / np.sqrt(HD) if h == H else 1.0
            s.m = sb(f"{n}_m", [128, h])
            s.neg = sb(f"{n}_neg", [128, 128], BF16)
            s.rows = sb(f"{n}_rows", [128, GH, 128], BF16)
            s.st = sb(f"{n}_st", [128, 2, 6])
            s.mv2 = sb(f"{n}_mv2", [128, 2])
            s.rs2 = sb(f"{n}_rs2", [128, 1])
            s.mv = sb(f"{n}_mv", [128, 2])
            s.ve = sb(f"{n}_ve", [128, 1])
            s.rs = sb(f"{n}_rs", [128, 1])
            s.r = sb(f"{n}_r", [128, 128])
        SELF.windowed, CROSS.windowed = False, True
        SELF.xin = sb("self_xin", [128, 128])
        SELF.x = sb("self_x", [128, 128])
        SELF.z = sb("self_z", [128, H, 129])
        SELF.rd = sb("self_rd", [128, H])
        SELF.y = sb("self_y", [128, H, 128])
        SELF.out = sb("self_out", [128, 128])
        CROSS.cin = sb("cross_cin", [128, 128])
        CROSS.cT = sb("cross_cT", [128, 128])
        CROSS.k = sb("cross_k", [128, 128])
        CROSS.q = sb("cross_q", [128, 128])
        CROSS.v = sb("cross_v", [128, 128])
        CROSS.x = sb("cross_x", [128, 128])
        CROSS.xb = sb("cross_xb", [128, 128])
        CROSS.vm = sb("cross_vm", [128, GH, 128])
        CROSS.o = sb("cross_o", [128, 128])
        CROSS.out = sb("cross_out", [128, 128])
        for l, s in enumerate(LOC):
            n = f"local{l}"
            s.x = sb(f"{n}_x", [128, 2, 128])
            s.xT = sb(f"{n}_xT", [128, 128])
            s.ss = sb(f"{n}_ss", [128, 2 * LH])
            s.sc = sb(f"{n}_sc", [128, 2 * LH])
            s.rn = sb(f"{n}_rn", [128, 2 * LH])
            s.qk = sb(f"{n}_qk", [128, 2, LH, LD])
            s.qs = sb(f"{n}_qs", [128, 2, LH, LD])
            s.sq = s.qs[:, :, :, :].rearrange("p a h d -> p (a h) d")
            s.qc = sb(f"{n}_qc", [128, 2, LH, LD])
            s.qr = s.qc[:, :, :, :].rearrange("p a h d -> p (a h d)")
            s.v = sb(f"{n}_v", [128, LH, LD + 1])
            s.k = sb(f"{n}_k", [128, LH // 2, 128])
            s.kb = sb(f"{n}_kb", [128, LH // 2, 128], BF16)
            s.q = sb(f"{n}_q", [128, LH // 2, 2, 128])
            s.qb = sb(f"{n}_qb", [128, LH // 2, 2, 128], BF16)
            s.e = sb(f"{n}_e", [128, LH, 128])
            s.rd = sb(f"{n}_rd", [128, LH])
            s.o = sb(f"{n}_o", [128, INNER])
            s.oT = sb(f"{n}_oT", [128, LH // 2, 128])
            s.mid = sb(f"{n}_mid", [128, 128])
            s.midb = sb(f"{n}_midb", [128, 128])
            s.hn = sb(f"{n}_hn", [128, 128])
            s.hT = sb(f"{n}_hT", [128, 128])
            s.gate = sb(f"{n}_gate", [128, 3, 128])
            s.hid = s.gate
            s.out = sb(f"{n}_out", [128, 2, 128])
            s.base = sb(f"{n}_base", [128, 128])

        block = ctx.enter_context(nc.Block())

        def loop(eng, iteration, prepare_local, before):
            fill = LAST + 1
            for n in range(fill):
                if n == before:
                    prepare_local()
                iteration(STEP * n)
            if B > fill:
                with eng.Fori(STEP * fill, STEP * B, STEP) as i:
                    iteration(i)
            for n in range(max(B, fill), B + LAST):
                iteration(STEP * n)

        def at(i, skew):
            if isinstance(i, int):
                v = i - STEP * skew
                return v if 0 <= v < STEP * B else None
            return i - STEP * skew if skew else i

        def sample_rows(a, v):
            if isinstance(v, int):
                return a[v * (T // STEP):v * (T // STEP) + T, :]
            return a.rearrange("(b t) d -> b t d", t=T)[bass.ds(v // STEP, 1), :, :].rearrange("b t d -> (b t) d")

        SETUP = [
            (con[:, :], consts), (wz[:, :], w_heads), (wq_s[:, :], wqT), (wk_s[:, :], wkT),
            (wv_s[:, :], wvT), (wo_s[:, :], woT),
            (bq_r[:, :], bq.partition_broadcast(128)), (bk_r[:, :], bk.partition_broadcast(128)),
            (bv_r[:, :], bv.partition_broadcast(128)), (bo_r[:, :], bo.partition_broadcast(128)),
        ]
        SETUP_LOCAL = []
        for l in range(2):
            SETUP_LOCAL += [
                (wqkv_s[l][:, :], wqkv[l]), (wo3_s[l][:, :, :], wo[l].rearrange("(c p) n -> p c n", p=128)),
                (w1_r[l][:, :], w1[l]), (b2_r[l][:, :], b2[l].partition_broadcast(128)),
                (lg_c[l][:, :], ln_g[l].rearrange("(p a) -> p a", a=1)),
                (lb_c[l][:, :], ln_b[l].rearrange("(p a) -> p a", a=1)),
                (w2_s[l][0:FC[0], 0:2, :], w2[l][0:2 * FC[0], :].rearrange("(c p) n -> p c n", p=FC[0])),
                (w2_s[l][0:FC[2], 2, :], w2[l][2 * FC[0]:HID, :]),
            ]
            for half in range(2):
                for c in range(3):
                    lo = half * HID + FO[c]
                    SETUP_LOCAL.append((b1_r[l][0:FC[c], 3 * half + c:3 * half + c + 1],
                                        b1[l][lo:lo + FC[c]].rearrange("(p a) -> p a", a=1)))
            for k, s in enumerate((k_scale, q_scale)):
                SETUP_LOCAL.append((scale_r[l][:, k, :], s[l].partition_broadcast(128)))
                for a in range(2):
                    SETUP_LOCAL.append((scale_x[l][:, k, 32 * a:32 * a + 32],
                                        s[l][32 * (1 - a):32 * (1 - a) + 32].partition_broadcast(128)))
        LOADED = 16 * len(SETUP)
        LOCAL_LOADED = 16 * len(SETUP_LOCAL)
        PREP_V_FIXED = 13
        PREP_V_LOCAL = 19
        PREP_V_BIAS = 27
        N_PREP_P = 6

        def stages(eng, order, prepare_local, self_stage, cross_stage, local_attention, local_mlp):
            def iteration(i):
                parts = {}
                if at(i, 1) is not None:
                    parts["S"] = self_stage(at(i, 1))
                if at(i, 2) is not None:
                    parts["C"] = cross_stage(at(i, 2))
                for l in range(2):
                    if at(i, 3 + l) is not None:
                        parts["AB"[l]] = local_attention(l, at(i, 3 + l))
                    if at(i, 4 + l) is not None:
                        parts["MN"[l]] = local_mlp(l, at(i, 4 + l))
                weave(order, parts)
            loop(eng, iteration, prepare_local, 3)

        @block.sync
        def _(sp):
            for tile, source in SETUP:
                sp.dma_start(tile, source).then_inc(loaded, 16)

            def prepare_local():
                for tile, source in SETUP_LOCAL:
                    sp.dma_start(tile, source).then_inc(local_loaded, 16)

            def iteration(i):
                v = at(i, 0)
                if v is not None:
                    if again(v):
                        sp.wait_ge(SELF.x_copied, v)
                    sp.dma_start(SELF.xin[:, :], sample_rows(x_rows, v)).then_inc(SELF.x_loaded, 16)
                v = at(i, 1)
                if v is not None:
                    if again(v):
                        sp.wait_ge(CROSS.cT_psum, v)
                    sp.dma_start(CROSS.cin[:, :], sample_rows(ctx_rows, v)).then_inc(CROSS.c_loaded, 16)
                v = at(i, 5)
                if v is not None:
                    sp.wait_ge(LOC[1].normed, v + STEP)
                    sp.dma_start(sample_rows(out_rows, v), LOC[1].out[:, 0, :]).then_inc(stored, 16)

            loop(nc.sync, iteration, prepare_local, 1)
            sp.wait_ge(stored, STEP * B)

        @block.tensor
        def _(pe):
            pe.wait_ge(loaded, LOADED)
            pe.wait_ge(prep_v, PREP_V_FIXED)
            pe.wait_ge(prep_p, N_PREP_P)

            def prepare_local():
                pe.wait_ge(local_loaded, LOCAL_LOADED)
                for l in range(2):
                    for half in range(2):
                        for c in range(3):
                            lo = half * HID + FO[c]
                            last = nc.tensor.matmul(LOC[l].b0[0:FC[c], 3 * half + c:3 * half + c + 1],
                                                    w1_r[l][:, lo:lo + FC[c]], lb_c[l][:, :], start=True, stop=True)
                last.then_inc(prep_mm, 1)
                pe.wait_ge(prep_v, PREP_V_BIAS)

            def max_to_rows(s, v):
                pe.wait_ge(s.neg_split, v + STEP)
                nc.tensor.transpose(s.b1.bitcast(BF16)[:, 0:128], s.neg[:, :], ident_b[:, :]).then_inc(s.rows_psum, STEP)

            def turn(s, bank, slots):
                for p in range(H // 2):
                    last = nc.tensor.transpose(bank.bitcast(BF16)[:, 128 * p:128 * p + 128],
                                               slots[:, 2 * p:2 * p + 2, :, :].rearrange("p h s d -> p (h s d)"), ident_b[:, :])
                last.then_inc(s.turned, 8)

            def pair_scores(s, g, bank):
                for p in range(2):
                    nc.tensor.matmul(bank[:, 256 * p:256 * p + 256], s.kT[:, 2 * g + p, :], s.qT[:, 2 * g + p, :, :],
                                     start=(p == 0), stop=False, skip_group_check=True)

            def core16(s, v):
                pe.wait_ge(s.k_op, v + STEP)
                pe.wait_ge(s.q_wide, v + STEP)
                for g in range(G):
                    bank = s.b0 if g % 2 else s.b1
                    if g >= 2:
                        pe.wait_ge(s.max_done, v + 4 * (g - 1))
                    for j in range(GH):
                        last = nc.tensor.matmul(bank[:, 128 * j:128 * j + 128], s.qT[:, 2 * g + j // 2, j % 2, :],
                                                s.kT[:, 2 * g + j // 2, :], start=(j == 0), stop=not s.windowed,
                                                skip_group_check=True)
                    if s.windowed:
                        last = nc.tensor.matmul(bank, ident_b[:, :], mask_w[:, :, :], start=False, stop=True,
                                                skip_group_check=True)
                    last.then_inc(s.scores_n_psum, 4)
                    yield
                pe.wait_ge(s.max_done, v + STEP)
                pair_scores(s, 0, s.b0)
                yield
                max_to_rows(s, v)
                yield
                for g in range(G):
                    bank = s.b1 if g % 2 else s.b0
                    if g == 0:
                        pe.wait_ge(s.rows_ready, v + STEP)
                    else:
                        if g >= 2:
                            pe.wait_ge(s.exp_done, v + 4 * (g - 1))
                        pair_scores(s, g, bank)
                    if s.windowed:
                        nc.tensor.matmul(bank, ident_b[:, :], mask_w[:, :, :], start=False, stop=False,
                                         skip_group_check=True)
                    nc.tensor.matmul(bank, group_b[:, g, :], s.rows[:, :, :], start=False, stop=True,
                                     skip_group_check=True).then_inc(s.scores_t_psum, 4)
                    yield

            def self_stage(v):
                s = SELF
                pe.wait_ge(s.x_copied, v + STEP)
                if again(v):
                    pe.wait_ge(s.y_ready, v - SET_UP[-1])
                nc.tensor.transpose(s.b0[:, 0:128], s.x[:, :], ident).then_inc(s.xT_psum, STEP)
                yield
                for g in range(G):
                    bank = s.b0 if g % 2 else s.b1
                    if g == 0:
                        pe.wait_ge(s.xT_ready, v + STEP)
                        if again(v):
                            pe.wait_ge(s.y_ready, v)
                    if g >= 2:
                        pe.wait_ge(s.z_ready, v + 4 * (g - 1))
                    nc.tensor.matmul(bank, s.xT[:, :], wz[:, 512 * g:512 * g + 512], start=True, stop=True)\
                        .then_inc(s.z_psum, 4)
                    yield
                pe.wait_ge(s.z_ready, v + 12)
                pe.wait_ge(s.low, v + 8)
                turn(s, s.b1, s.ks)
                yield
                pe.wait_ge(s.z_ready, v + STEP)
                pe.wait_ge(s.low, v + STEP)
                turn(s, s.b0, s.qs)
                yield
                yield from core16(s, v)
                for n, (h0, hn) in enumerate(SETS):
                    bank = s.b1 if n % 2 else s.b0
                    pe.wait_ge(s.exp_done, v + 4 * max((h0 + hn - 1) // GH + 1, 3 + n if n < 2 else 0))
                    if n >= 2:
                        pe.wait_ge(s.y_ready, v + 2 * (n - 1))
                    for j in range(hn):
                        last = nc.tensor.matmul(bank[:, 129 * j:129 * j + 129], s.e[:, h0 + j, :],
                                                s.z[:, h0 + j, :], start=True, stop=True)
                    last.then_inc(s.av_psum, SET_UP[n])
                    yield

            def cross_stage(v):
                s = CROSS
                pe.wait_ge(s.c_loaded, v + STEP)
                if again(v):
                    pe.wait_ge(s.o_ready, v)
                nc.tensor.transpose(s.b0[:, 0:128], s.cin[:, :], ident).then_inc(s.cT_psum, STEP)
                yield
                pe.wait_ge(s.cT_ready, v + STEP)
                if again(v):
                    pe.wait_ge(s.resid, v)
                nc.tensor.matmul(s.b1[:, 0:128], s.cT[:, :], wk_s[:, :], start=True, stop=True).then_inc(s.k_psum, STEP)
                nc.tensor.matmul(s.b0[:, 0:128], s.cT[:, :], wv_s[:, :], start=True, stop=True).then_inc(s.v_psum, STEP)
                yield
                pe.wait_ge(s.low, v + 8)
                turn(s, s.b1, s.ks)
                yield
                pe.wait_ge(s.x_copied, v + STEP)
                pe.wait_ge(s.v_ready, v + STEP)
                nc.tensor.transpose(s.b0[:, 0:128], s.x[:, :], ident).then_inc(s.xT_psum, STEP)
                yield
                pe.wait_ge(s.xT_ready, v + STEP)
                nc.tensor.matmul(s.b0[:, 0:128], s.xT[:, :], wq_s[:, :], start=True, stop=True).then_inc(s.q_psum, STEP)
                yield
                pe.wait_ge(s.low, v + STEP)
                turn(s, s.b0, s.qs)
                yield
                yield from core16(s, v)
                pe.wait_ge(s.exp_done, v + STEP)
                for j in range(GH):
                    for g in range(G):
                        last = nc.tensor.matmul(s.b1[32 * g:32 * g + 32, 0:128], own[:, j, 32 * g:32 * g + 32],
                                                s.e[:, GH * g + j, :], start=(j == 0), stop=(j == GH - 1))
                last.then_inc(s.av_psum, 8)
                yield
                pe.wait_ge(s.v_own, v + STEP)
                for j in range(GH):
                    for g in range(G):
                        last = nc.tensor.matmul(s.b0[32 * g:32 * g + 32, 0:128], s.vm[:, j, 32 * g:32 * g + 32],
                                                s.e[:, GH * g + j, :], start=(j == 0), stop=(j == GH - 1))
                last.then_inc(s.av_psum, 8)
                yield
                pe.wait_ge(s.o_ready, v + STEP)
                last = nc.tensor.matmul(s.b1[:, 0:128], s.o[:, :], wo_s[:, :], start=True, stop=True)
                last.then_inc(s.proj_psum, STEP)
                yield

            def masked_scores(s, g, bank):
                for p in range(2):
                    nc.tensor.matmul(bank[:, 256 * p:256 * p + 256], s.k[:, 2 * g + p, :], s.q[:, 2 * g + p, :, :],
                                     start=(p == 0), stop=False, skip_group_check=True)
                nc.tensor.matmul(bank, ident_b[:, :], mask_t[:, :, :], start=False, stop=False, skip_group_check=True)

            def local_attention(l, v):
                s = LOC[l]
                pe.wait_ge(s.x_copied, v + STEP)
                if again(v):
                    pe.wait_ge(s.hid_done, v)
                nc.tensor.transpose(s.b1[:, 0:128], s.x[:, 0, :], ident).then_inc(s.xT_psum, STEP)
                yield
                pe.wait_ge(s.xT_ready, v + STEP)
                nc.tensor.matmul(s.b1, s.xT[:, :], wqkv_s[l][:, 0:INNER], start=True, stop=True)\
                    .then_inc(s.qkv_psum, 8)
                yield
                if again(v):
                    pe.wait_ge(s.resid, v)
                nc.tensor.matmul(s.b0, s.xT[:, :], wqkv_s[l][:, INNER:2 * INNER], start=True, stop=True)\
                    .then_inc(s.qkv_psum, 8)
                yield
                pe.wait_ge(s.qk_norm, v + 8)
                nc.tensor.matmul(s.b1, s.xT[:, :], wqkv_s[l][:, 2 * INNER:3 * INNER], start=True, stop=True)\
                    .then_inc(s.v_psum, STEP)
                yield
                pe.wait_ge(s.roped, v + 8)
                pe.wait_ge(s.v_ready, v + STEP)
                for p in range(LH // 2):
                    last = nc.tensor.transpose(s.b1[:, 128 * p:128 * p + 128],
                                               s.qr[:, INNER + 128 * p:INNER + 128 * p + 128], ident)
                last.then_inc(s.qkT_psum, 8)
                yield
                pe.wait_ge(s.roped, v + STEP)
                for p in range(LH // 2):
                    last = nc.tensor.transpose(s.b0[:, 128 * p:128 * p + 128], s.qr[:, 128 * p:128 * p + 128], ident)
                last.then_inc(s.qkT_psum, 8)
                yield
                pe.wait_ge(s.low, v + STEP)
                for g in range(2):
                    bank = s.b0 if g else s.b1
                    for j in range(GH):
                        nc.tensor.matmul(bank[:, 128 * j:128 * j + 128], s.qb[:, 2 * g + j // 2, j % 2, :],
                                         s.kb[:, 2 * g + j // 2, :], start=(j == 0), stop=False,
                                         skip_group_check=True)
                    nc.tensor.matmul(bank, ident_b[:, :], mask_n[:, :, :], start=False, stop=True,
                                     skip_group_check=True).then_inc(s.scores_n_psum, 8)
                    yield
                pe.wait_ge(s.max_done, v + STEP)
                masked_scores(s, 0, s.b0)
                yield
                max_to_rows(s, v)
                yield
                pe.wait_ge(s.rows_ready, v + STEP)
                nc.tensor.matmul(s.b0, group_b[:, 0, :], s.rows[:, :, :], start=False, stop=True,
                                 skip_group_check=True).then_inc(s.scores_t_psum, 8)
                yield
                masked_scores(s, 1, s.b1)
                nc.tensor.matmul(s.b1, group_b[:, 1, :], s.rows[:, :, :], start=False, stop=True,
                                 skip_group_check=True).then_inc(s.scores_t_psum, 8)
                yield
                for g in range(2):
                    bank = s.b1 if g else s.b0
                    pe.wait_ge(s.exp_done, v + 8 * g + 8)
                    for j in range(GH):
                        last = nc.tensor.matmul(bank[:, (LD + 1) * j:(LD + 1) * j + LD + 1], s.e[:, GH * g + j, :],
                                                s.v[:, GH * g + j, :], start=True, stop=True)
                    last.then_inc(s.av_psum, 8)
                    yield
                for p in range(LH // 2):
                    if p % 2 == 0:
                        pe.wait_ge(s.o_ready, v + 4 * p + 8)
                    last = nc.tensor.transpose(s.b0[:, 128 * p:128 * p + 128], s.o[:, 128 * p:128 * p + 128], ident)
                last.then_inc(s.oT_psum, STEP)
                yield
                pe.wait_ge(s.oT_ready, v + STEP)
                for p in range(LH // 2):
                    last = nc.tensor.matmul(s.b1[:, 0:128], s.oT[:, p, :], wo3_s[l][:, p, :],
                                            start=(p == 0), stop=(p == LH // 2 - 1))
                last.then_inc(s.proj_psum, STEP)
                yield

            def local_mlp(l, v):
                s = LOC[l]
                pe.wait_ge(s.mid_done, v + STEP)
                nc.tensor.matmul(s.b0[:, 0:64], shift_m, s.mid[:, 64:128], start=True, stop=True)\
                    .then_inc(s.shifted_psum, STEP)
                yield
                pe.wait_ge(s.hnorm, v + STEP)
                nc.tensor.transpose(s.b1[:, 0:128], s.hn[:, :], ident).then_inc(s.hT_psum, STEP)
                yield
                pe.wait_ge(s.hT_ready, v + STEP)
                for c in range(3):
                    lo = HID + FO[c]
                    last = nc.tensor.matmul(s.b0[0:FC[c], 128 * c:128 * c + 128], w1_s[l][:, lo:lo + FC[c]],
                                            s.hT[:, :], start=True, stop=True)
                last.then_inc(s.mlp_in_psum, 8)
                yield
                for c in range(3):
                    last = nc.tensor.matmul(s.b1[0:FC[c], 128 * c:128 * c + 128], w1_s[l][:, FO[c]:FO[c] + FC[c]],
                                            s.hT[:, :], start=True, stop=True)
                last.then_inc(s.mlp_in_psum, 8)
                yield
                pe.wait_ge(s.hid_done, v + STEP)
                for c in range(3):
                    last = nc.tensor.matmul(s.b0[:, 0:128], s.hid[0:FC[c], c, :], w2_s[l][0:FC[c], c, :],
                                            start=(c == 0), stop=(c == 2))
                last.then_inc(s.mlp_psum, STEP)
                yield

            stages(nc.tensor, ORDER_TENSOR, prepare_local, self_stage, cross_stage, local_attention, local_mlp)


        @block.scalar
        def _(act):
            act.wait_ge(loaded, LOADED)
            act.wait_ge(prep_v, PREP_V_FIXED)

            def prepare_local():
                act.wait_ge(prep_v, PREP_V_BIAS)

            def turned_queries(s, v):
                act.wait_ge(s.turned, v + STEP)
                for a in range(2):
                    nc.scalar.activation(s.qT[64 * a:64 * a + 64, :, a, :],
                                         s.b0.bitcast(BF16)[64 * a:64 * a + 64, :].rearrange("p (c t) -> p c t", c=H // 2),
                                         ACT.Copy).then_inc(s.q_wide, 8)
                    yield

            def exps(s, v, g, n):
                bank = s.b1 if g % 2 else s.b0
                act.wait_ge(s.scores_t_psum, v + STEP // n * (g + 1))
                nc.scalar.activation(s.e[:, GH * g:GH * g + GH, :], bank.rearrange("p (j t) -> p j t", j=GH), ACT.Exp,
                                     scale=s.scale)\
                    .then_inc(s.exp_done, STEP // n)

            def self_stage(v):
                s = SELF
                act.wait_ge(s.xT_psum, v + STEP)
                nc.scalar.activation(s.xT[:, :], s.b0[:, 0:128], ACT.Copy).then_inc(s.xT_ready, STEP)
                yield
                for g in range(G):
                    bank = s.b0 if g % 2 else s.b1
                    act.wait_ge(s.z_psum, v + 4 * g + 4)
                    nc.scalar.activation(s.z[:, GH * g:GH * g + GH, 0:128], bank.rearrange("p (j n) -> p j n", j=GH), ACT.Copy)\
                        .then_inc(s.z_ready, 4)
                    yield
                yield from turned_queries(s, v)
                for g in range(G):
                    exps(s, v, g, G)
                    yield

            def cross_stage(v):
                s = CROSS
                act.wait_ge(s.cT_psum, v + STEP)
                nc.scalar.activation(s.cT[:, :], s.b0[:, 0:128], ACT.Copy).then_inc(s.cT_ready, STEP)
                yield
                act.wait_ge(s.xT_psum, v + STEP)
                nc.scalar.activation(s.xT[:, :], s.b0[:, 0:128], ACT.Copy).then_inc(s.xT_ready, STEP)
                yield
                yield from turned_queries(s, v)
                for g in range(G):
                    exps(s, v, g, G)
                    yield

            def local_attention(l, v):
                s = LOC[l]
                act.wait_ge(s.xT_psum, v + STEP)
                nc.scalar.activation(s.xT[0:64, :], s.b1[0:64, 0:128], ACT.Copy).then_inc(s.xT_ready, 8)
                nc.scalar.activation(s.xT[64:128, 1:128], s.b1[64:128, 0:127], ACT.Copy).then_inc(s.xT_ready, 8)
                yield
                for a in (1, 0):
                    act.wait_ge(s.qkv_psum, v + STEP - 8 * a)
                    nc.scalar.activation(s.sq[:, LH * a:LH * a + LH, :],
                                         s.ps[:, INNER * a:INNER * a + INNER].rearrange("p (h d) -> p h d", d=LD), ACT.Square)\
                        .then_inc(s.squares, 8)
                    yield
                yield
                act.wait_ge(s.v_psum, v + STEP)
                nc.scalar.activation(s.v[:, :, 0:LD], s.b1.rearrange("p (h d) -> p h d", h=LH), ACT.Copy).then_inc(s.v_ready, STEP)
                yield
                act.wait_ge(s.qkT_psum, v + 8)
                for a in range(2):
                    nc.scalar.activation(s.q[64 * a:64 * a + 64, :, a, :],
                                         s.b1[64 * a:64 * a + 64, :].rearrange("p (c t) -> p c t", c=LH // 2), ACT.Copy)\
                        .then_inc(s.q_split, 8)
                    yield
                act.wait_ge(s.qkT_psum, v + STEP)
                nc.scalar.activation(s.k[:, :, :], s.b0.rearrange("p (c t) -> p c t", c=LH // 2), ACT.Copy)\
                    .then_inc(s.kT_ready, STEP)
                yield
                exps(s, v, 0, 2)
                yield
                exps(s, v, 1, 2)
                yield
                act.wait_ge(s.oT_psum, v + STEP)
                nc.scalar.activation(s.oT[:, :, :], s.b0.rearrange("p (c t) -> p c t", c=LH // 2), ACT.Copy)\
                    .then_inc(s.oT_ready, STEP)
                yield

            def local_mlp(l, v):
                s = LOC[l]
                act.wait_ge(s.hT_psum, v + STEP)
                nc.scalar.activation(s.hT[:, :], s.b1[:, 0:128], ACT.Copy).then_inc(s.hT_ready, STEP)
                yield
                act.wait_ge(s.mlp_in_psum, v + 8)
                for c in range(3):
                    last = nc.scalar.activation(s.gate[0:FC[c], c, :], s.b0[0:FC[c], 128 * c:128 * c + 128], ACT.Gelu,
                                                bias=b1_s[l][0:FC[c], 3 + c:4 + c])
                last.then_inc(s.gelu_done, STEP)
                yield

            stages(nc.scalar, ORDER_SCALAR, prepare_local, self_stage, cross_stage, local_attention, local_mlp)

        @block.vector
        def _(dve):
            for s in LOC:
                nc.vector.memset(s.v[:, :, LD:LD + 1], 1.0).then_inc(prep_v, 1)
            nc.vector.memset(SELF.z[:, :, 128:129], 1.0).then_inc(prep_v, 1)
            for s in (SELF, CROSS, LOC[0], LOC[1]):
                nc.vector.memset(s.neg[:, :], 0.0).then_inc(prep_v, 1)
            for s in LOC:
                nc.vector.memset(s.q[:, :, :, :], 0.0).then_inc(prep_v, 1)
                nc.vector.memset(s.xT[64:128, 0:1], 0.0).then_inc(prep_v, 1)
            for s in (SELF, CROSS):
                nc.vector.memset(s.qT[:, :, :, :], 0.0).then_inc(prep_v, 1)
            dve.wait_ge(loaded, LOADED)
            dve.wait_ge(prep_p, N_PREP_P)

            def prepare_local():
                dve.wait_ge(local_loaded, LOCAL_LOADED)
                for l in range(2):
                    nc.vector.tensor_scalar(w1_s[l][:, :], w1_r[l][:, :], lg_c[l][:, :], None, ALU.mult).then_inc(prep_v, 1)
                for l in range(2):
                    nc.vector.tensor_tensor(cos_t[l][:, :, :], scale_r[l][:, :, :],
                                            con[:, C_COS:C_COS + 2 * LD].rearrange("p (a d) -> p a d", a=2), ALU.mult)\
                        .then_inc(prep_v, 1)
                    nc.vector.tensor_tensor(sin_t[l][:, :, :], scale_x[l][:, :, :],
                                            con[:, C_SIN:C_SIN + 2 * LD].rearrange("p (a d) -> p a d", a=2), ALU.mult)\
                        .then_inc(prep_v, 1)
                dve.wait_ge(prep_mm, 1)
                for l in range(2):
                    for c0, c1, f in ((0, 2, FC[0]), (2, 3, FC[2]), (3, 5, FC[0]), (5, 6, FC[2])):
                        nc.vector.tensor_tensor(b1_s[l][0:f, c0:c1], LOC[l].b0[0:f, c0:c1], b1_r[l][0:f, c0:c1], ALU.add)\
                            .then_inc(prep_v, 1)

            def row_max(s, v, g, bank, n):
                dve.wait_ge(s.scores_n_psum, v + STEP // n * (g + 1))
                nc.vector.tensor_reduce(s.m[:, GH * g:GH * g + GH], bank.rearrange("p (j t) -> p j t", j=GH), AX.X, ALU.max)\
                    .then_inc(s.max_done, STEP // n)

            def split_max(s, v):
                h = s.heads
                dve.wait_ge(s.max_done, v + STEP)
                nc.vector.tensor_scalar(s.neg[:, 0:h], s.m[:, :], -1.0, None, ALU.mult).then_inc(s.neg_split, 8)
                yield
                dve.wait_ge(s.neg_split, v + 8)
                nc.vector.scalar_tensor_tensor(out=s.neg[:, 16:16 + h], in0=s.m[:, :], scalar=-1.0, in1=s.neg[:, 0:h],
                                               op0=ALU.mult, op1=ALU.subtract).then_inc(s.neg_split, 8)

            def split_parts(s, v, value, parts, before, up):
                nc.vector.tensor_scalar(parts[:, 0, :], value, 1.0, None, ALU.mult).then_inc(s.parts, up)
                yield
                dve.wait_ge(s.parts, v + before + up)
                nc.vector.tensor_tensor(s.left[:, :], value, parts[:, 0, :], ALU.subtract).then_inc(s.parts, up)
                yield
                dve.wait_ge(s.parts, v + before + 2 * up)
                nc.vector.tensor_scalar(parts[:, 1, :], s.left[:, :], 1.0, None, ALU.mult).then_inc(s.parts, up)
                yield
                dve.wait_ge(s.parts, v + before + 3 * up)
                nc.vector.tensor_tensor(parts[:, 2, :], s.left[:, :], parts[:, 1, :], ALU.subtract).then_inc(s.parts, up)
                yield

            def turned_keys(s, v):
                dve.wait_ge(s.turned, v + 8)
                nc.vector.tensor_scalar(s.kT[:, :, :], s.b1.bitcast(BF16).rearrange("p (c t) -> p c t", c=H // 2), 1.0, None,
                                        ALU.mult).then_inc(s.k_op, STEP)

            def spread_rows(s, v):
                dve.wait_ge(s.rows_psum, v + STEP)
                nc.vector.tensor_tensor(s.rows[:, :, :],
                                        s.b1.bitcast(BF16)[:, 0:128].unsqueeze(1).to_broadcast([128, GH, 128]),
                                        row_mask.unsqueeze(2).to_broadcast([128, GH, 128]), ALU.mult)\
                    .then_inc(s.rows_ready, STEP)

            def moments(s, v):
                dve.wait_ge(s.resid, v + STEP)
                nc.vector.bn_stats(s.st[:, 0, :], s.r[:, :]).then_inc(s.moments, 8)
                yield
                dve.wait_ge(s.moments, v + 8)
                nc.vector.bn_aggr(s.mv[:, :], s.st[:, 0, :]).then_inc(s.moments, 8)

            def normalise(s, v, out):
                dve.wait_ge(s.rstd, v + STEP)
                nc.vector.tensor_scalar(out, s.r[:, :], s.mv[:, 0:1], s.rs[:, :], ALU.subtract, ALU.mult)\
                    .then_inc(s.normed, STEP)

            def self_stage(v):
                s = SELF
                dve.wait_ge(s.x_copied, v + STEP)
                yield from split_parts(s, v, s.x[:, :], s.kp, 0, 4)
                turned_keys(s, v)
                yield
                for g in range(G):
                    row_max(s, v, g, s.b0 if g % 2 else s.b1, G)
                    yield
                yield from split_max(s, v)
                yield
                spread_rows(s, v)
                yield
                done = 0
                for n, (h0, hn) in enumerate(SETS):
                    done += SET_UP[n]
                    bank = (s.b1 if n % 2 else s.b0)[:, 0:129 * hn].rearrange("p (j n) -> p j n", n=129)
                    dve.wait_ge(s.av_psum, v + done)
                    nc.vector.reciprocal(s.rd[:, h0:h0 + hn].unsqueeze(2), bank[:, :, 128:129]).then_inc(s.rden, SET_UP[n])
                    yield
                    dve.wait_ge(s.rden, v + done)
                    nc.vector.tensor_tensor(s.y[:, h0:h0 + hn, :], bank[:, :, 0:128],
                                            s.rd[:, h0:h0 + hn].unsqueeze(2).to_broadcast([128, hn, 128]), ALU.mult)\
                        .then_inc(s.y_ready, SET_UP[n])
                    yield
                dve.wait_ge(s.tree, v + STEP)
                nc.vector.tensor_tensor(s.r[:, :], s.y[:, 0, :], s.y[:, 1, :], ALU.add).then_inc(s.resid, 8)
                yield
                dve.wait_ge(s.resid, v + 8)
                nc.vector.tensor_tensor(s.r[:, :], s.r[:, :], s.x[:, :], ALU.add).then_inc(s.resid, 8)
                yield from moments(s, v)
                yield
                if again(v):
                    dve.wait_ge(CROSS.x_bias, v)
                normalise(s, v, s.out[:, :])
                yield

            def cross_stage(v):
                s = CROSS
                dve.wait_ge(s.k_psum, v + STEP)
                nc.vector.tensor_tensor(s.k[:, :], s.b1[:, 0:128], bk_r[:, :], ALU.add).then_inc(s.biased, 8)
                yield
                dve.wait_ge(s.biased, v + 8)
                yield from split_parts(s, v, s.k[:, :], s.kp, 0, 2)
                dve.wait_ge(s.v_psum, v + STEP)
                nc.vector.tensor_tensor(s.v[:, :], s.b0[:, 0:128], bv_r[:, :], ALU.add).then_inc(s.v_ready, STEP)
                yield
                turned_keys(s, v)
                yield
                dve.wait_ge(s.q_psum, v + STEP)
                nc.vector.tensor_tensor(s.q[:, :], s.b0[:, 0:128], bq_r[:, :], ALU.add).then_inc(s.biased, 8)
                yield
                dve.wait_ge(s.biased, v + STEP)
                yield from split_parts(s, v, s.q[:, :], s.qp, 8, 2)
                for g in range(G):
                    row_max(s, v, g, s.b0 if g % 2 else s.b1, G)
                    yield
                yield from split_max(s, v)
                yield
                spread_rows(s, v)
                yield
                dve.wait_ge(s.av_psum, v + 8)
                nc.vector.reciprocal(s.o[:, :], s.b1[:, 0:128]).then_inc(s.inverse, STEP)
                yield
                dve.wait_ge(s.inverse, v + STEP)
                dve.wait_ge(s.av_psum, v + STEP)
                nc.vector.tensor_tensor(s.o[:, :], s.b0[:, 0:128], s.o[:, :], ALU.mult).then_inc(s.o_ready, STEP)
                yield
                dve.wait_ge(s.proj_psum, v + STEP)
                dve.wait_ge(s.x_bias, v + STEP)
                nc.vector.tensor_tensor(s.r[:, :], s.b1[:, 0:128], s.xb[:, :], ALU.add).then_inc(s.resid, STEP)
                yield from moments(s, v)
                yield
                if again(v):
                    dve.wait_ge(LOC[0].x_copied, v)
                normalise(s, v, s.out[:, :])
                yield

            def local_attention(l, v):
                s = LOC[l]
                for a in (1, 0):
                    dve.wait_ge(s.squares, v + STEP - 8 * a)
                    nc.vector.tensor_reduce(s.ss[:, LH * a:LH * a + LH], s.sq[:, LH * a:LH * a + LH, :], AX.X, ALU.add)\
                        .then_inc(s.square_sum, 8)
                    yield
                for a in (1, 0):
                    dve.wait_ge(s.rnorm, v + STEP - 8 * a)
                    nc.vector.tensor_tensor(s.qk[:, a, :, :],
                                            s.ps[:, INNER * a:INNER * a + INNER].rearrange("p (h d) -> p h d", d=LD),
                                            s.rn[:, LH * a:LH * a + LH].unsqueeze(2).to_broadcast([128, LH, LD]), ALU.mult)\
                        .then_inc(s.qk_norm, 8)
                    yield
                for a in (1, 0):
                    dve.wait_ge(s.qk_norm, v + STEP - 8 * a)
                    nc.vector.tensor_tensor(s.qc[:, a, :, :], s.qk[:, a, :, :],
                                            cos_t[l][:, a, :].unsqueeze(1).to_broadcast([128, LH, LD]), ALU.mult)\
                        .then_inc(s.rot_cos, 8)
                    yield
                    dve.wait_ge(s.rot_cos, v + STEP - 8 * a)
                    dve.wait_ge(s.rot_sin, v + STEP - 8 * a)
                    nc.vector.tensor_tensor(s.qc[:, a, :, :], s.qc[:, a, :, :], s.qs[:, a, :, :], ALU.add).then_inc(s.roped, 8)
                    yield
                for g in range(2):
                    row_max(s, v, g, s.b0 if g else s.b1, 2)
                    yield
                yield from split_max(s, v)
                yield
                spread_rows(s, v)
                yield
                for g in range(2):
                    bank = (s.b1 if g else s.b0)[:, 0:GH * (LD + 1)].rearrange("p (j d) -> p j d", j=GH)
                    dve.wait_ge(s.av_psum, v + 8 * g + 8)
                    nc.vector.reciprocal(s.rd[:, GH * g:GH * g + GH].unsqueeze(2), bank[:, :, LD:LD + 1]).then_inc(s.inverse, 8)
                    yield
                    dve.wait_ge(s.inverse, v + 8 * g + 8)
                    nc.vector.tensor_tensor(s.o[:, 256 * g:256 * g + 256].rearrange("p (j d) -> p j d", j=GH), bank[:, :, 0:LD],
                                            s.rd[:, GH * g:GH * g + GH].unsqueeze(2).to_broadcast([128, GH, LD]), ALU.mult)\
                        .then_inc(s.o_ready, 8)
                    yield
                dve.wait_ge(s.proj_psum, v + STEP)
                nc.vector.tensor_tensor(s.mid[:, :], s.b1[:, 0:128], s.x[:, 0, :], ALU.add).then_inc(s.mid_done, STEP)
                yield

            def local_mlp(l, v):
                s = LOC[l]
                dve.wait_ge(s.mid_done, v + STEP)
                nc.vector.bn_stats(s.st[:, 0, :], s.mid[:, 0:64]).then_inc(s.mid_moments, 4)
                yield
                dve.wait_ge(s.shifted_psum, v + STEP)
                nc.vector.bn_stats(s.st[:, 1, :], s.b0[:, 0:64]).then_inc(s.mid_moments, 4)
                yield
                dve.wait_ge(s.mid_moments, v + 8)
                nc.vector.bn_aggr(s.mv2[:, :], s.st[:, :, :].rearrange("p a b -> p (a b)")).then_inc(s.mid_moments, 8)
                yield
                dve.wait_ge(s.mid_rstd, v + STEP)
                nc.vector.tensor_scalar(s.hn[:, 0:64], s.mid[:, 0:64], s.mv2[:, 0:1], s.rs2[:, :],
                                        ALU.subtract, ALU.mult).then_inc(s.hnorm, 8)
                nc.vector.tensor_scalar(s.hn[:, 64:128], s.b0[:, 0:64], s.mv2[:, 0:1], s.rs2[:, :],
                                        ALU.subtract, ALU.mult).then_inc(s.hnorm, 8)
                yield
                dve.wait_ge(s.mlp_in_psum, v + STEP)
                dve.wait_ge(s.gelu_done, v + STEP)
                for c in range(3):
                    last = nc.vector.scalar_tensor_tensor(
                        out=s.hid[0:FC[c], c, :], in0=s.b1[0:FC[c], 128 * c:128 * c + 128], scalar=b1_s[l][0:FC[c], c:c + 1],
                        in1=s.gate[0:FC[c], c, :], op0=ALU.add, op1=ALU.mult)
                last.then_inc(s.hid_done, STEP)
                yield
                dve.wait_ge(s.mlp_psum, v + STEP)
                dve.wait_ge(s.mid_bias, v + STEP)
                if l == 0:
                    if again(v):
                        dve.wait_ge(LOC[1].x_copied, v)
                    nc.vector.tensor_tensor(s.out[:, 0, :], s.b0[:, 0:128], s.midb[:, :], ALU.add).then_inc(s.resid, STEP)
                    yield
                else:
                    nc.vector.tensor_tensor(s.r[:, :], s.b0[:, 0:128], s.midb[:, :], ALU.add).then_inc(s.resid, STEP)
                    yield from moments(s, v)
                    yield
                    if again(v):
                        dve.wait_ge(stored, v)
                    normalise(s, v, s.out[:, 0, :])
                yield

            stages(nc.vector, ORDER_VECTOR, prepare_local, self_stage, cross_stage, local_attention, local_mlp)

        @block.gpsimd
        def _(pool):
            nc.gpsimd.memset(half_neg[:, :], -0.5).then_inc(prep_p, 1)
            pool.wait_ge(loaded, LOADED)

            def copy(out, in_):
                return nc.gpsimd.tensor_scalar(out, in_, 1.0, 0.0, ALU.mult, ALU.add)

            copy(ident_b[:, :], ident).then_inc(prep_p, 1)
            copy(group_b[:, :, :], con[:, C_GRP:C_GRP + 512].rearrange("p (g t) -> p g t", g=4)).then_inc(prep_p, 1)
            for tile, at_ in ((mask_n, C_MASKN), (mask_t, C_MASKT), (mask_w, C_BAND)):
                copy(tile[:, :, :], con[:, at_:at_ + 128].unsqueeze(1).to_broadcast([128, GH, 128])).then_inc(prep_p, 1)
            pool.wait_ge(prep_v, PREP_V_FIXED)

            def prepare_local():
                pool.wait_ge(local_loaded, LOCAL_LOADED)
                pool.wait_ge(prep_v, PREP_V_LOCAL)

            def inverse_root(s, v, moments_done, mv, out, done):
                pool.wait_ge(moments_done, v + STEP)
                nc.gpsimd.tensor_scalar(s.ve[:, :], mv[:, 1:2], EPS, 1.0, ALU.add, ALU.mult).then_inc(done, 8)
                yield
                pool.wait_ge(done, v + 8)
                nc.gpsimd.tensor_tensor(out, s.ve[:, :], half_neg[:, 0:1], ALU.pow).then_inc(done, 8)

            def key_slots(s, v, split_done):
                pool.wait_ge(s.parts, v + split_done)
                for i, (at_, n) in enumerate(((0, 3), (3, 3), (6, 2))):
                    copy(s.ks[:, :, at_:at_ + n, :],
                                s.kp[:, i, :].rearrange("p (h d) -> p h d", h=H).unsqueeze(2).to_broadcast([128, H, n, HD]))\
                        .then_inc(s.low, (2, 2, 4)[i])
                    yield

            def query_slots(s, v):
                if s is not SELF:
                    pool.wait_ge(s.parts, v + STEP)
                for i, n in enumerate((3, 3, 2)):
                    copy(s.qs[:, :, i:SLOTS:3, :],
                                s.qp[:, i, :].rearrange("p (h d) -> p h d", h=H).unsqueeze(2).to_broadcast([128, H, n, HD]))\
                        .then_inc(s.low, (2, 2, 4)[i])
                    yield

            def self_stage(v):
                s = SELF
                pool.wait_ge(s.x_loaded, v + STEP)
                if again(v):
                    pool.wait_ge(s.resid, v)
                copy(s.x[:, :], s.xin[:, :]).then_inc(s.x_copied, STEP)
                yield
                yield from key_slots(s, v, STEP)
                yield from query_slots(s, v)
                pool.wait_ge(s.y_ready, v + 6)
                nc.gpsimd.tensor_tensor(s.y[:, 0:4, :], s.y[:, 0:4, :], s.y[:, 4:8, :], ALU.add).then_inc(s.tree, 4)
                yield
                pool.wait_ge(s.y_ready, v + STEP)
                nc.gpsimd.tensor_tensor(s.y[:, 8:12, :], s.y[:, 8:12, :], s.y[:, 12:16, :], ALU.add).then_inc(s.tree, 4)
                yield
                pool.wait_ge(s.tree, v + 8)
                nc.gpsimd.tensor_tensor(s.y[:, 0:4, :], s.y[:, 0:4, :], s.y[:, 8:12, :], ALU.add).then_inc(s.tree, 4)
                yield
                pool.wait_ge(s.tree, v + 12)
                nc.gpsimd.tensor_tensor(s.y[:, 0:2, :], s.y[:, 0:2, :], s.y[:, 2:4, :], ALU.add).then_inc(s.tree, 4)
                yield
                yield from inverse_root(s, v, s.moments, s.mv, s.rs[:, :], s.rstd)
                yield

            def cross_stage(v):
                s = CROSS
                pool.wait_ge(SELF.normed, v + STEP)
                if again(v):
                    pool.wait_ge(s.resid, v)
                copy(s.x[:, :], SELF.out[:, :]).then_inc(s.x_copied, STEP)
                nc.gpsimd.tensor_tensor(s.xb[:, :], SELF.out[:, :], bo_r[:, :], ALU.add).then_inc(s.x_bias, STEP)
                yield
                yield from key_slots(s, v, 8)
                pool.wait_ge(s.v_ready, v + STEP)
                nc.gpsimd.tensor_tensor(s.vm[:, :, :], s.v[:, :].unsqueeze(1).to_broadcast([128, GH, 128]), own, ALU.mult)\
                    .then_inc(s.v_own, STEP)
                yield
                yield from query_slots(s, v)
                yield from inverse_root(s, v, s.moments, s.mv, s.rs[:, :], s.rstd)
                yield

            def local_attention(l, v):
                s = LOC[l]
                if l == 0:
                    pool.wait_ge(CROSS.normed, v + STEP)
                    if again(v):
                        pool.wait_ge(s.mid_done, v)
                        pool.wait_ge(s.kept, v)
                    copy(s.x[:, 0, :], CROSS.out[:, :]).then_inc(s.x_copied, STEP)
                else:
                    pool.wait_ge(LOC[0].resid, v + STEP)
                    pool.wait_ge(LOC[0].kept, v + STEP)
                    if again(v):
                        pool.wait_ge(s.mid_done, v)
                        pool.wait_ge(s.base_bias, v)
                    copy(s.x[:, :, :], LOC[0].out[:, :, :]).then_inc(s.x_copied, STEP)
                yield
                pool.wait_ge(s.x_copied, v + STEP)
                if l == 0:
                    if again(v):
                        pool.wait_ge(LOC[1].x_copied, v)
                    copy(s.out[:, 1, :], s.x[:, 0, :]).then_inc(s.kept, STEP)
                else:
                    if again(v):
                        pool.wait_ge(s.mid_bias, v)
                    nc.gpsimd.tensor_tensor(s.base[:, :], s.x[:, 1, :], b2_r[l][:, :], ALU.add).then_inc(s.base_bias, STEP)
                yield
                for a in (1, 0):
                    heads = slice(LH * a, LH * a + LH)
                    pool.wait_ge(s.square_sum, v + STEP - 8 * a)
                    nc.gpsimd.tensor_scalar(s.sc[:, heads], s.ss[:, heads], 1e-24, 1.0, ALU.max, ALU.mult)\
                        .then_inc(s.rnorm, 4)
                    yield
                    pool.wait_ge(s.rnorm, v + 12 - 8 * a)
                    nc.gpsimd.tensor_tensor(s.rn[:, heads], s.sc[:, heads], half_neg[:, 0:LH], ALU.pow).then_inc(s.rnorm, 4)
                    yield
                for a in (1, 0):
                    pool.wait_ge(s.qk_norm, v + STEP - 8 * a)
                    nc.gpsimd.tensor_tensor(
                        s.qs[:, a, :, :].rearrange("p h (u d) -> p h u d", u=2),
                        s.qk[:, a, :, :].rearrange("p h (u d) -> p h u d", u=2)[:, :, ::-1, :],
                        sin_t[l][:, a, :].rearrange("p (u d) -> p u d", u=2).unsqueeze(1).to_broadcast([128, LH, 2, LD // 2]),
                        ALU.mult).then_inc(s.rot_sin, 8)
                    yield
                pool.wait_ge(s.q_split, v + STEP)
                copy(s.qb[:, :, :, :].rearrange("p c a t -> p (c a) t"), s.q[:, :, :, :].rearrange("p c a t -> p (c a) t"))\
                    .then_inc(s.low, 8)
                yield
                pool.wait_ge(s.kT_ready, v + STEP)
                copy(s.kb[:, :, :], s.k[:, :, :]).then_inc(s.low, 8)
                yield

            def local_mlp(l, v):
                s = LOC[l]
                pool.wait_ge(s.mid_done, v + STEP)
                addend = b2_r[l] if l == 0 else s.base
                if l == 1:
                    pool.wait_ge(s.base_bias, v + STEP)
                nc.gpsimd.tensor_tensor(s.midb[:, :], s.mid[:, :], addend[:, :], ALU.add).then_inc(s.mid_bias, STEP)
                yield
                yield from inverse_root(s, v, s.mid_moments, s.mv2, s.rs2[:, :], s.mid_rstd)
                yield
                if l == 1:
                    yield from inverse_root(s, v, s.moments, s.mv, s.rs[:, :], s.rstd)
                yield

            stages(nc.gpsimd, ORDER_GPSIMD, prepare_local, self_stage, cross_stage, local_attention, local_mlp)


def kernel(**inputs):
    import numpy as _np
    import concourse.bacc as _bacc
    from concourse import mybir as _mybir
    from concourse.bass_utils import run_bass_kernel_spmd as _run

    a = {k: _np.ascontiguousarray(v) for k, v in inputs.items()}
    w = a["L0_attn_weight"]
    arrays = {
        "x": a["x"], "ctx_in": a["ctx_1024"], "consts": shape_constants(),
        "w_heads": _np.ascontiguousarray(w.reshape(H, D, D).transpose(1, 0, 2)).reshape(D, H * D),
        "wqT": _np.ascontiguousarray(a["L0_xattn_Wq"].T), "bq": a["L0_xattn_bq"],
        "wkT": _np.ascontiguousarray(a["L0_xattn_Wk"].T), "bk": a["L0_xattn_bk"],
        "wvT": _np.ascontiguousarray(a["L0_xattn_Wv"].T), "bv": a["L0_xattn_bv"],
        "woT": _np.ascontiguousarray(a["L0_xattn_Wo"].T), "bo": a["L0_xattn_bo"],
    }
    for n in ("wqkv", "q_scale", "k_scale", "wo", "ln_g", "ln_b", "w1", "b1", "w2", "b2"):
        arrays[n] = a[f"L0_ffn_{n}"]
    nc = _bacc.Bacc("TRN2", target_bir_lowering=False, num_devices=1)
    args = [nc.dram_tensor(n, t.shape, _mybir.dt.from_np(t.dtype), kind="ExternalInput").ap()
            for n, t in arrays.items()]
    args.append(nc.dram_tensor("out", a["x"].shape, _mybir.dt.float32, kind="ExternalOutput").ap())
    decoder_kernel(nc, *args)
    r = _run(nc, [arrays], core_ids=[0])
    return r.results[0]["out"]
```
